# Optimizing a Trainium2 kernel written in Bass

```python
import numpy as np
import jax
import jax.numpy as jnp

def _softmax(x, axis=-1):
    return jax.nn.softmax(x, axis=axis)

def _gelu(x):
    return jax.nn.gelu(x, approximate=True)

def _silu(x):
    return jax.nn.silu(x)

def _sigmoid(x):
    return jax.nn.sigmoid(x)

def _layernorm(x, axis=-1, eps=1e-05):
    m = jnp.mean(x, axis=axis, keepdims=True)
    v = jnp.var(x, axis=axis, keepdims=True)
    return (x - m) / jnp.sqrt(v + eps)

def _scatter_add(tgt, idx, src, axis=0):
    return tgt.at[idx].add(src)

def _segment_sum(src, seg, n):
    return jax.ops.segment_sum(src, seg, n)
kernel_name = 'mk_recurrent_d2_jaxref_r4_5af280'

def setup_inputs(seed: int=0):
    np.random.seed(seed)
    _w = jnp.asarray

    def _L0_attn_setup():
        import jax, jax.numpy as jnp
        import numpy as np
        D_MODEL = 256
        N_HEADS = 16
        D_HEAD = D_MODEL // N_HEADS
        SEQ = 1024
        BATCH = 1
        key = jax.random.key(seed)
        kx, kq, kk, kv, ko = jax.random.split(key, 5)
        scale = (1.0 / D_MODEL) ** 0.5
        return {'x': jax.random.normal(kx, (BATCH, SEQ, D_MODEL), dtype=jnp.float32), 'W_Q': jax.random.normal(kq, (D_MODEL, D_MODEL), dtype=jnp.float32) * scale, 'W_K': jax.random.normal(kk, (D_MODEL, D_MODEL), dtype=jnp.float32) * scale, 'W_V': jax.random.normal(kv, (D_MODEL, D_MODEL), dtype=jnp.float32) * scale, 'W_o': jax.random.normal(ko, (D_MODEL, D_MODEL), dtype=jnp.float32) * scale}
    _L0_attn_in = _L0_attn_setup()

    def _L0_ffn_setup():
        import jax, jax.numpy as jnp
        import numpy as np
        E, D, F = (8, 256, 1024)
        LN_EPS = 1e-05
        key = jax.random.key(seed)
        k = jax.random.split(key, 8)
        x = jax.random.normal(k[0], (4, 512, D), jnp.float32)
        centroids = jax.random.normal(k[1], (E, D), jnp.float32) * 0.1
        ln_g = jnp.ones((E, D), jnp.float32)
        ln_b = jnp.zeros((E, D), jnp.float32)
        w1 = jax.random.normal(k[2], (E, F, D), jnp.float32) * (1.0 / np.sqrt(D))
        b1 = jnp.zeros((E, F), jnp.float32)
        w2 = jax.random.normal(k[3], (E, D, F), jnp.float32) * (1.0 / np.sqrt(F))
        b2 = jnp.zeros((E, D), jnp.float32)
        return {'input_features': x, 'centroids': centroids, 'ln_g': ln_g, 'ln_b': ln_b, 'w1': w1, 'b1': b1, 'w2': w2, 'b2': b2}
    _L0_ffn_in = _L0_ffn_setup()

    def _L1_attn_setup():
        import jax, jax.numpy as jnp
        import numpy as np
        ROPE_THETA = 10000.0
        N_HEAD = 16

        def _rope(x, theta):
            T, D = (x.shape[-2], x.shape[-1])
            pos = jnp.arange(T, dtype=jnp.float32)
            inv_freq = 1.0 / theta ** (jnp.arange(0, D, 2, dtype=jnp.float32) / D)
            freqs = pos[:, None] * inv_freq[None, :]
            cos = jnp.cos(freqs).astype(x.dtype)[None, None]
            sin = jnp.sin(freqs).astype(x.dtype)[None, None]
            x_even = x[..., ::2]
            x_odd = x[..., 1::2]
            rot = jnp.stack((x_even * cos - x_odd * sin, x_even * sin + x_odd * cos), axis=-1)
            return rot.reshape(x.shape)
        key = jax.random.key(seed)
        ks = jax.random.split(key, 5)
        B, T, E = (4, 512, 256)
        s = 0.02
        return {'x': jax.random.normal(ks[0], (B, T, E), jnp.float32), 'Wqkv': jax.random.normal(ks[1], (E, 3 * E), jnp.float32) * s, 'bqkv': jax.random.normal(ks[2], (3 * E,), jnp.float32) * s, 'Wproj': jax.random.normal(ks[3], (E, E), jnp.float32) * s, 'bproj': jax.random.normal(ks[4], (E,), jnp.float32) * s}
    _L1_attn_in = _L1_attn_setup()

    def _L1_ffn_setup():
        import jax, jax.numpy as jnp
        import numpy as np
        B, S, H, I, E, K = (4, 512, 256, 256, 8, 2)
        LIMIT = 7.0
        ALPHA = 1.702
        EPS = 1e-05
        key = jax.random.key(seed)
        ks = jax.random.split(key, 5)
        x = jax.random.normal(ks[0], (B, S, H), dtype=jnp.float32)
        norm_weight = jnp.ones((H,), dtype=jnp.float32)
        gate_weight = (jax.random.normal(ks[1], (E, H), dtype=jnp.float32) / np.sqrt(H)).astype(jnp.bfloat16)
        gate_bias = jnp.zeros((E,), dtype=jnp.bfloat16)
        mlp1_weight = (jax.random.normal(ks[2], (E, 2 * I, H), dtype=jnp.float32) / np.sqrt(H)).astype(jnp.bfloat16)
        mlp1_bias = jnp.zeros((E, 2 * I), dtype=jnp.bfloat16)
        mlp2_weight = (jax.random.normal(ks[3], (E, H, I), dtype=jnp.float32) / np.sqrt(I)).astype(jnp.bfloat16)
        mlp2_bias = jnp.zeros((E, H), dtype=jnp.bfloat16)
        return {'x': x, 'norm_weight': norm_weight, 'gate_weight': gate_weight, 'gate_bias': gate_bias, 'mlp1_weight': mlp1_weight, 'mlp1_bias': mlp1_bias, 'mlp2_weight': mlp2_weight, 'mlp2_bias': mlp2_bias}
    _L1_ffn_in = _L1_ffn_setup()
    _d = {'L0_attn_x': _L0_attn_in['x'], 'L0_attn_W_Q': _L0_attn_in['W_Q'], 'L0_attn_W_K': _L0_attn_in['W_K'], 'L0_attn_W_V': _L0_attn_in['W_V'], 'L0_attn_W_o': _L0_attn_in['W_o'], 'L0_ffn_centroids': _L0_ffn_in['centroids'], 'L0_ffn_ln_g': _L0_ffn_in['ln_g'], 'L0_ffn_ln_b': _L0_ffn_in['ln_b'], 'L0_ffn_w1': _L0_ffn_in['w1'], 'L0_ffn_b1': _L0_ffn_in['b1'], 'L0_ffn_w2': _L0_ffn_in['w2'], 'L0_ffn_b2': _L0_ffn_in['b2'], 'L1_attn_Wqkv': _L1_attn_in['Wqkv'], 'L1_attn_bqkv': _L1_attn_in['bqkv'], 'L1_attn_Wproj': _L1_attn_in['Wproj'], 'L1_attn_bproj': _L1_attn_in['bproj'], 'L1_ffn_norm_weight': _L1_ffn_in['norm_weight'], 'L1_ffn_gate_weight': _L1_ffn_in['gate_weight'], 'L1_ffn_gate_bias': _L1_ffn_in['gate_bias'], 'L1_ffn_mlp1_weight': _L1_ffn_in['mlp1_weight'], 'L1_ffn_mlp1_bias': _L1_ffn_in['mlp1_bias'], 'L1_ffn_mlp2_weight': _L1_ffn_in['mlp2_weight'], 'L1_ffn_mlp2_bias': _L1_ffn_in['mlp2_bias']}
    _x0 = _d['L0_attn_x']
    _d['L0_attn_x'] = jax.random.normal(jax.random.fold_in(jax.random.key(seed), 1), (2, 2048, 256), dtype=_x0.dtype)
    del _x0
    return _d

def reference(L0_attn_x, L0_attn_W_Q, L0_attn_W_K, L0_attn_W_V, L0_attn_W_o, L0_ffn_centroids, L0_ffn_ln_g, L0_ffn_ln_b, L0_ffn_w1, L0_ffn_b1, L0_ffn_w2, L0_ffn_b2, L1_attn_Wqkv, L1_attn_bqkv, L1_attn_Wproj, L1_attn_bproj, L1_ffn_norm_weight, L1_ffn_gate_weight, L1_ffn_gate_bias, L1_ffn_mlp1_weight, L1_ffn_mlp1_bias, L1_ffn_mlp2_weight, L1_ffn_mlp2_bias):

    def _L0_attn_ref(x, W_Q, W_K, W_V, W_o):
        import jax, jax.numpy as jnp
        import numpy as np
        D_MODEL = 256
        N_HEADS = 16
        D_HEAD = D_MODEL // N_HEADS
        SEQ = 1024
        BATCH = 1
        B, S, _ = x.shape

        def heads(w):
            return (x @ w).reshape(B, S, N_HEADS, D_HEAD).transpose(0, 2, 1, 3)
        Q, K, V = (heads(W_Q), heads(W_K), heads(W_V))
        scores = jnp.einsum('bhqd,bhkd->bhqk', Q, K) / D_HEAD ** 0.5
        causal = jnp.triu(jnp.full((S, S), -jnp.inf, dtype=scores.dtype), k=1)
        scores = scores + causal
        probs = jax.nn.softmax(scores, axis=-1)
        out = jnp.einsum('bhqk,bhkd->bhqd', probs, V)
        out = out.transpose(0, 2, 1, 3).reshape(B, S, D_MODEL)
        return out @ W_o

    def _L0_ffn_ref(input_features, centroids, ln_g, ln_b, w1, b1, w2, b2):
        import jax, jax.numpy as jnp
        import numpy as np
        E, D, F = (8, 256, 1024)
        LN_EPS = 1e-05
        x = input_features.reshape(-1, D)
        aff = jax.lax.stop_gradient(x) @ centroids.T
        assign = jnp.argmax(aff, axis=1)
        onehot = jax.nn.one_hot(assign, E, dtype=x.dtype)
        mu = jnp.mean(x, axis=-1, keepdims=True)
        var = jnp.mean((x - mu) ** 2, axis=-1, keepdims=True)
        xhat = (x - mu) * jax.lax.rsqrt(var + LN_EPS)
        xn = xhat[None, :, :] * ln_g[:, None, :] + ln_b[:, None, :]
        h = jax.nn.relu(jnp.einsum('etd,efd->etf', xn, w1) + b1[:, None, :])
        y = x[None, :, :] + jnp.einsum('etf,edf->etd', h, w2) + b2[:, None, :]
        alpha = jax.nn.sigmoid(x @ centroids.T)
        a = alpha.T[:, :, None]
        gated = a * y + (1.0 - a) * x[None, :, :]
        out = jnp.einsum('te,etd->td', onehot, gated)
        return out.reshape(input_features.shape)

    def _L1_attn_ref(x, Wqkv, bqkv, Wproj, bproj):
        import jax, jax.numpy as jnp
        import numpy as np
        ROPE_THETA = 10000.0
        N_HEAD = 16

        def _rope(x, theta):
            T, D = (x.shape[-2], x.shape[-1])
            pos = jnp.arange(T, dtype=jnp.float32)
            inv_freq = 1.0 / theta ** (jnp.arange(0, D, 2, dtype=jnp.float32) / D)
            freqs = pos[:, None] * inv_freq[None, :]
            cos = jnp.cos(freqs).astype(x.dtype)[None, None]
            sin = jnp.sin(freqs).astype(x.dtype)[None, None]
            x_even = x[..., ::2]
            x_odd = x[..., 1::2]
            rot = jnp.stack((x_even * cos - x_odd * sin, x_even * sin + x_odd * cos), axis=-1)
            return rot.reshape(x.shape)
        B, T, E = x.shape
        H = N_HEAD
        D = E // H
        qkv = x @ Wqkv + bqkv
        q, k, v = jnp.split(qkv, 3, axis=-1)
        q = q.reshape(B, T, H, D).transpose(0, 2, 1, 3)
        k = k.reshape(B, T, H, D).transpose(0, 2, 1, 3)
        v = v.reshape(B, T, H, D).transpose(0, 2, 1, 3)
        q = _rope(q, ROPE_THETA)
        k = _rope(k, ROPE_THETA)
        scores = jnp.einsum('bhqd,bhkd->bhqk', q, k) * D ** (-0.5)
        causal = jnp.tril(jnp.ones((T, T), dtype=bool))
        scores = jnp.where(causal[None, None], scores, -jnp.inf)
        weights = jax.nn.softmax(scores, axis=-1)
        out = jnp.einsum('bhqk,bhkd->bhqd', weights, v)
        out = out.transpose(0, 2, 1, 3).reshape(B, T, E)
        return out @ Wproj + bproj

    def _L1_ffn_ref(x, norm_weight, gate_weight, gate_bias, mlp1_weight, mlp1_bias, mlp2_weight, mlp2_bias):
        import jax, jax.numpy as jnp
        import numpy as np
        B, S, H, I, E, K = (4, 512, 256, 256, 8, 2)
        LIMIT = 7.0
        ALPHA = 1.702
        EPS = 1e-05
        xc = x.astype(jnp.bfloat16)
        xf = xc.astype(jnp.float32)
        rms = jnp.mean(xf * xf, axis=-1, keepdims=True)
        normed = (xf * jax.lax.rsqrt(rms + EPS) * norm_weight).astype(jnp.bfloat16)
        nf = normed.astype(jnp.float32)
        logits = (jnp.einsum('bsh,eh->bse', nf, gate_weight.astype(jnp.float32)) + gate_bias.astype(jnp.float32)).astype(jnp.bfloat16).astype(jnp.float32)
        scores, idx = jax.lax.top_k(logits, K)
        w = jax.nn.softmax(scores, axis=-1)
        combine = jnp.sum(jax.nn.one_hot(idx, E, dtype=jnp.float32) * w[..., None], axis=-2)
        p1 = jnp.einsum('bsh,eoh->bseo', nf, mlp1_weight.astype(jnp.float32)) + mlp1_bias.astype(jnp.float32)
        g = jnp.minimum(p1[..., 0::2], LIMIT)
        lin = jnp.clip(p1[..., 1::2], -LIMIT, LIMIT)
        act = g * jax.nn.sigmoid(ALPHA * g) * (lin + 1.0)
        p2 = jnp.einsum('bsei,ehi->bseh', act, mlp2_weight.astype(jnp.float32)) + mlp2_bias.astype(jnp.float32)
        combined = jnp.einsum('bseh,bse->bsh', p2, combine)
        out = (xc + combined.astype(jnp.bfloat16)).astype(x.dtype)
        return out
    x = L0_attn_x
    xn = _layernorm(x, axis=-1)
    s = _L0_attn_ref(xn, L0_attn_W_Q, L0_attn_W_K, L0_attn_W_V, L0_attn_W_o)
    g = _silu(_L0_ffn_ref(xn, L0_ffn_centroids, L0_ffn_ln_g, L0_ffn_ln_b, L0_ffn_w1, L0_ffn_b1, L0_ffn_w2, L0_ffn_b2))
    x = x + s * g
    xn = _layernorm(x, axis=-1)
    s = _L1_attn_ref(xn, L1_attn_Wqkv, L1_attn_bqkv, L1_attn_Wproj, L1_attn_bproj)
    g = _silu(_L1_ffn_ref(xn, L1_ffn_norm_weight, L1_ffn_gate_weight, L1_ffn_gate_bias, L1_ffn_mlp1_weight, L1_ffn_mlp1_bias, L1_ffn_mlp2_weight, L1_ffn_mlp2_bias))
    x = x + s * g
    return x

_drawn_inputs = setup_inputs


def setup_inputs(seed=0):
    import zlib

    import numpy as np

    out = dict(_drawn_inputs(seed))
    spreads = {'L0_ffn_ln_g': (1.0, 0.6),
     'L0_ffn_ln_b': (0.0, 0.8),
     'L0_ffn_b1': (0.0, 0.8),
     'L0_ffn_b2': (0.0, 0.8),
     'L1_ffn_norm_weight': (1.0, 0.6),
     'L1_ffn_gate_bias': (0.0, 0.8),
     'L1_ffn_mlp1_bias': (0.0, 0.8),
     'L1_ffn_mlp2_bias': (0.0, 2.0)}
    factors = {'L1_attn_Wqkv': 8.0,
     'L1_attn_bqkv': 8.0,
     'L1_attn_Wproj': 7.272,
     'L1_attn_bproj': 12.747,
     'L1_ffn_gate_weight': 6.13,
     'L1_ffn_mlp1_weight': 5.711,
     'L1_ffn_mlp2_weight': 5.409}
    for name, (base, spread) in spreads.items():
        noise = np.random.default_rng([zlib.crc32(name.encode()), seed]).standard_normal(out[name].shape)
        drawn = base * np.exp(spread * noise) if base else spread * noise
        out[name] = jnp.asarray(drawn.astype(out[name].dtype))
    for name, factor in factors.items():
        out[name] = (out[name] * factor).astype(out[name].dtype)
    return out
```

```python
from contextlib import ExitStack

import numpy as np

import concourse.bass as bass
from concourse import mybir

F32 = mybir.dt.float32
BF16 = mybir.dt.bfloat16
I32 = mybir.dt.int32
U32 = mybir.dt.uint32
ALU = mybir.AluOpType
ACT = mybir.ActivationFunctionType
AX = mybir.AxisListType

P = 128
D = 256
KD = D // P
H = 16
DH = D // H
HG = 4
NG = H // HG
GW = HG * DH
S = 2048
NB = 2
TS = S // P
NT = NB * TS
NU = NB * NG
NE = 8
F0 = 1024
F1 = 256
EPS = 1e-5
SLOT0 = 40
SLOT1 = 72
CH = 512
CT = CH // P
NC = S // CH
NPART = 6
KR = NPART * DH
MR = 2
BIG = -1.0e30

C_ID, C_UP, C_MQ, C_MK, C_ONE, C_K128, C_SLOT, C_PICK = 0, 128, 256, 384, 512, 640, 704, 784
C_COLS = 792


def constant_table():
    t = np.zeros((P, C_COLS), np.float32)
    r = np.arange(P)
    t[:, C_ID:C_ID + P] = np.eye(P)
    t[:, C_UP:C_UP + P] = r[:, None] < r[None, :]
    t[:, C_MQ:C_MQ + P] = np.where(r[None, :] > r[:, None], BIG, 0)
    t[:, C_MK:C_MK + P] = np.where(r[:, None] > r[None, :], BIG, 0)
    t[:, C_ONE:C_ONE + P] = 1
    t[:, C_K128:C_K128 + 64] = 128 * np.arange(64)
    t[:, C_SLOT:C_SLOT + 80] = np.arange(80)
    t[:, C_PICK:C_PICK + NE] = NE - np.arange(NE)
    return t


def rotary_tables():
    inv = np.float32(1.0) / np.float32(10000.0) ** (np.arange(0, DH, 2, dtype=np.float32) / np.float32(DH))
    f = np.arange(S, dtype=np.float32)[:, None] * inv[None, :].astype(np.float32)
    lay = lambda a: np.ascontiguousarray(a.reshape(TS, P, DH // 2).transpose(1, 0, 2).reshape(P, -1))
    return lay(np.cos(f).astype(np.float32)), lay(np.sin(f).astype(np.float32))


class Core:

    def __init__(self, nc, stack):
        self.nc, self.stack, self.held = nc, stack, []

    def sb(self, name, shape, dt=F32, stack=None):
        return (stack or self.stack).enter_context(self.nc.sbuf_tensor(name, shape, dt))

    def ps(self, name, cols, dt=F32, stack=None):
        return (stack or self.stack).enter_context(self.nc.psum_tensor(name, [P, cols], dt))

    def sem(self, name):
        return self.stack.enter_context(self.nc.semaphore(name))

    def phase_sem(self, name):
        self.held.append(self.nc.alloc_semaphore(name))
        return self.held[-1]

    def end_phase(self):
        self.nc.clear_and_free_semaphores(self.held)
        self.held = []
        self.nc.all_engine_barrier()

    def dram(self, name, shape, dt=F32):
        return self.nc.dram_tensor(name, shape, dt).ap()


def bc(ap, axis, n):
    ap = ap.unsqueeze(axis)
    shape = list(ap.shape)
    shape[axis] = n
    return ap.to_broadcast(shape)


def load_constants(core, T):
    nc = core.nc
    T.cst = core.sb("cst", [P, C_COLS])
    T.idb = core.sb("idb", [P, P], BF16)
    T.mqb = core.sb("mqb", [P, P], BF16)
    T.mkb = core.sb("mkb", [P, P], BF16)
    T.zero = core.sb("zero", [P, D])
    T.idf = T.cst[:, C_ID:C_ID + P]
    cst_in = core.sem("cst_in")
    zero_done = core.sem("zero_done")
    with nc.Block() as block:
        @block.sync
        def _(sp):
            sp.dma_start(T.cst[:, :], T.cst_dram).then_inc(cst_in, 16)

        @block.gpsimd
        def _(pool):
            pool.memset(T.zero[:, :], 0.0).then_inc(zero_done, 1)

        @block.vector
        def _(dve):
            dve.wait_ge(cst_in, 16)
            dve.tensor_copy(T.idb[:, :], T.idf)
            dve.tensor_copy(T.mqb[:, :], T.cst[:, C_MQ:C_MQ + P])
            dve.tensor_copy(T.mkb[:, :], T.cst[:, C_MK:C_MK + P])


def row_stats(core, dve, X2, bs, mean, dif, var, stat, merged):
    with dve.Fori(0, NT) as t:
        dve.bn_stats(bs[:, :, :].rearrange("p t s -> p (t s)")[:, bass.ds(t * 6, 6)],
                     X2[:, bass.ds(t * D, D)]).then_inc(stat, 1)
    dve.wait_ge(stat, NT)
    dve.tensor_tensor(mean[:, :], bs[:, :, 1], bs[:, :, 4], ALU.add).then_inc(merged, 1)
    dve.tensor_tensor(dif[:, :], bs[:, :, 1], bs[:, :, 4], ALU.subtract).then_inc(merged, 1)
    dve.tensor_tensor(var[:, :], bs[:, :, 2], bs[:, :, 5], ALU.add).then_inc(merged, 1)
    dve.wait_ge(merged, 3)
    dve.tensor_scalar(mean[:, :], mean[:, :], 0.5, None, ALU.mult).then_inc(merged, 1)
    dve.tensor_tensor(dif[:, :], dif[:, :], dif[:, :], ALU.mult).then_inc(merged, 1)
    dve.tensor_scalar(var[:, :], var[:, :], 1.0 / D, EPS, ALU.mult, ALU.add).then_inc(merged, 1)
    dve.wait_ge(merged, 6)
    return dve.scalar_tensor_tensor(var[:, :], dif[:, :], 0.25, var[:, :], ALU.mult, ALU.add)


def norm_project(core, T, L, x_dram, w_dram, X):
    nc = core.nc
    W3 = 3 * D
    with ExitStack() as st:
        sb = lambda n, s, d=F32: core.sb(f"a{L}_{n}", s, d, st)
        ps = lambda n, c, d=F32: core.ps(f"a{L}_{n}", c, d, st)
        sem = lambda n: core.phase_sem(f"a{L}_{n}")
        w = sb("w", [P, KD, W3])
        cent = sb("cent", [P, KD, NE])
        bs = sb("bs", [P, NT, 6])
        mean = sb("mean", [P, NT])
        dif = sb("dif", [P, NT])
        var = sb("var", [P, NT])
        std = sb("std", [P, NT])
        rstd = sb("rstd", [P, NT])
        xs = [sb(f"xs{u}", [P, D]) for u in range(2)]
        xT = [sb(f"xT{u}", [P, D]) for u in range(2)]
        qs = [sb(f"qs{u}", [P, W3]) for u in range(2)]
        psT = [ps(f"psT{u}", 512) for u in range(2)]
        psQ = [ps(f"psQ{u}", 1024) for u in range(2)]
        x_in = [sem(f"x_in{q}") for q in range(4)]
        w_in = sem("w_in")
        stat = sem("stat")
        merged = sem("merged")
        var_ok = sem("var_ok")
        std_ok = sem("std_ok")
        rstd_ok = sem("rstd_ok")
        xn_ready = sem("xn_ready")
        xn_kept = sem("xn_kept")
        transposed = sem("transposed")
        xT_ready = sem("xT_ready")
        projected = sem("projected")
        left_act = sem("left_act")
        left_dve = sem("left_dve")
        out = [sem(f"out{u}") for u in range(2)]
        xn_out = sem("xn_out")
        X2 = X[:, :, :].rearrange("p t d -> p (t d)")
        aff2 = T.aff[:, :, :].rearrange("p t e -> p (t e)")
        xd = x_dram.rearrange("(t p) d -> p t d", p=P)
        if L:
            bias = sb("bias", [P, W3])
            cosT = sb("cos", [P, TS * DH // 2])
            sinT = sb("sin", [P, TS * DH // 2])
            qo = [sb(f"qo{u}", [P, NG, 2 * GW]) for u in range(2)]
            dm = [sb(f"dm{u}", [P, 2, NG * 2 * HG * DH // 2]) for u in range(2)]
            pm = [sb(f"pm{u}", [P, 2, NG * 2 * HG * DH // 2]) for u in range(2)]
            tab_in = sem("tab_in")
            passed = sem("passed")
            biased = sem("biased")
            dve_mul = sem("dve_mul")
            pool_mul = sem("pool_mul")
            turned_even = sem("turned_even")
            turned_odd = sem("turned_odd")
            outq = [sem(f"outq{u}") for u in range(2)]

        with nc.Block() as block:
            @block.sync
            def _(sp):
                for q in range(4):
                    sp.dma_start(X[:, 8 * q:8 * q + 8, :], xd[:, 8 * q:8 * q + 8, :]).then_inc(x_in[q], 16)
                    if q == 0:
                        sp.dma_start(w[:, :, :], w_dram.rearrange("(k p) n -> p k n", p=P)).then_inc(w_in, 16)
                        if L == 0:
                            sp.dma_start(cent[:, :, :],
                                         T.cent_dram.rearrange("(k p) n -> p k n", p=P)).then_inc(w_in, 16)
                        else:
                            sp.dma_start(bias[:, :], T.bqkv_dram.partition_broadcast(P)).then_inc(tab_in, 16)
                            sp.dma_start(cosT[:, :], T.cos_dram).then_inc(tab_in, 16)
                            sp.dma_start(sinT[:, :], T.sin_dram).then_inc(tab_in, 16)
                if L == 0:
                    for e in range(NE):
                        sp.dma_start(T.w1[:, e, :, :], T.w1_dram[e].rearrange("(k p) f -> p k f", p=P))\
                            .then_inc(T.w1_in, 16)
                        sp.dma_start(T.w2[:, e, :, :], T.w2_dram[e].rearrange("(k p) d -> p k d", p=P))\
                            .then_inc(T.w2_in, 16)
                sp.sem_inc(out[0], 16)
                sp.sem_inc(out[1], 16)
                if L:
                    sp.sem_inc(outq[0], 16)
                    sp.sem_inc(outq[1], 16)
                for b in range(NB):
                    with sp.Fori(0, TS // 2) as i:
                        for u in range(2):
                            n = b * TS + 2 * i + u
                            dst = T.qkv[b * NG:b * NG + NG].rearrange("g p t c -> p g t c")[
                                :, :, bass.ds(2 * i + u, 1), :]
                            src = qs[u][:, :].rearrange("p (g t c) -> p g t c", g=NG, t=1)
                            if L == 0:
                                sp.wait_ge(left_act, n + 3)
                                sp.wait_ge(left_dve, n + 3)
                                sp.dma_start(dst, src).then_inc(out[u], 16)
                            else:
                                sp.wait_ge(biased, n + 3)
                                sp.dma_start(dst[:, :, :, 2 * GW:3 * GW],
                                             src[:, :, :, 2 * GW:3 * GW]).then_inc(out[u], 16)
                                sp.wait_ge(turned_even, n + 1)
                                sp.sem_inc(passed, 1)
                                sp.wait_ge(turned_odd, n + 3)
                                sp.sem_inc(passed, 1)
                                sp.dma_start(dst[:, :, :, 0:2 * GW],
                                             qo[u][:, :, :].rearrange("p g (t c) -> p g t c", t=1))\
                                    .then_inc(outq[u], 16)
                sp.wait_ge(xn_kept, NT)
                sp.dma_start(T.xn_dram.rearrange("(t p) d -> p t d", p=P), X[:, :, :]).then_inc(xn_out, 16)
                for u in range(2):
                    sp.wait_ge(out[u], 16 * (NT // 2 + 1))
                    if L:
                        sp.wait_ge(outq[u], 16 * (NT // 2 + 1))
                sp.wait_ge(xn_out, 16)

            @block.vector
            def _(dve):
                dve.sem_inc(biased if L else left_dve, 2)
                for q in range(4):
                    dve.wait_ge(x_in[q], 16)
                row_stats(core, dve, X2, bs, mean, dif, var, stat, merged).then_inc(var_ok, 1)
                dve.wait_ge(std_ok, 1)
                dve.reciprocal(rstd[:, :], std[:, :]).then_inc(rstd_ok, 1)
                dve.wait_ge(rstd_ok, 1)
                if L:
                    dve.wait_ge(tab_in, 48)
                for b in range(NB):
                    with dve.Fori(0, TS // 2) as i:
                        for u in range(2):
                            n = b * TS + 2 * i + u
                            dve.wait_ge(transposed, n + 1)
                            x_t = X2[:, bass.ds(n * D, D)]
                            mu, rs = mean[:, bass.ds(n, 1)], rstd[:, bass.ds(n, 1)]
                            dve.tensor_scalar(xs[u][:, :], x_t, mu, rs, ALU.subtract, ALU.mult)\
                                .then_inc(xn_ready, 1)
                            dve.tensor_scalar(x_t, x_t, mu, rs, ALU.subtract, ALU.mult)\
                                .then_inc(xn_kept, 1)
                        for u in range(2):
                            n = b * TS + 2 * i + u
                            dve.wait_ge(projected, n + 3)
                            dve.wait_ge(out[u], 16 * (b * TS // 2 + i) + 16)
                            if L == 0:
                                dve.tensor_copy(qs[u][:, 512:W3], psQ[u][:, 512:W3])
                                dve.tensor_copy(aff2[:, bass.ds(n * NE, NE)],
                                                psQ[u][:, W3:W3 + NE]).then_inc(left_dve, 1)
                                continue
                            dve.wait_ge(turned_odd, n + 1)
                            dve.tensor_tensor(qs[u][:, :], psQ[u][:, 0:W3], bias[:, :], ALU.add)\
                                .then_inc(biased, 1)
                            dve.wait_ge(biased, n + 3)
                            dve.wait_ge(outq[u], 16 * (b * TS // 2 + i) + 16)
                            qk = qs[u][:, :].rearrange("p (g c) -> p g c", g=NG)[:, :, 0:2 * GW]\
                                .rearrange("p g (h f z) -> p g h f z", f=DH // 2, z=2)
                            o = qo[u][:, :, :].rearrange("p g (h f z) -> p g h f z", f=DH // 2, z=2)
                            tab = lambda t_: t_[:, bass.ds((2 * i + u) * (DH // 2), DH // 2)]
                            m = dm[u][:, :, :].rearrange("p a (g h f) -> p a g h f", g=NG, f=DH // 2)
                            cs = bc(bc(tab(cosT), 1, 2 * HG), 1, NG)
                            sn = bc(bc(tab(sinT), 1, 2 * HG), 1, NG)
                            dve.tensor_tensor(m[:, 0], qk[:, :, :, :, 0], cs, ALU.mult)
                            dve.tensor_tensor(m[:, 1], qk[:, :, :, :, 1], sn, ALU.mult).then_inc(dve_mul, 1)
                            dve.wait_ge(dve_mul, n + 1)
                            dve.tensor_tensor(o[:, :, :, :, 0], m[:, 0], m[:, 1], ALU.subtract)\
                                .then_inc(turned_even, 1)

            if L:
                @block.gpsimd
                def _(pool):
                    pool.sem_inc(turned_odd, 2)
                    pool.wait_ge(tab_in, 48)
                    for b in range(NB):
                        with pool.Fori(0, TS // 2) as i:
                            for u in range(2):
                                n = b * TS + 2 * i + u
                                pool.wait_ge(biased, n + 3)
                                pool.wait_ge(outq[u], 16 * (b * TS // 2 + i) + 16)
                                qk = qs[u][:, :].rearrange("p (g c) -> p g c", g=NG)[:, :, 0:2 * GW]\
                                    .rearrange("p g (h f z) -> p g h f z", f=DH // 2, z=2)
                                o = qo[u][:, :, :].rearrange("p g (h f z) -> p g h f z", f=DH // 2, z=2)
                                tab = lambda t_: t_[:, bass.ds((2 * i + u) * (DH // 2), DH // 2)]
                                m = pm[u][:, :, :].rearrange("p a (g h f) -> p a g h f", g=NG, f=DH // 2)
                                cs = bc(bc(tab(cosT), 1, 2 * HG), 1, NG)
                                sn = bc(bc(tab(sinT), 1, 2 * HG), 1, NG)
                                pool.tensor_tensor(m[:, 0], qk[:, :, :, :, 0], sn, ALU.mult)\
                                    .then_inc(pool_mul, 1)
                                pool.tensor_tensor(m[:, 1], qk[:, :, :, :, 1], cs, ALU.mult)\
                                    .then_inc(pool_mul, 1)
                                pool.wait_ge(pool_mul, 2 * n + 2)
                                pool.tensor_tensor(o[:, :, :, :, 1], m[:, 0], m[:, 1], ALU.add)\
                                    .then_inc(turned_odd, 1)

            @block.scalar
            def _(act):
                act.sem_inc(xT_ready, 2)
                act.sem_inc(left_act, 2)
                act.wait_ge(var_ok, 1)
                act.activation(std[:, :], var[:, :], ACT.Sqrt).then_inc(std_ok, 1)
                with act.Fori(0, NT // 2) as i:
                    for u in range(2):
                        n = 2 * i + u
                        act.wait_ge(transposed, n + 3)
                        act.wait_ge(projected, n + 1)
                        act.copy(xT[u][:, :], psT[u][:, 0:D]).then_inc(xT_ready, 1)
                    if L == 0:
                        for u in range(2):
                            n = 2 * i + u
                            act.wait_ge(projected, n + 3)
                            act.wait_ge(out[u], 16 * i + 16)
                            act.copy(qs[u][:, 0:512], psQ[u][:, 0:512]).then_inc(left_act, 1)

            @block.tensor
            def _(pe):
                pe.sem_inc(transposed, 2)
                pe.sem_inc(projected, 2)
                pe.wait_ge(w_in, 16 if L else 32)
                with pe.Fori(0, NT // 2) as i:
                    for u in range(2):
                        n = 2 * i + u
                        pe.wait_ge(xn_ready, n + 1)
                        pe.wait_ge(xT_ready, n + 1)
                        for k in range(KD):
                            t = pe.transpose(psT[u][:, k * P:k * P + P], xs[u][:, k * P:k * P + P], T.idf)
                        t.then_inc(transposed, 1)
                    for u in range(2):
                        n = 2 * i + u
                        pe.wait_ge(xT_ready, n + 3)
                        if L == 0:
                            pe.wait_ge(left_act, n + 1)
                            pe.wait_ge(left_dve, n + 1)
                        else:
                            pe.wait_ge(biased, n + 1)
                        for a, z in ((0, 512), (512, W3)):
                            for k in range(KD):
                                m = pe.matmul(psQ[u][:, a:z], xT[u][:, k * P:k * P + P], w[:, k, a:z],
                                              start=(k == 0), stop=(k == KD - 1))
                        if L == 0:
                            for k in range(KD):
                                m = pe.matmul(psQ[u][:, W3:W3 + NE], xT[u][:, k * P:k * P + P],
                                              cent[:, k, :], start=(k == 0), stop=(k == KD - 1))
                        m.then_inc(projected, 1)
        core.end_phase()


def norm_again(core, X):
    nc = core.nc
    with ExitStack() as st:
        sb = lambda n, s, d=F32: core.sb(f"n_{n}", s, d, st)
        sem = lambda n: core.phase_sem(f"n_{n}")
        bs = sb("bs", [P, NT, 6])
        mean, dif, var, std, rstd = (sb(n, [P, NT]) for n in ("mean", "dif", "var", "std", "rstd"))
        stat, merged, var_ok, std_ok, rstd_ok = (sem(n) for n in ("stat", "merged", "var_ok", "std_ok", "rstd_ok"))
        X2 = X[:, :, :].rearrange("p t d -> p (t d)")
        with nc.Block() as block:
            @block.vector
            def _(dve):
                row_stats(core, dve, X2, bs, mean, dif, var, stat, merged).then_inc(var_ok, 1)
                dve.wait_ge(std_ok, 1)
                dve.reciprocal(rstd[:, :], std[:, :]).then_inc(rstd_ok, 1)
                dve.wait_ge(rstd_ok, 1)
                with dve.Fori(0, NT) as n:
                    x_t = X2[:, bass.ds(n * D, D)]
                    dve.tensor_scalar(x_t, x_t, mean[:, bass.ds(n, 1)], rstd[:, bass.ds(n, 1)],
                                      ALU.subtract, ALU.mult)

            @block.scalar
            def _(act):
                act.wait_ge(var_ok, 1)
                act.activation(std[:, :], var[:, :], ACT.Sqrt).then_inc(std_ok, 1)
        core.end_phase()


def scores_of_layer1(core, T, X):
    nc = core.nc
    with ExitStack() as st:
        sb = lambda n, s, d=F32: core.sb(f"r_{n}", s, d, st)
        ps = lambda n, c, d=F32: core.ps(f"r_{n}", c, d, st)
        sem = lambda n: core.phase_sem(f"r_{n}")
        nw = sb("nw", [P, D])
        gw = sb("gw", [P, KD, NE], BF16)
        gb = sb("gb", [P, NE], BF16)
        xc = sb("xc", [P, NT, D], BF16)
        sq = [sb(f"sq{u}", [P, D]) for u in range(2)]
        ss = sb("ss", [P, NT])
        ms = sb("ms", [P, NT])
        std = sb("std", [P, NT])
        rstd = sb("rstd", [P, NT])
        nT = [sb(f"nT{u}", [P, D], BF16) for u in range(2)]
        lg = sb("lg", [P, NT, NE], BF16)
        psT = [ps(f"psT{u}", 1024, BF16) for u in range(2)]
        psL = [ps(f"psL{u}", 512) for u in range(2)]
        tab_in = sem("tab_in")
        cast = sem("cast")
        squared = sem("squared")
        mean_ok = sem("mean_ok")
        std_ok = sem("std_ok")
        rstd_ok = sem("rstd_ok")
        normed = sem("normed")
        transposed = sem("transposed")
        copied = sem("copied")
        scored = sem("scored")
        left = sem("left")
        X2 = X[:, :, :].rearrange("p t d -> p (t d)")
        xc2 = xc[:, :, :].rearrange("p t d -> p (t d)")
        nf2 = T.nf[:, :, :].rearrange("p t d -> p (t d)")
        lg2 = lg[:, :, :].rearrange("p t e -> p (t e)")
        with nc.Block() as block:
            @block.sync
            def _(sp):
                sp.dma_start(nw[:, :], T.nw_dram.partition_broadcast(P)).then_inc(tab_in, 16)
                sp.dma_start(gw[:, :, :], T.gw_dram.rearrange("(k p) n -> p k n", p=P)).then_inc(tab_in, 16)
                sp.dma_start(gb[:, :], T.gb_dram.partition_broadcast(P)).then_inc(tab_in, 16)

            @block.vector
            def _(dve):
                dve.sem_inc(left, 2)
                with dve.Fori(0, NT // 8) as i:
                    dve.tensor_copy(xc2[:, bass.ds(i * 8 * D, 8 * D)],
                                    X2[:, bass.ds(i * 8 * D, 8 * D)]).then_inc(cast, 1)
                dve.wait_ge(squared, NT + 2)
                dve.tensor_scalar(ms[:, :], ss[:, :], 1.0 / D, EPS, ALU.mult, ALU.add).then_inc(mean_ok, 1)
                dve.wait_ge(std_ok, 1)
                dve.reciprocal(rstd[:, :], std[:, :]).then_inc(rstd_ok, 1)
                dve.wait_ge(rstd_ok, 1)
                dve.wait_ge(tab_in, 48)
                with dve.Fori(0, NT // 2) as i:
                    for u in range(2):
                        n = 2 * i + u
                        dve.scalar_tensor_tensor(nf2[:, bass.ds(n * D, D)], xc2[:, bass.ds(n * D, D)],
                                                 rstd[:, bass.ds(n, 1)], nw[:, :],
                                                 ALU.mult, ALU.mult).then_inc(normed, 1)
                    for u in range(2):
                        n = 2 * i + u
                        dve.wait_ge(scored, n + 3)
                        dve.tensor_tensor(lg2[:, bass.ds(n * NE, NE)], psL[u][:, 0:NE], gb[:, :],
                                          ALU.add).then_inc(left, 1)
                dve.wait_ge(left, NT + 2)
                dve.tensor_copy(T.aff[:, :, :], lg[:, :, :])

            @block.scalar
            def _(act):
                act.sem_inc(copied, 2)
                act.wait_ge(cast, NT // 8)
                act.sem_inc(squared, 2)
                with act.Fori(0, NT // 2) as i:
                    for u in range(2):
                        n = 2 * i + u
                        act.wait_ge(squared, n + 1)
                        act.activation(sq[u][:, :], xc2[:, bass.ds(n * D, D)], ACT.Square,
                                       accum_out=ss[:, bass.ds(n, 1)]).then_inc(squared, 1)
                act.wait_ge(mean_ok, 1)
                act.activation(std[:, :], ms[:, :], ACT.Sqrt).then_inc(std_ok, 1)
                with act.Fori(0, NT // 2) as i:
                    for u in range(2):
                        n = 2 * i + u
                        act.wait_ge(transposed, n + 1)
                        act.wait_ge(scored, n + 1)
                        act.copy(nT[u][:, :], psT[u][:, 0:D]).then_inc(copied, 1)

            @block.tensor
            def _(pe):
                pe.sem_inc(scored, 2)
                pe.wait_ge(tab_in, 48)
                with pe.Fori(0, NT // 2) as i:
                    for u in range(2):
                        n = 2 * i + u
                        pe.wait_ge(normed, n + 1)
                        pe.wait_ge(copied, n + 1)
                        for k in range(KD):
                            t = pe.transpose(psT[u][:, k * P:k * P + P], nf2[:, bass.ds(n * D + k * P, P)],
                                             T.idb[:, :])
                        t.then_inc(transposed, 1)
                    for u in range(2):
                        n = 2 * i + u
                        pe.wait_ge(copied, n + 3)
                        pe.wait_ge(left, n + 1)
                        for k in range(KD):
                            m = pe.matmul(psL[u][:, 0:NE], nT[u][:, k * P:k * P + P], gw[:, k, :],
                                          start=(k == 0), stop=(k == KD - 1))
                        m.then_inc(scored, 1)
        core.end_phase()


def route(core, T, L):
    nc = core.nc
    NCH = L + 1
    NV = NCH * NT
    NS = (SLOT1 if L else SLOT0) + 1
    with ExitStack() as st:
        sb = lambda n, s, d=F32: core.sb(f"t{L}_{n}", s, d, st)
        ps = lambda n, c, d=F32: core.ps(f"t{L}_{n}", c, d, st)
        sem = lambda n: core.phase_sem(f"t{L}_{n}")
        aff = sb("aff", [P, NT, NE])
        mx = sb("mx", [P, NCH, NT])
        eq = sb("eq", [P, NT, NE])
        pk = sb("pk", [P, NT])
        oh = sb("oh", [P, NV, NE])
        tot = sb("tot", [P, NV, NE])
        run = [sb(f"run{i}", [P, NV, NE]) for i in range(2)]
        over = sb("over", [P, NE, NV])
        nt_e = sb("nt_e", [P, NE])
        cum = [sb(f"cum{i}", [P, NE]) for i in range(2)]
        base = sb("base", [P, NE])
        past = sb("past", [P, NS, NE])
        eidf = sb("eidf", [P, NS])
        where = sb("where", [P, NV, NE])
        posf = sb("posf", [P, NV])
        ex = sb("ex", [P, 3, NT])
        psR = ps("psR", 512)
        psS = ps("psS", 512)
        step = sem("step")
        onehot = sem("onehot")
        ranked = sem("ranked")
        differ = sem("differ")
        expd = sem("expd")
        placed = sem("placed")
        scattered = sem("scattered")
        k128 = T.cst[:, C_K128:C_K128 + NV]
        slot = T.cst[:, C_SLOT:C_SLOT + NS]
        pick = T.cst[:, C_PICK:C_PICK + NE]
        with nc.Block() as block:
            @block.vector
            def _(dve):
                done = [0]

                def then(ins):
                    done[0] += 1
                    ins.then_inc(step, 1)
                    dve.wait_ge(step, done[0])

                then(dve.tensor_copy(aff[:, :, :], T.aff[:, :, :]))
                for c in range(NCH):
                    ohc = oh[:, c * NT:(c + 1) * NT, :]
                    then(dve.tensor_reduce(mx[:, c, :], aff[:, :, :], AX.X, ALU.max))
                    then(dve.tensor_tensor(eq[:, :, :], aff[:, :, :], bc(mx[:, c, :], 2, NE), ALU.is_ge))
                    then(dve.tensor_tensor(eq[:, :, :], eq[:, :, :], bc(pick, 1, NT), ALU.mult))
                    then(dve.tensor_reduce(pk[:, :], eq[:, :, :], AX.X, ALU.max))
                    then(dve.tensor_tensor(ohc, bc(pk[:, :], 2, NE), bc(pick, 1, NT), ALU.is_equal))
                    if c + 1 < NCH:
                        then(dve.scalar_tensor_tensor(aff[:, :, :], ohc, BIG, aff[:, :, :],
                                                      ALU.mult, ALU.add))
                dve.sem_inc(onehot, 1)
                dve.wait_ge(ranked, 1)
                then(dve.tensor_copy(tot[:, :, :].rearrange("p t e -> p (t e)"), psS[:, 0:NV * NE]))
                src, sh, k = tot, 1, 0
                while sh < NV:
                    dst = run[k % 2]
                    dve.tensor_copy(dst[:, 0:sh, :], src[:, 0:sh, :])
                    then(dve.tensor_tensor(dst[:, sh:NV, :], src[:, sh:NV, :], src[:, 0:NV - sh, :], ALU.add))
                    src, sh, k = dst, 2 * sh, k + 1
                count = src[:, NV - 1, :]
                then(dve.tensor_tensor(over[:, :, :], bc(count, 2, NV), bc(k128, 1, NE), ALU.is_gt))
                then(dve.tensor_reduce(nt_e[:, :], over[:, :, :], AX.X, ALU.add))
                prev, sh, j = nt_e, 1, 0
                while sh < NE:
                    dst = cum[j % 2]
                    dve.tensor_copy(dst[:, 0:sh], prev[:, 0:sh])
                    then(dve.tensor_tensor(dst[:, sh:NE], prev[:, sh:NE], prev[:, 0:NE - sh], ALU.add))
                    prev, sh, j = dst, 2 * sh, j + 1
                then(dve.tensor_tensor(base[:, :], prev[:, :], nt_e[:, :], ALU.subtract))
                then(dve.tensor_scalar(base[:, :], base[:, :], float(P), None, ALU.mult))
                then(dve.tensor_tensor(past[:, :, :], bc(slot, 2, NE), bc(prev[:, :], 1, NS), ALU.is_ge))
                then(dve.tensor_reduce(eidf[:, :], past[:, :, :], AX.X, ALU.add))
                then(dve.tensor_scalar(eidf[:, :], eidf[:, :], float(NE - 1), None, ALU.min))
                dve.tensor_copy(T.eid[:, 0:NS], eidf[:, :])
                then(dve.tensor_tensor(where[:, :, :], src[:, :, :], tot[:, :, :], ALU.subtract))
                then(dve.tensor_tensor(where[:, :, :], where[:, :, :], bc(base[:, :], 1, NV), ALU.add))
                then(dve.tensor_tensor(where[:, :, :].rearrange("p t e -> p (t e)"),
                                       where[:, :, :].rearrange("p t e -> p (t e)"),
                                       psR[:, 0:NV * NE], ALU.add))
                then(dve.tensor_tensor(where[:, :, :], where[:, :, :], oh[:, :, :], ALU.mult))
                then(dve.tensor_reduce(posf[:, :], where[:, :, :], AX.X, ALU.add))
                dve.tensor_copy(T.pos[:, 0:NV], posf[:, :]).then_inc(placed, 1)
                if L == 0:
                    dve.tensor_copy(T.top[:, 0, :], mx[:, 0, :])
                else:
                    dve.tensor_tensor(ex[:, 0, :], mx[:, 1, :], mx[:, 0, :], ALU.subtract).then_inc(differ, 1)
                    dve.wait_ge(expd, 1)
                    then(dve.tensor_scalar(ex[:, 2, :], ex[:, 1, :], 1.0, None, ALU.add))
                    then(dve.reciprocal(T.top[:, 0, :], ex[:, 2, :]))
                    then(dve.tensor_tensor(T.top[:, 1, :], ex[:, 1, :], T.top[:, 0, :], ALU.mult))

            @block.scalar
            def _(act):
                if L:
                    act.wait_ge(differ, 1)
                    act.activation(ex[:, 1, :], ex[:, 0, :], ACT.Exp).then_inc(expd, 1)

            @block.tensor
            def _(pe):
                pe.wait_ge(onehot, 1)
                flat = oh[:, :, :].rearrange("p t e -> p (t e)")
                pe.matmul(psR[:, 0:NV * NE], T.cst[:, C_UP:C_UP + P], flat, start=True, stop=True)
                pe.matmul(psS[:, 0:NV * NE], T.cst[:, C_ONE:C_ONE + P], flat, start=True, stop=True)\
                    .then_inc(ranked, 1)

            @block.gpsimd
            def _(pool):
                pool.wait_ge(placed, 1)
                pool.wait_ge(T.cleared[L], 16)
                for v in range(NV):
                    rows = T.nf[:, v % NT, :] if L else T.X[:, v, :]
                    pool.indirect_dma_start(
                        out=T.sorted_dram[L], out_offset=bass.IndirectOffsetOnAxis(ap=T.pos[:, v:v + 1], axis=0),
                        in_=rows, in_offset=None).then_inc(scattered, 16)
                pool.wait_ge(scattered, 16 * NV)
        core.end_phase()


def experts0(core, T):
    nc = core.nc
    with ExitStack() as st:
        sb = lambda n, s, d=F32: core.sb(f"e0_{n}", s, d, st)
        ps = lambda n, c, d=F32: core.ps(f"e0_{n}", c, d, st)
        sem = lambda n: core.phase_sem(f"e0_{n}")
        FC = F0 // P
        b1 = sb("b1", [P, NE * F0])
        b2 = sb("b2", [P, NE * D])
        gb = sb("gb", [P, NE, 2, KD])
        xs = [sb(f"xs{u}", [P, D]) for u in range(2)]
        xT = [sb(f"xT{u}", [P, KD, P]) for u in range(2)]
        h = sb("h", [P, F0])
        hT = sb("hT", [P, F0])
        y = [sb(f"y{u}", [P, D]) for u in range(2)]
        psT = ps("psT", 512)
        psH = ps("psH", 1024)
        psG = ps("psG", 1024)
        psY = ps("psY", 512)
        tab_in = sem("tab_in")
        x_in = [sem(f"x_in{u}") for u in range(2)]
        y_out = [sem(f"y_out{u}") for u in range(2)]
        x_turned = sem("x_turned")
        xT_ready = sem("xT_ready")
        hidden = sem("hidden")
        h_ready = sem("h_ready")
        h_turned = sem("h_turned")
        hT_ready = sem("hT_ready")
        result = sem("result")
        y_ready = sem("y_ready")
        w1f = T.w1[:, :, :, :].rearrange("p e k f -> p (e k f)")
        w2f = T.w2[:, :, :, :].rearrange("p e k d -> p (e k d)")
        gbf = gb[:, :, :, :].rearrange("p e a k -> p (e a k)")
        xd = T.sorted_dram[0].rearrange("(s p) d -> s p d", p=P)
        yd = T.result_dram[0].rearrange("(s p) d -> s p d", p=P)
        NS = SLOT0
        with nc.Block() as block:
            @block.sync
            def _(sp):
                sp.dma_start(gb[:, :, :, :], T.gb0_dram.rearrange("p (e a k) -> p e a k", e=NE, a=2))\
                    .then_inc(tab_in, 16)
                sp.dma_start(b1[:, :], T.b1_dram.partition_broadcast(P)).then_inc(tab_in, 16)
                sp.dma_start(b2[:, :], T.b2_dram.partition_broadcast(P)).then_inc(tab_in, 16)
                sp.sem_inc(y_out[0], 16)
                sp.sem_inc(y_out[1], 16)
                sp.dma_start(xs[0][:, :], xd[0]).then_inc(x_in[0], 16)
                with sp.Fori(0, NS // 2) as i:
                    for u in range(2):
                        s = 2 * i + u
                        sp.wait_ge(x_turned, s + 2)
                        sp.dma_start(xs[1 - u][:, :], xd[bass.ds(s + 1, 1)].rearrange("s p d -> (s p) d"))\
                            .then_inc(x_in[1 - u], 16)
                        sp.wait_ge(y_ready, s + 2)
                        sp.dma_start(yd[bass.ds(s, 1)].rearrange("s p d -> (s p) d"), y[u][:, :])\
                            .then_inc(y_out[u], 16)
                for u in range(2):
                    sp.wait_ge(y_out[u], 16 * (NS // 2 + 1))
                sp.wait_ge(x_in[0], 16 * (NS // 2 + 1))

            @block.vector
            def _(dve):
                dve.sem_inc(h_ready, 1)
                dve.sem_inc(y_ready, 1)
                dve.wait_ge(tab_in, 48)
                def bias1(s):
                    e = dve.value_load(T.eid[0:1, bass.ds(s, 1)], min_val=0, max_val=NE - 1)
                    dve.wait_ge(hidden, s + 3)
                    dve.wait_ge(h_turned, s + 1)
                    dve.tensor_tensor(h[:, :], psH[:, :], b1[:, bass.ds(e * F0, F0)], ALU.add)\
                        .then_inc(h_ready, 1)

                def bias2(s, u, k_out):
                    e = dve.value_load(T.eid[0:1, bass.ds(s, 1)], min_val=0, max_val=NE - 1)
                    dve.wait_ge(result, s + 2)
                    dve.wait_ge(y_out[u], k_out)
                    dve.tensor_tensor(y[u][:, :], psY[:, 0:D], b2[:, bass.ds(e * D, D)], ALU.add)\
                        .then_inc(y_ready, 1)

                bias1(0)
                with dve.Fori(0, NS // 2) as i:
                    for u in range(2):
                        s = 2 * i + u
                        bias1(s + 1)
                        bias2(s, u, 16 * i + 16)

            @block.scalar
            def _(act):
                act.sem_inc(xT_ready, 1)
                act.sem_inc(hT_ready, 1)
                act.wait_ge(tab_in, 48)

                def affine(u, s):
                    e = act.value_load(T.eid[0:1, bass.ds(s, 1)], min_val=0, max_val=NE - 1)
                    act.wait_ge(x_turned, s + 3)
                    act.wait_ge(hidden, s + 1)
                    for k in range(KD):
                        a = act.activation(xT[u][:, k, :], psT[:, k * P:k * P + P], ACT.Identity,
                                           scale=gbf[:, bass.ds(e * 4 + k, 1)],
                                           bias=gbf[:, bass.ds(e * 4 + 2 + k, 1)])
                    a.then_inc(xT_ready, 1)

                affine(0, 0)
                with act.Fori(0, NS // 2) as i:
                    for u in range(2):
                        s = 2 * i + u
                        act.wait_ge(h_turned, s + 2)
                        act.wait_ge(result, s + 1)
                        for a in range(2):
                            r = act.activation(hT[:, a * 512:a * 512 + 512], psG[:, a * 512:a * 512 + 512],
                                               ACT.Relu)
                        r.then_inc(hT_ready, 1)
                        affine(1 - u, s + 1)

            @block.tensor
            def _(pe):
                pe.sem_inc(x_turned, 2)
                pe.sem_inc(hidden, 2)
                pe.sem_inc(h_turned, 1)
                pe.sem_inc(result, 1)
                pe.wait_ge(T.w1_in, 16 * NE)
                pe.wait_ge(T.w2_in, 16 * NE)

                def turn_x(u, s, loads):
                    pe.wait_ge(x_in[u], 16 * loads)
                    pe.wait_ge(xT_ready, s + 1)
                    for k in range(KD):
                        t = pe.transpose(psT[:, k * P:k * P + P], xs[u][:, k * P:k * P + P], T.idf)
                    t.then_inc(x_turned, 1)

                def layer1(u, s):
                    e = pe.value_load(T.eid[0:1, bass.ds(s, 1)], min_val=0, max_val=NE - 1)
                    pe.wait_ge(xT_ready, s + 2)
                    pe.wait_ge(h_ready, s + 1)
                    for n in range(2):
                        for k in range(KD):
                            m = pe.matmul(psH[:, n * 512:n * 512 + 512], xT[u][:, k, :],
                                          w1f[:, bass.ds(e * (KD * F0) + k * F0 + n * 512, 512)],
                                          start=(k == 0), stop=(k == KD - 1))
                    m.then_inc(hidden, 1)

                turn_x(0, 0, 1)
                layer1(0, 0)
                with pe.Fori(0, NS // 2) as i:
                    for u in range(2):
                        s = 2 * i + u
                        pe.wait_ge(h_ready, s + 2)
                        pe.wait_ge(hT_ready, s + 1)
                        for f in range(FC):
                            t = pe.transpose(psG[:, f * P:f * P + P], h[:, f * P:f * P + P], T.idf)
                        t.then_inc(h_turned, 1)
                        turn_x(1 - u, s + 1, i + u + 1)
                        layer1(1 - u, s + 1)
                        e = pe.value_load(T.eid[0:1, bass.ds(s, 1)], min_val=0, max_val=NE - 1)
                        pe.wait_ge(hT_ready, s + 2)
                        pe.wait_ge(y_ready, s + 1)
                        for f in range(FC):
                            m = pe.matmul(psY[:, 0:D], hT[:, f * P:f * P + P],
                                          w2f[:, bass.ds(e * (FC * D) + f * D, D)],
                                          start=(f == 0), stop=(f == FC - 1))
                        m.then_inc(result, 1)
        core.end_phase()


def experts1(core, T):
    nc = core.nc
    with ExitStack() as st:
        sb = lambda n, s, d=F32: core.sb(f"e1_{n}", s, d, st)
        ps = lambda n, c, d=F32: core.ps(f"e1_{n}", c, d, st)
        sem = lambda n: core.phase_sem(f"e1_{n}")
        W = 2 * F1
        NPT = 3
        w1 = sb("w1", [P, NE, KD, W], BF16)
        w2 = sb("w2", [P, NE, F1 // P, D], BF16)
        b1h = sb("b1h", [P, NE * W], BF16)
        b2h = sb("b2h", [P, NE * D], BF16)
        xs = [sb(f"xs{u}", [P, D], BF16) for u in range(2)]
        xT = [sb(f"xT{u}", [P, KD, P], BF16) for u in range(2)]
        p1 = [sb(f"p1{u}", [P, W]) for u in range(2)]
        g = [sb(f"g{u}", [P, F1]) for u in range(2)]
        sg = [sb(f"sg{u}", [P, F1]) for u in range(2)]
        lin = [sb(f"lin{u}", [P, F1]) for u in range(2)]
        gl = [sb(f"gl{u}", [P, F1]) for u in range(2)]
        r1 = [sb(f"r1{u}", [P, F1]) for u in range(2)]
        r2 = [sb(f"r2{u}", [P, F1]) for u in range(2)]
        parts = [sb(f"parts{u}", [P, NPT, F1], BF16) for u in range(2)]
        aT = [sb(f"aT{u}", [P, NPT * F1], BF16) for u in range(2)]
        y = [sb(f"y{u}", [P, D]) for u in range(2)]
        psX = [ps(f"psX{u}", 1024, BF16) for u in range(2)]
        psP = [ps(f"psP{u}", 512) for u in range(2)]
        psA = [ps(f"psA{u}", 1024, BF16) for u in range(2)]
        psY = [ps(f"psY{u}", 512) for u in range(2)]
        tab_in = sem("tab_in")
        x_in = [sem(f"x_in{u}") for u in range(2)]
        y_out = [sem(f"y_out{u}") for u in range(2)]
        x_turned = sem("x_turned")
        xT_ready = sem("xT_ready")
        hidden = sem("hidden")
        p1_ready = sem("p1_ready")
        g_ready = sem("g_ready")
        sig_ready = sem("sig_ready")
        lin1 = sem("lin1")
        lin2 = sem("lin2")
        gl_ready = sem("gl_ready")
        acted = sem("acted")
        part1 = sem("part1")
        rest1 = sem("rest1")
        part2 = sem("part2")
        split = sem("split")
        a_turned = sem("a_turned")
        aT_ready = sem("aT_ready")
        result = sem("result")
        y_ready = sem("y_ready")
        w1f = w1[:, :, :, :].rearrange("p e k f -> p (e k f)")
        w2f = w2[:, :, :, :].rearrange("p e k d -> p (e k d)")
        xd = T.sorted_dram[1].rearrange("(s p) d -> s p d", p=P)
        yd = T.result_dram[1].rearrange("(s p) d -> s p d", p=P)
        NS = SLOT1
        with nc.Block() as block:
            @block.sync
            def _(sp):
                sp.dma_start(w1[:, :, :, :], T.m1_dram.rearrange("e (k p) f -> p e k f", p=P)).then_inc(tab_in, 16)
                sp.dma_start(w2[:, :, :, :], T.m2_dram.rearrange("e (k p) d -> p e k d", p=P)).then_inc(tab_in, 16)
                sp.dma_start(b1h[:, :], T.mb1_dram.partition_broadcast(P)).then_inc(tab_in, 16)
                sp.dma_start(b2h[:, :], T.mb2_dram.partition_broadcast(P)).then_inc(tab_in, 16)
                sp.sem_inc(y_out[0], 16)
                sp.sem_inc(y_out[1], 16)
                for u in range(2):
                    sp.dma_start(xs[u][:, :], xd[u]).then_inc(x_in[u], 16)
                with sp.Fori(0, NS // 2 - 1) as i:
                    for u in range(2):
                        s = 2 * i + u
                        sp.wait_ge(x_turned, s + 3)
                        sp.dma_start(xs[u][:, :], xd[bass.ds(s + 2, 1)].rearrange("s p d -> (s p) d"))\
                            .then_inc(x_in[u], 16)
                    for u in range(2):
                        s = 2 * i + u
                        sp.wait_ge(y_ready, s + 3)
                        sp.dma_start(yd[bass.ds(s, 1)].rearrange("s p d -> (s p) d"), y[u][:, :])\
                            .then_inc(y_out[u], 16)
                for u in range(2):
                    sp.wait_ge(y_ready, NS - 2 + u + 3)
                    sp.dma_start(yd[NS - 2 + u], y[u][:, :]).then_inc(y_out[u], 16)
                for u in range(2):
                    sp.wait_ge(y_out[u], 16 * (NS // 2 + 1))

            @block.vector
            def _(dve):
                dve.sem_inc(p1_ready, 2)
                dve.sem_inc(y_ready, 2)
                dve.wait_ge(tab_in, 64)
                with dve.Fori(0, NS // 2) as i:
                    for u in range(2):
                        s = 2 * i + u
                        e = dve.value_load(T.eid[0:1, bass.ds(s, 1)], min_val=0, max_val=NE - 1)
                        dve.wait_ge(hidden, s + 3)
                        dve.tensor_tensor(p1[u][:, :], psP[u][:, :], b1h[:, bass.ds(e * W, W)], ALU.add)\
                            .then_inc(p1_ready, 1)
                        dve.wait_ge(p1_ready, s + 3)
                        dve.tensor_scalar(g[u][:, :], p1[u][:, 0:F1], 7.0, None, ALU.min).then_inc(g_ready, 1)
                        dve.tensor_scalar(lin[u][:, :], p1[u][:, F1:W], 7.0, -7.0, ALU.min, ALU.max)\
                            .then_inc(lin1, 1)
                    for u in range(2):
                        s = 2 * i + u
                        dve.wait_ge(sig_ready, s + 1)
                        dve.tensor_tensor(gl[u][:, :], g[u][:, :], sg[u][:, :], ALU.mult).then_inc(gl_ready, 1)
                        dve.wait_ge(gl_ready, s + 1)
                        dve.wait_ge(lin1, s + 1)
                        dve.scalar_tensor_tensor(r1[u][:, :], lin[u][:, :], 1.0, gl[u][:, :], ALU.add, ALU.mult)\
                            .then_inc(acted, 1)
                        dve.wait_ge(acted, s + 1)
                        dve.wait_ge(a_turned, s + 1)
                        dve.tensor_copy(parts[u][:, 0, :], r1[u][:, :]).then_inc(part1, 1)
                        dve.wait_ge(part1, s + 1)
                        dve.tensor_tensor(r2[u][:, :], r1[u][:, :], parts[u][:, 0, :], ALU.subtract)\
                            .then_inc(rest1, 1)
                        dve.wait_ge(rest1, s + 1)
                        dve.tensor_copy(parts[u][:, 1, :], r2[u][:, :]).then_inc(part2, 1)
                        dve.wait_ge(part2, s + 1)
                        dve.tensor_tensor(parts[u][:, 2, :], r2[u][:, :], parts[u][:, 1, :], ALU.subtract)\
                            .then_inc(split, 1)
                    for u in range(2):
                        s = 2 * i + u
                        e = dve.value_load(T.eid[0:1, bass.ds(s, 1)], min_val=0, max_val=NE - 1)
                        dve.wait_ge(result, s + 3)
                        dve.wait_ge(y_out[u], 16 * i + 16)
                        dve.tensor_tensor(y[u][:, :], psY[u][:, 0:D], b2h[:, bass.ds(e * D, D)], ALU.add)\
                            .then_inc(y_ready, 1)

            @block.scalar
            def _(act):
                act.sem_inc(xT_ready, 2)
                act.sem_inc(aT_ready, 2)
                with act.Fori(0, NS // 2) as i:
                    for u in range(2):
                        s = 2 * i + u
                        act.wait_ge(x_turned, s + 3)
                        act.wait_ge(hidden, s + 1)
                        act.copy(xT[u][:, :, :].rearrange("p k t -> p (k t)"), psX[u][:, 0:D])\
                            .then_inc(xT_ready, 1)
                    for u in range(2):
                        s = 2 * i + u
                        act.wait_ge(g_ready, s + 1)
                        act.activation(sg[u][:, :], g[u][:, :], ACT.Sigmoid, scale=1.702).then_inc(sig_ready, 1)
                    for u in range(2):
                        s = 2 * i + u
                        act.wait_ge(a_turned, s + 3)
                        act.wait_ge(result, s + 1)
                        act.copy(aT[u][:, :], psA[u][:, 0:NPT * F1]).then_inc(aT_ready, 1)

            @block.tensor
            def _(pe):
                pe.sem_inc(x_turned, 2)
                pe.sem_inc(hidden, 2)
                pe.sem_inc(a_turned, 2)
                pe.sem_inc(result, 2)
                pe.wait_ge(tab_in, 64)
                with pe.Fori(0, NS // 2) as i:
                    for u in range(2):
                        s = 2 * i + u
                        pe.wait_ge(x_in[u], 16 * i + 16)
                        pe.wait_ge(xT_ready, s + 1)
                        for k in range(KD):
                            t = pe.transpose(psX[u][:, k * P:k * P + P], xs[u][:, k * P:k * P + P], T.idb[:, :])
                        t.then_inc(x_turned, 1)
                    for u in range(2):
                        s = 2 * i + u
                        e = pe.value_load(T.eid[0:1, bass.ds(s, 1)], min_val=0, max_val=NE - 1)
                        pe.wait_ge(xT_ready, s + 3)
                        pe.wait_ge(p1_ready, s + 1)
                        for k in range(KD):
                            m = pe.matmul(psP[u][:, :], xT[u][:, k, :], w1f[:, bass.ds(e * (KD * W) + k * W, W)],
                                          start=(k == 0), stop=(k == KD - 1))
                        m.then_inc(hidden, 1)
                    for u in range(2):
                        s = 2 * i + u
                        pe.wait_ge(split, s + 1)
                        pe.wait_ge(aT_ready, s + 1)
                        for a in range(NPT):
                            for k in range(F1 // P):
                                c = a * F1 + k * P
                                t = pe.transpose(psA[u][:, c:c + P], parts[u][:, a, k * P:k * P + P],
                                                 T.idb[:, :])
                        t.then_inc(a_turned, 1)
                    for u in range(2):
                        s = 2 * i + u
                        e = pe.value_load(T.eid[0:1, bass.ds(s, 1)], min_val=0, max_val=NE - 1)
                        pe.wait_ge(aT_ready, s + 3)
                        pe.wait_ge(y_ready, s + 1)
                        for a in range(NPT):
                            for k in range(F1 // P):
                                c = a * F1 + k * P
                                m = pe.matmul(psY[u][:, 0:D], aT[u][:, c:c + P],
                                              w2f[:, bass.ds(e * (F1 // P * D) + k * D, D)],
                                              start=(a == 0 and k == 0), stop=(a == NPT - 1 and k == F1 // P - 1))
                        m.then_inc(result, 1)
        core.end_phase()


def gate(core, T, L):
    nc = core.nc
    with ExitStack() as st:
        sb = lambda n, s, d=F32: core.sb(f"g{L}_{n}", s, d, st)
        sem = lambda n: core.phase_sem(f"g{L}_{n}")
        R = 4
        xn = [sb(f"xn{u}", [P, D]) for u in range(R)]
        ya = [sb(f"ya{u}", [P, D]) for u in range(R)]
        yb = [sb(f"yb{u}", [P, D]) for u in range(R)]
        va = [sb(f"va{u}", [P, D]) for u in range(R)]
        vb = [sb(f"vb{u}", [P, D]) for u in range(R)]
        hb = [sb(f"hb{u}", [P, 2, D], BF16) for u in range(R)]
        fo = [sb(f"fo{u}", [P, D], BF16 if L else F32) for u in range(R)]
        go = [sb(f"go{u}", [P, D]) for u in range(R)]
        al = sb("al", [P, NT])
        be = sb("be", [P, NT])
        xn_in = [sem(f"xn_in{u}") for u in range(R)]
        y_in = [sem(f"y_in{u}") for u in range(R)]
        g_out = [sem(f"g_out{u}") for u in range(R)]
        alpha_ok = sem("alpha_ok")
        beta_ok = sem("beta_ok")
        step = sem("step")
        mixed = sem("mixed")
        gated = sem("gated")
        xd = T.xn_dram.rearrange("(t p) d -> t p d", p=P)
        gd = T.gate_dram.rearrange("(t p) d -> t p d", p=P)
        NR = NT // R
        with nc.Block() as block:
            @block.sync
            def _(sp):
                for t in range(NT):
                    u = t % R
                    if t >= R:
                        sp.wait_ge(mixed, t - R + 1)
                    sp.dma_start(xn[u][:, :], xd[t]).then_inc(xn_in[u], 16)
                    if t >= R - 1:
                        v = t - R + 1
                        sp.wait_ge(gated, v + 1)
                        sp.dma_start(gd[v], go[v % R][:, :]).then_inc(g_out[v % R], 16)
                for v in range(NT - R + 1, NT):
                    sp.wait_ge(gated, v + 1)
                    sp.dma_start(gd[v], go[v % R][:, :]).then_inc(g_out[v % R], 16)
                for u in range(R):
                    sp.wait_ge(g_out[u], 16 * NR)

            @block.gpsimd
            def _(pool):
                for t in range(NT):
                    u = t % R
                    if t >= R:
                        pool.wait_ge(mixed, t - R + 1)
                    for c in range(L + 1):
                        v = c * NT + t
                        pool.indirect_dma_start(
                            out=(yb if c else ya)[u][:, :], out_offset=None, in_=T.result_dram[L],
                            in_offset=bass.IndirectOffsetOnAxis(ap=T.pos[:, v:v + 1], axis=0))\
                            .then_inc(y_in[u], 16)

            @block.vector
            def _(dve):
                done = [0]

                def then(ins):
                    done[0] += 1
                    ins.then_inc(step, 1)
                    dve.wait_ge(step, done[0])

                if L == 0:
                    dve.wait_ge(alpha_ok, 1)
                    dve.tensor_scalar(be[:, :], al[:, :], -1.0, 1.0, ALU.mult, ALU.add).then_inc(beta_ok, 1)
                    dve.wait_ge(beta_ok, 1)
                for t in range(NT):
                    u = t % R
                    k = t // R + 1
                    dve.wait_ge(xn_in[u], 16 * k)
                    dve.wait_ge(y_in[u], 16 * (L + 1) * k)
                    if t >= R:
                        dve.wait_ge(gated, t - R + 1)
                    if L == 0:
                        then(dve.tensor_tensor(va[u][:, :], xn[u][:, :], ya[u][:, :], ALU.add))
                        then(dve.tensor_scalar(vb[u][:, :], xn[u][:, :], be[:, t:t + 1], None, ALU.mult))
                        dve.scalar_tensor_tensor(fo[u][:, :], va[u][:, :], al[:, t:t + 1], vb[u][:, :],
                                                 ALU.mult, ALU.add).then_inc(mixed, 1)
                    else:
                        then(dve.tensor_scalar(va[u][:, :], yb[u][:, :], T.top[:, 1, t:t + 1], None, ALU.mult))
                        dve.tensor_copy(hb[u][:, 1, :], xn[u][:, :])
                        then(dve.scalar_tensor_tensor(hb[u][:, 0, :], ya[u][:, :], T.top[:, 0, t:t + 1],
                                                      va[u][:, :], ALU.mult, ALU.add))
                        dve.tensor_tensor(fo[u][:, :], hb[u][:, 0, :], hb[u][:, 1, :], ALU.add)\
                            .then_inc(mixed, 1)

            @block.scalar
            def _(act):
                if L == 0:
                    act.activation(al[:, :], T.top[:, 0, :], ACT.Sigmoid).then_inc(alpha_ok, 1)
                for t in range(NT):
                    u = t % R
                    act.wait_ge(mixed, t + 1)
                    if t >= R:
                        act.wait_ge(g_out[u], 16 * (t // R))
                    act.activation(go[u][:, :], fo[u][:, :], ACT.Silu).then_inc(gated, 1)
        core.end_phase()


def combine(core, T, L, O, x_dram, w_dram, out_dram):
    nc = core.nc
    with ExitStack() as st:
        sb = lambda n, s, d=F32: core.sb(f"c{L}_{n}", s, d, st)
        ps = lambda n, c, d=F32: core.ps(f"c{L}_{n}", c, d, st)
        sem = lambda n: core.phase_sem(f"c{L}_{n}")
        w = sb("w", [P, KD, D])
        bias = sb("bias", [P, D])
        x = [sb(f"x{u}", [P, D]) for u in range(2)]
        g = [sb(f"g{u}", [P, D]) for u in range(2)]
        os_ = [sb(f"os{u}", [P, D]) for u in range(2)]
        oT = [sb(f"oT{u}", [P, D]) for u in range(2)]
        s0 = [sb(f"s0{u}", [P, D]) for u in range(2)]
        s1 = [sb(f"s1{u}", [P, D]) for u in range(2)]
        r = [sb(f"r{u}", [P, D]) for u in range(2)]
        psT = [ps(f"psT{u}", 512) for u in range(2)]
        psS = [ps(f"psS{u}", 512) for u in range(2)]
        passed = sem("passed")
        w_in = sem("w_in")
        xg_in = [sem(f"xg_in{u}") for u in range(2)]
        staged = sem("staged")
        turned = sem("turned")
        oT_ready = sem("oT_ready")
        product = sem("product")
        biased = sem("biased")
        gated = sem("gated")
        added = sem("added")
        out = [sem(f"out{u}") for u in range(2)]
        xd = x_dram.rearrange("(t p) d -> t p d", p=P)
        gd = T.gate_dram.rearrange("(t p) d -> t p d", p=P)
        od = out_dram.rearrange("(t p) d -> t p d", p=P)
        tile = lambda ap, n: ap[bass.ds(n, 1)].rearrange("t p d -> (t p) d")
        with nc.Block() as block:
            @block.sync
            def _(sp):
                sp.dma_start(w[:, :, :], w_dram.rearrange("(k p) n -> p k n", p=P)).then_inc(w_in, 16)
                if L:
                    sp.dma_start(bias[:, :], T.bproj_dram.partition_broadcast(P)).then_inc(w_in, 16)
                sp.sem_inc(out[0], 16)
                sp.sem_inc(out[1], 16)
                with sp.Fori(0, NT // 2) as i:
                    for u in range(2):
                        n = 2 * i + u
                        sp.wait_ge(added, n + 1)
                        sp.dma_start(x[u][:, :], tile(xd, n)).then_inc(xg_in[u], 16)
                        sp.dma_start(g[u][:, :], tile(gd, n)).then_inc(xg_in[u], 16)
                for u in range(2):
                    sp.wait_ge(out[u], 16 * (NT // 2 + 1))

            @block.gpsimd
            def _(pool):
                for b in range(NB):
                    with pool.Fori(0, TS // 2) as i:
                        for u in range(2):
                            n = b * TS + 2 * i + u
                            pool.wait_ge(turned, n + 1)
                            pool.sem_inc(passed, 1)
                            src = O[:, b * NG:(b + 1) * NG, :, :].rearrange("p g t c -> p g (t c)")[
                                :, :, bass.ds((2 * i + u) * GW, GW)]
                            pool.tensor_copy(os_[u][:, :].rearrange("p (g c) -> p g c", g=NG), src)\
                                .then_inc(staged, 1)

            @block.tensor
            def _(pe):
                pe.sem_inc(turned, 2)
                pe.sem_inc(product, 2)
                pe.wait_ge(w_in, 32 if L else 16)
                with pe.Fori(0, NT // 2) as i:
                    for u in range(2):
                        n = 2 * i + u
                        pe.wait_ge(staged, n + 1)
                        pe.wait_ge(oT_ready, n + 1)
                        for k in range(KD):
                            t = pe.transpose(psT[u][:, k * P:k * P + P], os_[u][:, k * P:k * P + P], T.idf)
                        t.then_inc(turned, 1)
                    for u in range(2):
                        n = 2 * i + u
                        pe.wait_ge(oT_ready, n + 3)
                        pe.wait_ge(biased, n + 1)
                        for k in range(KD):
                            m = pe.matmul(psS[u][:, 0:D], oT[u][:, k * P:k * P + P], w[:, k, :],
                                          start=(k == 0), stop=(k == KD - 1))
                        m.then_inc(product, 1)

            @block.vector
            def _(dve):
                dve.sem_inc(biased, 2)
                dve.sem_inc(added, 2)
                if L:
                    dve.wait_ge(w_in, 32)
                with dve.Fori(0, NT // 2) as i:
                    for u in range(2):
                        n = 2 * i + u
                        dve.wait_ge(product, n + 3)
                        dve.wait_ge(xg_in[u], 32 * i + 32)
                        if L:
                            dve.tensor_tensor(s0[u][:, :], psS[u][:, 0:D], bias[:, :], ALU.add)\
                                .then_inc(biased, 1)
                            dve.wait_ge(biased, n + 3)
                            dve.tensor_tensor(s1[u][:, :], s0[u][:, :], g[u][:, :], ALU.mult)\
                                .then_inc(gated, 1)
                            dve.wait_ge(gated, n + 1)
                        else:
                            dve.tensor_tensor(s1[u][:, :], psS[u][:, 0:D], g[u][:, :], ALU.mult)\
                                .then_inc(biased, 1)
                            dve.wait_ge(biased, n + 3)
                        dve.wait_ge(out[u], 16 * i + 16)
                        dve.tensor_tensor(r[u][:, :], s1[u][:, :], x[u][:, :], ALU.add).then_inc(added, 1)

            @block.scalar
            def _(act):
                act.sem_inc(oT_ready, 2)
                with act.Fori(0, NT // 2) as i:
                    for u in range(2):
                        n = 2 * i + u
                        act.wait_ge(turned, n + 3)
                        act.wait_ge(product, n + 1)
                        act.copy(oT[u][:, :], psT[u][:, 0:D]).then_inc(oT_ready, 1)
                    for u in range(2):
                        n = 2 * i + u
                        act.wait_ge(added, n + 3)
                        act.dma_start(tile(od, n), r[u][:, :]).then_inc(out[u], 16)
        core.end_phase()


def attention_plan(first, last):
    def max_steps(nxt, c):
        out = []
        for i4 in range(CT):
            for h in range(HG):
                out.append(("max", nxt, c, i4, h, 0))
                if CT * c + i4 >= 8:
                    out.append(("max", nxt, c, i4, h, 1))
        return out

    turn = [("turn", 1, b % 2, b // 2 % HG, b // (2 * HG)) for b in range(4 * HG)]
    if first:
        return turn + max_steps(1, 0) + [("lift", 1, 0, 0), ("lift", 1, 0, 1)]
    plan = []
    for c in range(NC):
        steps = CT * (c + 1)
        slots = [[] for _ in range(HG * steps)]
        if c < NC - 1:
            work = max_steps(0, c + 1)
            span = range(0, HG * (steps - 1))
        else:
            work = [] if last else turn
            span = range(0, HG * 8)
        for n, w in enumerate(work):
            slots[span[n * len(span) // len(work)]].append(w)
        if c == NC - 1 and not last:
            span = range(HG * 9, HG * (steps - 1))
            work = max_steps(1, 0)
            for n, w in enumerate(work):
                slots[span[n * len(span) // len(work)]].append(w)
        for j in range(steps):
            for h in range(HG):
                plan.append(("score", 0, c, j, h))
                plan += slots[HG * j + h]
            if j:
                if j == 1 and c:
                    plan.append(("finish", 0, c - 1))
                plan.append(("value", 0, c, j - 1))
            elif c:
                plan.append(("value", 0, c - 1, CT * c - 1))
                plan.append(("take", 0, c - 1))
        if c < NC - 1:
            plan += [("lift", 0, c + 1, 0), ("lift", 0, c + 1, 1)]
    if not last:
        plan += [("lift", 1, 0, 0), ("lift", 1, 0, 1)]
    plan += [("value", 0, NC - 1, CT * NC - 1), ("take", 0, NC - 1), ("finish", 0, NC - 1)]
    return plan


def numbered(plan):
    seen, bank, out = {}, 0, []
    for s in plan:
        k = seen.get(s[0], 0)
        seen[s[0]] = k + 1
        out.append((s, k, bank))
        bank += s[0] in ("turn", "lift", "finish")
    return out, seen, bank


def attention(core, T, L, O):
    nc = core.nc
    first, first_n, first_bank = numbered(attention_plan(True, False))
    body, body_n, body_bank = numbered(attention_plan(False, False))
    tail, _, _ = numbered(attention_plan(False, True))
    with ExitStack() as st:
        sb = lambda n, s, d=F32: core.sb(f"s{L}_{n}", s, d, st)
        ps = lambda n, c, d=F32: core.ps(f"s{L}_{n}", c, d, st)
        sem = lambda n: core.phase_sem(f"s{L}_{n}")
        raw = [sb(f"raw{u}", [P, TS, 3 * GW]) for u in range(2)]
        rest = sb("rest", [P, TS, GW])
        qst = sb("qst", [P, TS, HG, NPART, DH], BF16)
        kst = sb("kst", [P, TS, HG, KR + MR], BF16)
        va = [sb(f"va{u}", [P, TS, HG, 32]) for u in range(2)]
        qT = [sb(f"qT{u}", [P, HG, S], BF16) for u in range(2)]
        kT = [sb(f"kT{u}", [P, HG, S], BF16) for u in range(2)]
        NPB = 8
        pr = [sb(f"pr{i}", [P, CH]) for i in range(NPB)]
        half = sb("half", [P, CT, HG, 2])
        nm = sb("nm", [P, CT, HG])
        nmp = sb("nmp", [P, CT, HG, MR], BF16)
        osb = sb("osb", [P, CH])
        rcp = sb("rcp", [P, CT, HG])
        psM = [ps(f"psM{i}", 1024) for i in range(2)]
        psS = [ps(f"psS{i}", CH) for i in range(2)]
        psV = ps("psV", CH)
        psX = ps("psX", 512)
        psXb = psX[:, :].bitcast(BF16)
        loaded = [sem(f"loaded{u}") for u in range(2)]
        pad_ok = sem("pad_ok")
        passed = sem("passed")
        split = sem("split")
        staged = sem("staged")
        stacks_used = sem("stacks_used")
        bank_full = sem("bank_full")
        bank_free = sem("bank_free")
        rowscores = sem("rowscores")
        reduced = sem("reduced")
        half_ok = sem("half_ok")
        max_split = sem("max_split")
        scored = sem("scored")
        exped = sem("exped")
        valued = sem("valued")
        taken = sem("taken")
        rcp_ok = sem("rcp_ok")
        O2 = O[:, :, :, :].rearrange("p n t c -> p (n t c)")
        qd = T.qkv.rearrange("n p t c -> n p (t c)")

        def segments(eng, emit):
            emit(first, None, -1)
            with eng.Fori(0, NU // 2 - 1) as i:
                emit(body, 2 * i, 0)
                emit(body, 2 * i + 1, 1)
            emit(body, NU - 2, 0)
            emit(tail, NU - 1, 1)

        def at(kind, n):
            return 0 if n is None else first_n.get(kind, 0) + body_n[kind] * n

        def bank_at(n):
            return 0 if n is None else first_bank + body_bank * n

        def va_free(i, u):
            return 2 if isinstance(i, int) and i == 0 else body_n["value"] * (2 * (i - 1) + u + 1) + 2

        def maxima_before(plan, k):
            lifts = [i for i, s in enumerate(plan) if s[0][0] == "lift"]
            return sum(s[0][0] == "max" for s in plan[:lifts[k]])

        def first_col(c, j):
            return max(0, j - CT * c) * P

        with nc.Block() as block:
            @block.sync
            def _(sp):
                for m in range(2):
                    sp.wait_ge(staged, m + 1)
                    sp.dma_start(raw[m][:, :, :].rearrange("p t c -> p (t c)"), qd[m]).then_inc(loaded[m], 16)
                with sp.Fori(1, NU // 2) as i:
                    for u in range(2):
                        m = 2 * i + u
                        sp.wait_ge(staged, m + 1)
                        sp.dma_start(raw[u][:, :, :].rearrange("p t c -> p (t c)"),
                                     qd[bass.ds(m, 1)].rearrange("n p c -> (n p) c")).then_inc(loaded[u], 16)

            @block.gpsimd
            def _(pool):
                pool.sem_inc(staged, 2)
                for u in range(2):
                    pool.memset(va[u][:, :, :, DH:32], 0.0).then_inc(pad_ok, 1)
                pool.memset(kst[:, :, :, KR:KR + MR], 1.0).then_inc(pad_ok, 1)
                pool.wait_ge(pad_ok, 3)
                for u in range(2):
                    pool.memset(va[u][:, :, :, DH:DH + 1], 1.0).then_inc(pad_ok, 1)
                pool.wait_ge(pad_ok, 5)
                def stage(i):
                    for u in range(2):
                        m = 2 * i + u
                        pool.wait_ge(loaded[u], 16 * i + 16)
                        pool.wait_ge(stacks_used, m + 1)
                        pool.sem_inc(passed, 1)
                        q = raw[u][:, :, 0:GW].rearrange("p t (h d) -> p t h d", h=HG)
                        k = raw[u][:, :, GW:2 * GW].rearrange("p t (h d) -> p t h d", h=HG)
                        r = rest[:, :, :].rearrange("p t (h d) -> p t h d", h=HG)
                        Q = lambda s: qst[:, :, :, s, :]
                        K = lambda s: kst[:, :, :, s * DH:(s + 1) * DH]
                        done = [0]

                        def then(ins):
                            done[0] += 1
                            ins.then_inc(split, 1)
                            pool.wait_ge(split, 8 * m + done[0])
                            pool.sem_inc(passed, 1)

                        then(pool.tensor_copy(Q(0), q))
                        pool.tensor_copy(Q(1), Q(0))
                        pool.tensor_copy(Q(3), Q(0))
                        then(pool.tensor_tensor(r, q, Q(0), ALU.subtract))
                        then(pool.tensor_copy(Q(2), r))
                        pool.tensor_copy(Q(4), Q(2))
                        then(pool.tensor_tensor(Q(5), r, Q(2), ALU.subtract))
                        then(pool.tensor_copy(K(0), k))
                        pool.tensor_copy(K(2), K(0))
                        pool.tensor_copy(K(5), K(0))
                        then(pool.tensor_tensor(r, k, K(0), ALU.subtract))
                        then(pool.tensor_copy(K(1), r))
                        pool.tensor_copy(K(4), K(1))
                        then(pool.tensor_tensor(K(3), r, K(1), ALU.subtract))
                        pool.wait_ge(valued, va_free(i, u))
                        pool.sem_inc(passed, 1)
                        pool.tensor_copy(va[u][:, :, :, 0:DH],
                                         raw[u][:, :, 2 * GW:3 * GW].rearrange("p t (h d) -> p t h d", h=HG))\
                            .then_inc(staged, 1)
                stage(0)
                with pool.Fori(1, NU // 2) as i:
                    stage(i)

            @block.tensor
            def _(pe):
                pe.sem_inc(stacks_used, 1)
                pe.sem_inc(valued, 2)

                def emit(plan, n, u):
                    for step, k, bank in plan:
                        kind, nxt = step[0], step[1]
                        par = (u + nxt) % 2
                        m = 0 if n is None else n + nxt
                        if kind == "turn":
                            _, _, isk, h, lo = step
                            if k == 0:
                                pe.wait_ge(staged, m + 3)
                            pe.wait_ge(bank_free, bank_at(n) + bank + 1)
                            rows = KR + MR if isk else KR
                            for t in range(8):
                                src = kst[:, 8 * lo + t, h, :] if isk else \
                                    qst[:, 8 * lo + t, h, :, :].rearrange("p s d -> p (s d)")
                                x = pe.transpose(psXb[0:rows, t * P:t * P + P], src, T.idb[:, :])
                            x.then_inc(bank_full, 1)
                            if k == 4 * HG - 1:
                                pe.wait_ge(bank_full, bank_at(n) + bank + 1)
                                pe.sem_inc(stacks_used, 1)
                        elif kind == "max":
                            _, _, c, i4, h, hf = step
                            if nxt and (c, i4, h) == (0, 0, 0):
                                pe.wait_ge(bank_free, bank_at(n) + bank + 1)
                            pe.wait_ge(reduced, at("max", n) + k + 1)
                            i = CT * c + i4
                            end = P * (i + 1)
                            k0, k1 = 1024 * hf, min(1024 * hf + 1024, end)
                            dst = psM[k % 2]
                            for a in range(k0, k1, 512):
                                z = min(a + 512, k1)
                                x = pe.matmul(dst[:, a - k0:z - k0], qT[par][0:KR, h, i * P:i * P + P],
                                              kT[par][0:KR, h, a:z], start=True, stop=(z < end))
                            if k1 == end:
                                x = pe.matmul(dst[:, end - P - k0:end - k0], T.idb[:, :], T.mqb[:, :],
                                              start=False, stop=True)
                            x.then_inc(rowscores, 1)
                        elif kind == "lift":
                            _, _, c, pair = step
                            if pair == 0:
                                pe.wait_ge(max_split, at("lift", n) // 2 + k // 2 + 1)
                            pe.wait_ge(bank_free, bank_at(n) + bank + 1)
                            for hh in range(2):
                                for i4 in range(CT):
                                    x = pe.transpose(psXb[KR:KR + MR, hh * CH + i4 * P:hh * CH + i4 * P + P],
                                                     nmp[:, i4, 2 * pair + hh, :], T.idb[:, :])
                            x.then_inc(bank_full, 1)
                        elif kind == "score":
                            _, _, c, j, h = step
                            if j == 0 and h == 0:
                                pe.wait_ge(bank_free, bank_at(n) + bank + 1)
                            pe.wait_ge(exped, at("score", n) + k + 1)
                            a = first_col(c, j)
                            diag = j >= CT * c
                            x = pe.matmul(psS[k % 2][:, a:CH], kT[par][0:KR + MR, h, j * P:j * P + P],
                                          qT[par][0:KR + MR, h, c * CH + a:c * CH + CH],
                                          start=True, stop=not diag)
                            if diag:
                                x = pe.matmul(psS[k % 2][:, a:a + P], T.idb[:, :], T.mkb[:, :],
                                              start=False, stop=True)
                            x.then_inc(scored, 1)
                        elif kind == "value":
                            _, _, c, j = step
                            pe.wait_ge(exped, at("score", n) + 4 * k + 4 + 2)
                            if j == 0:
                                pe.wait_ge(taken, at("take", n) + c + 1)
                            a = first_col(c, j)
                            for h in range(HG):
                                x = pe.matmul(psV[32 * h:32 * h + 32, a:CH], va[par][:, j, h, :],
                                              pr[(4 * k + h) % NPB][:, a:CH],
                                              start=(j == 0), stop=(j == CT * c + CT - 1))
                            x.then_inc(valued, 1)
                        elif kind == "finish":
                            _, _, c = step
                            pe.wait_ge(taken, at("take", n) + c + 2)
                            pe.wait_ge(bank_free, bank_at(n) + bank + 1)
                            for i4 in range(CT):
                                x = pe.transpose(psX[:, i4 * P:i4 * P + P], osb[:, i4 * P:i4 * P + P], T.idf)
                            x.then_inc(bank_full, 1)

                segments(pe, emit)

            @block.scalar
            def _(act):
                act.sem_inc(exped, 2)

                def emit(plan, n, u):
                    for step, k, bank in plan:
                        kind, nxt = step[0], step[1]
                        par = (u + nxt) % 2
                        if kind == "turn":
                            _, _, isk, h, lo = step
                            act.wait_ge(bank_full, bank_at(n) + bank + 1)
                            rows = KR + MR if isk else KR
                            dst = kT[par] if isk else qT[par]
                            act.copy(dst[0:rows, h, lo * 1024:lo * 1024 + 1024], psXb[0:rows, 0:1024])\
                                .then_inc(bank_free, 1)
                        elif kind == "score":
                            _, _, c, j, h = step
                            a = first_col(c, j)
                            act.wait_ge(scored, at("score", n) + k + 1)
                            if h == 0:
                                act.wait_ge(valued, at("value", n) + k // 4 + 1)
                            act.activation(pr[k % NPB][:, a:CH], psS[k % 2][:, a:CH], ACT.Exp,
                                           scale=float(DH) ** -0.5).then_inc(exped, 1)

                segments(act, emit)

            @block.vector
            def _(dve):
                dve.sem_inc(bank_free, 1)
                dve.sem_inc(reduced, 2)
                dve.sem_inc(taken, 1)

                def emit(plan, n, u):
                    for step, k, bank in plan:
                        kind, nxt = step[0], step[1]
                        par = (u + nxt) % 2
                        if kind == "max":
                            _, _, c, i4, h, hf = step
                            dve.wait_ge(rowscores, at("max", n) + k + 1)
                            w = min(1024, P * (CT * c + i4 + 1) - 1024 * hf)
                            dve.tensor_reduce(half[:, i4, h, hf:hf + 1], psM[k % 2][:, 0:w], AX.X, ALU.max,
                                              negate=True).then_inc(reduced, 1)
                        elif kind == "lift":
                            _, _, c, pair = step
                            if pair == 0:
                                g = at("lift", n) // 2 + k // 2
                                dve.wait_ge(reduced, at("max", n) + maxima_before(plan, k) + 2)
                                if c >= 2:
                                    dve.tensor_tensor(nm[:, :, :], half[:, :, :, 0], half[:, :, :, 1], ALU.min)\
                                        .then_inc(half_ok, 1)
                                else:
                                    dve.tensor_copy(nm[:, :, :], half[:, :, :, 0]).then_inc(half_ok, 1)
                                dve.wait_ge(half_ok, 2 * g + 1)
                                dve.tensor_copy(nmp[:, :, :, 0], nm[:, :, :]).then_inc(half_ok, 1)
                                dve.wait_ge(half_ok, 2 * g + 2)
                                dve.tensor_tensor(nmp[:, :, :, 1], nm[:, :, :], nmp[:, :, :, 0], ALU.subtract)\
                                    .then_inc(max_split, 1)
                            dve.wait_ge(bank_full, bank_at(n) + bank + 1)
                            dve.tensor_copy(qT[par][KR:KR + MR, 2 * pair:2 * pair + 2, c * CH:c * CH + CH],
                                            psXb[KR:KR + MR, :].rearrange("p (h q) -> p h q", h=2))\
                                .then_inc(bank_free, 1)
                        elif kind == "take":
                            _, _, c = step
                            dve.wait_ge(valued, at("value", n) + CT * (c + 1) * (c + 2) // 2 + 2)
                            dve.tensor_copy(osb[:, :], psV[:, :]).then_inc(taken, 1)
                        elif kind == "finish":
                            _, _, c = step
                            dve.wait_ge(bank_full, bank_at(n) + bank + 1)
                            view = psX[:, :].rearrange("p (t h w) -> p t h w", t=CT, h=HG)
                            dve.reciprocal(rcp[:, :, :], view[:, :, :, DH]).then_inc(rcp_ok, 1)
                            dve.wait_ge(rcp_ok, at("finish", n) + k + 1)
                            dst = O2[:, bass.ds(n * (TS * GW) + c * CT * GW, CT * GW)]
                            dve.tensor_tensor(dst.rearrange("p (t h d) -> p t h d", t=CT, h=HG),
                                              view[:, :, :, 0:DH], bc(rcp[:, :, :], 3, DH), ALU.mult)\
                                .then_inc(bank_free, 1)

                segments(dve, emit)
        core.end_phase()


def build(nc, ins, out):
    with ExitStack() as stack:
        core = Core(nc, stack)

        class T:
            pass

        T.cst_dram, T.cos_dram, T.sin_dram = ins["cst"], ins["cos"], ins["sin"]
        T.cent_dram, T.w1_dram, T.w2_dram = ins["cent"], ins["w1"], ins["w2"]
        T.gb0_dram, T.b1_dram, T.b2_dram = ins["gb0"], ins["b1"], ins["b2"]
        T.bqkv_dram, T.bproj_dram = ins["bqkv"], ins["bproj"]
        T.nw_dram, T.gw_dram, T.gb_dram = ins["nw"], ins["gw"], ins["gb"]
        T.m1_dram, T.m2_dram, T.mb1_dram, T.mb2_dram = ins["m1"], ins["m2"], ins["mb1"], ins["mb2"]
        T.qkv = core.dram("qkv", [NU, P, TS, 3 * GW])
        T.xn_dram = core.dram("xn", [NT * P, D])
        T.gate_dram = core.dram("gatev", [NT * P, D])
        x1_dram = core.dram("x1", [NT * P, D])
        T.sorted_dram = [core.dram("sorted0", [(SLOT0 + 1) * P, D]), core.dram("sorted1", [(SLOT1 + 1) * P, D], BF16)]
        T.result_dram = [core.dram("result0", [SLOT0 * P, D]), core.dram("result1", [SLOT1 * P, D])]
        load_constants(core, T)
        T.w1_in = core.sem("w1_in")
        T.w2_in = core.sem("w2_in")
        T.cleared = [core.sem("cleared0"), core.sem("cleared1")]
        T.aff = core.sb("aff", [P, NT, NE])
        T.pos = core.sb("pos", [P, 2 * NT], U32)
        T.eid = core.sb("eid", [P, SLOT1 + 1], I32)
        T.top = core.sb("top", [P, 2, NT])

        with nc.Block() as block:
            @block.scalar
            def _(act):
                act.dma_start(T.sorted_dram[0].rearrange("(s p) d -> p s d", p=P),
                              bc(T.zero[:, :], 1, SLOT0 + 1)).then_inc(T.cleared[0], 16)
                act.dma_start(T.sorted_dram[1].rearrange("(s p) d -> p s d", p=P),
                              bc(T.zero[:, 0:D // 2].bitcast(BF16), 1, SLOT1 + 1)).then_inc(T.cleared[1], 16)

        with ExitStack() as st:
            T.w1 = core.sb("w1", [P, NE, KD, F0], F32, st)
            T.w2 = core.sb("w2", [P, NE, F0 // P, D], F32, st)
            with ExitStack() as sx:
                T.X = core.sb("X0", [P, NT, D], F32, sx)
                norm_project(core, T, 0, ins["x"], ins["wqkv0"], T.X)
                norm_again(core, T.X)
                route(core, T, 0)
            experts0(core, T)
        gate(core, T, 0)
        with ExitStack() as st:
            O = core.sb("O0", [P, NU, TS, GW], F32, st)
            attention(core, T, 0, O)
            combine(core, T, 0, O, ins["x"], ins["wo0"], x1_dram)

        with ExitStack() as st:
            T.X = core.sb("X1", [P, NT, D], F32, st)
            T.nf = core.sb("nf", [P, NT, D], BF16, st)
            norm_project(core, T, 1, x1_dram, ins["wqkv1"], T.X)
            scores_of_layer1(core, T, T.X)
            route(core, T, 1)
        experts1(core, T)
        gate(core, T, 1)
        with ExitStack() as st:
            O = core.sb("O1", [P, NU, TS, GW], F32, st)
            attention(core, T, 1, O)
            combine(core, T, 1, O, x1_dram, ins["wo1"], out)


def kernel(**inputs):
    import numpy as _np
    import concourse.bacc as _bacc
    from concourse import mybir as _mybir
    from concourse.bass_utils import run_bass_kernel_spmd as _run

    a = {k: _np.asarray(v) for k, v in inputs.items()}
    def grouped(q, k, v):
        parts = [_np.reshape(m, m.shape[:-1] + (NG, GW)) for m in (q, k, v)]
        return _np.ascontiguousarray(_np.stack(parts, axis=-2).reshape(q.shape[:-1] + (3 * D,)))

    wq1 = a["L1_attn_Wqkv"]
    bq1 = a["L1_attn_bqkv"]
    m1 = a["L1_ffn_mlp1_weight"]
    mb1 = a["L1_ffn_mlp1_bias"]
    cos, sin = rotary_tables()
    col = lambda t: t.reshape(NE, KD, P).transpose(2, 0, 1)
    arrays = {
        "x": a["L0_attn_x"].reshape(NT * P, D),
        "wqkv0": grouped(a["L0_attn_W_Q"], a["L0_attn_W_K"], a["L0_attn_W_V"]),
        "wo0": a["L0_attn_W_o"],
        "cent": a["L0_ffn_centroids"].T,
        "w1": a["L0_ffn_w1"].transpose(0, 2, 1),
        "w2": a["L0_ffn_w2"].transpose(0, 2, 1),
        "b1": a["L0_ffn_b1"].reshape(-1),
        "b2": a["L0_ffn_b2"].reshape(-1),
        "gb0": _np.stack([col(a["L0_ffn_ln_g"]), col(a["L0_ffn_ln_b"])], axis=2).reshape(P, -1),
        "wqkv1": grouped(wq1[:, 0:D], wq1[:, D:2 * D], wq1[:, 2 * D:]),
        "bqkv": grouped(bq1[0:D], bq1[D:2 * D], bq1[2 * D:]),
        "wo1": a["L1_attn_Wproj"],
        "bproj": a["L1_attn_bproj"],
        "nw": a["L1_ffn_norm_weight"],
        "gw": a["L1_ffn_gate_weight"].T,
        "gb": a["L1_ffn_gate_bias"],
        "m1": _np.concatenate([m1[:, 0::2], m1[:, 1::2]], axis=1).transpose(0, 2, 1),
        "mb1": _np.concatenate([mb1[:, 0::2], mb1[:, 1::2]], axis=1).reshape(-1),
        "m2": a["L1_ffn_mlp2_weight"].transpose(0, 2, 1),
        "mb2": a["L1_ffn_mlp2_bias"].reshape(-1),
        "cst": constant_table(), "cos": cos, "sin": sin,
    }
    nc = _bacc.Bacc("TRN2", target_bir_lowering=False, num_devices=1)
    feed, ins = {}, {}
    for name, v in arrays.items():
        v = _np.ascontiguousarray(v)
        feed["in_" + name] = v
        ins[name] = nc.dram_tensor("in_" + name, v.shape, _mybir.dt.from_np(v.dtype), kind="ExternalInput").ap()
    out = nc.dram_tensor("out", (NT * P, D), _mybir.dt.from_np(_np.dtype("float32")), kind="ExternalOutput").ap()
    build(nc, ins, out)
    r = _run(nc, [feed], core_ids=[0])
    return r.results[0]["out"].reshape(NB, S, D)
```

```python
from contextlib import ExitStack

import numpy as np

import concourse.bass as bass
from concourse import mybir

F32 = mybir.dt.float32
BF16 = mybir.dt.bfloat16
I32 = mybir.dt.int32
U32 = mybir.dt.uint32
ALU = mybir.AluOpType
ACT = mybir.ActivationFunctionType
AX = mybir.AxisListType

P = 128
D = 256
KD = D // P
H = 16
DH = D // H
HG = 4
NG = H // HG
GW = HG * DH
S = 2048
NB = 2
TS = S // P
NT = NB * TS
NU = NB * NG
NE = 8
F0 = 1024
F1 = 256
EPS = 1e-5
SLOT0 = 40
SLOT1 = 72
CH = 512
CT = CH // P
NC = S // CH
NPART = 6
KR = NPART * DH
MR = 2
BIG = -1.0e30

C_ID, C_UP, C_MQ, C_MK, C_ONE, C_K128, C_SLOT, C_PICK = 0, 128, 256, 384, 512, 640, 704, 784
C_COLS = 792


def constant_table():
    t = np.zeros((P, C_COLS), np.float32)
    r = np.arange(P)
    t[:, C_ID:C_ID + P] = np.eye(P)
    t[:, C_UP:C_UP + P] = r[:, None] < r[None, :]
    t[:, C_MQ:C_MQ + P] = np.where(r[None, :] > r[:, None], BIG, 0)
    t[:, C_MK:C_MK + P] = np.where(r[:, None] > r[None, :], BIG, 0)
    t[:, C_ONE:C_ONE + P] = 1
    t[:, C_K128:C_K128 + 64] = 128 * np.arange(64)
    t[:, C_SLOT:C_SLOT + 80] = np.arange(80)
    t[:, C_PICK:C_PICK + NE] = NE - np.arange(NE)
    return t


def rotary_tables():
    inv = np.float32(1.0) / np.float32(10000.0) ** (np.arange(0, DH, 2, dtype=np.float32) / np.float32(DH))
    f = np.arange(S, dtype=np.float32)[:, None] * inv[None, :].astype(np.float32)
    lay = lambda a: np.ascontiguousarray(a.reshape(TS, P, DH // 2).transpose(1, 0, 2).reshape(P, -1))
    return lay(np.cos(f).astype(np.float32)), lay(np.sin(f).astype(np.float32))


class Core:

    def __init__(self, nc, stack):
        self.nc, self.stack, self.held = nc, stack, []

    def sb(self, name, shape, dt=F32, stack=None):
        return (stack or self.stack).enter_context(self.nc.sbuf_tensor(name, shape, dt))

    def ps(self, name, cols, dt=F32, stack=None):
        return (stack or self.stack).enter_context(self.nc.psum_tensor(name, [P, cols], dt))

    def sem(self, name):
        return self.stack.enter_context(self.nc.semaphore(name))

    def phase_sem(self, name):
        self.held.append(self.nc.alloc_semaphore(name))
        return self.held[-1]

    def end_phase(self):
        self.nc.clear_and_free_semaphores(self.held)
        self.held = []
        self.nc.all_engine_barrier()

    def dram(self, name, shape, dt=F32):
        return self.nc.dram_tensor(name, shape, dt).ap()


def bc(ap, axis, n):
    ap = ap.unsqueeze(axis)
    shape = list(ap.shape)
    shape[axis] = n
    return ap.to_broadcast(shape)


def load_constants(core, T):
    nc = core.nc
    T.cst = core.sb("cst", [P, C_COLS])
    T.idb = core.sb("idb", [P, P], BF16)
    T.mqb = core.sb("mqb", [P, P], BF16)
    T.mkb = core.sb("mkb", [P, P], BF16)
    T.zero = core.sb("zero", [P, D])
    T.idf = T.cst[:, C_ID:C_ID + P]
    cst_in = core.sem("cst_in")
    zero_done = core.sem("zero_done")
    with nc.Block() as block:
        @block.sync
        def _(sp):
            sp.dma_start(T.cst[:, :], T.cst_dram).then_inc(cst_in, 16)

        @block.gpsimd
        def _(pool):
            pool.memset(T.zero[:, :], 0.0).then_inc(zero_done, 1)

        @block.vector
        def _(dve):
            dve.wait_ge(cst_in, 16)
            dve.tensor_copy(T.idb[:, :], T.idf)
            dve.tensor_copy(T.mqb[:, :], T.cst[:, C_MQ:C_MQ + P])
            dve.tensor_copy(T.mkb[:, :], T.cst[:, C_MK:C_MK + P])


def row_stats(core, dve, X2, bs, mean, dif, var, stat, merged):
    with dve.Fori(0, NT) as t:
        dve.bn_stats(bs[:, :, :].rearrange("p t s -> p (t s)")[:, bass.ds(t * 6, 6)],
                     X2[:, bass.ds(t * D, D)]).then_inc(stat, 1)
    dve.wait_ge(stat, NT)
    dve.tensor_tensor(mean[:, :], bs[:, :, 1], bs[:, :, 4], ALU.add).then_inc(merged, 1)
    dve.tensor_tensor(dif[:, :], bs[:, :, 1], bs[:, :, 4], ALU.subtract).then_inc(merged, 1)
    dve.tensor_tensor(var[:, :], bs[:, :, 2], bs[:, :, 5], ALU.add).then_inc(merged, 1)
    dve.wait_ge(merged, 3)
    dve.tensor_scalar(mean[:, :], mean[:, :], 0.5, None, ALU.mult).then_inc(merged, 1)
    dve.tensor_tensor(dif[:, :], dif[:, :], dif[:, :], ALU.mult).then_inc(merged, 1)
    dve.tensor_scalar(var[:, :], var[:, :], 1.0 / D, EPS, ALU.mult, ALU.add).then_inc(merged, 1)
    dve.wait_ge(merged, 6)
    return dve.scalar_tensor_tensor(var[:, :], dif[:, :], 0.25, var[:, :], ALU.mult, ALU.add)


def norm_project(core, T, L, x_dram, w_dram, X):
    nc = core.nc
    W3 = 3 * D
    with ExitStack() as st:
        sb = lambda n, s, d=F32: core.sb(f"a{L}_{n}", s, d, st)
        ps = lambda n, c, d=F32: core.ps(f"a{L}_{n}", c, d, st)
        sem = lambda n: core.phase_sem(f"a{L}_{n}")
        w = sb("w", [P, KD, W3])
        cent = sb("cent", [P, KD, NE])
        bs = sb("bs", [P, NT, 6])
        mean = sb("mean", [P, NT])
        dif = sb("dif", [P, NT])
        var = sb("var", [P, NT])
        std = sb("std", [P, NT])
        rstd = sb("rstd", [P, NT])
        xs = [sb(f"xs{u}", [P, D]) for u in range(2)]
        xT = [sb(f"xT{u}", [P, D]) for u in range(2)]
        qs = [sb(f"qs{u}", [P, W3]) for u in range(2)]
        psT = [ps(f"psT{u}", 512) for u in range(2)]
        psQ = [ps(f"psQ{u}", 1024) for u in range(2)]
        x_in = [sem(f"x_in{q}") for q in range(4)]
        w_in = sem("w_in")
        stat = sem("stat")
        merged = sem("merged")
        var_ok = sem("var_ok")
        std_ok = sem("std_ok")
        rstd_ok = sem("rstd_ok")
        xn_ready = sem("xn_ready")
        xn_kept = sem("xn_kept")
        transposed = sem("transposed")
        xT_ready = sem("xT_ready")
        projected = sem("projected")
        left_act = sem("left_act")
        left_dve = sem("left_dve")
        out = [sem(f"out{u}") for u in range(2)]
        xn_out = sem("xn_out")
        X2 = X[:, :, :].rearrange("p t d -> p (t d)")
        aff2 = T.aff[:, :, :].rearrange("p t e -> p (t e)")
        xd = x_dram.rearrange("(t p) d -> p t d", p=P)
        if L:
            bias = sb("bias", [P, W3])
            cosT = sb("cos", [P, TS * DH // 2])
            sinT = sb("sin", [P, TS * DH // 2])
            qo = [sb(f"qo{u}", [P, NG, 2 * GW]) for u in range(2)]
            dm = [sb(f"dm{u}", [P, 2, NG * 2 * HG * DH // 2]) for u in range(2)]
            pm = [sb(f"pm{u}", [P, 2, NG * 2 * HG * DH // 2]) for u in range(2)]
            tab_in = sem("tab_in")
            passed = sem("passed")
            biased = sem("biased")
            dve_mul = sem("dve_mul")
            pool_mul = sem("pool_mul")
            turned_even = sem("turned_even")
            turned_odd = sem("turned_odd")
            outq = [sem(f"outq{u}") for u in range(2)]

        with nc.Block() as block:
            @block.sync
            def _(sp):
                for q in range(4):
                    sp.dma_start(X[:, 8 * q:8 * q + 8, :], xd[:, 8 * q:8 * q + 8, :]).then_inc(x_in[q], 16)
                    if q == 0:
                        sp.dma_start(w[:, :, :], w_dram.rearrange("(k p) n -> p k n", p=P)).then_inc(w_in, 16)
                        if L == 0:
                            sp.dma_start(cent[:, :, :],
                                         T.cent_dram.rearrange("(k p) n -> p k n", p=P)).then_inc(w_in, 16)
                        else:
                            sp.dma_start(bias[:, :], T.bqkv_dram.partition_broadcast(P)).then_inc(tab_in, 16)
                            sp.dma_start(cosT[:, :], T.cos_dram).then_inc(tab_in, 16)
                            sp.dma_start(sinT[:, :], T.sin_dram).then_inc(tab_in, 16)
                if L == 0:
                    for e in range(NE):
                        sp.dma_start(T.w1[:, e, :, :], T.w1_dram[e].rearrange("(k p) f -> p k f", p=P))\
                            .then_inc(T.w1_in, 16)
                        sp.dma_start(T.w2[:, e, :, :], T.w2_dram[e].rearrange("(k p) d -> p k d", p=P))\
                            .then_inc(T.w2_in, 16)
                sp.sem_inc(out[0], 16)
                sp.sem_inc(out[1], 16)
                if L:
                    sp.sem_inc(outq[0], 16)
                    sp.sem_inc(outq[1], 16)
                for b in range(NB):
                    with sp.Fori(0, TS // 2) as i:
                        for u in range(2):
                            n = b * TS + 2 * i + u
                            dst = T.qkv[b * NG:b * NG + NG].rearrange("g p t c -> p g t c")[
                                :, :, bass.ds(2 * i + u, 1), :]
                            src = qs[u][:, :].rearrange("p (g t c) -> p g t c", g=NG, t=1)
                            if L == 0:
                                sp.wait_ge(left_act, n + 3)
                                sp.wait_ge(left_dve, n + 3)
                                sp.dma_start(dst, src).then_inc(out[u], 16)
                            else:
                                sp.wait_ge(biased, n + 3)
                                sp.dma_start(dst[:, :, :, 2 * GW:3 * GW],
                                             src[:, :, :, 2 * GW:3 * GW]).then_inc(out[u], 16)
                                sp.wait_ge(turned_even, n + 1)
                                sp.sem_inc(passed, 1)
                                sp.wait_ge(turned_odd, n + 3)
                                sp.sem_inc(passed, 1)
                                sp.dma_start(dst[:, :, :, 0:2 * GW],
                                             qo[u][:, :, :].rearrange("p g (t c) -> p g t c", t=1))\
                                    .then_inc(outq[u], 16)
                sp.wait_ge(xn_kept, NT)
                sp.dma_start(T.xn_dram.rearrange("(t p) d -> p t d", p=P), X[:, :, :]).then_inc(xn_out, 16)
                for u in range(2):
                    sp.wait_ge(out[u], 16 * (NT // 2 + 1))
                    if L:
                        sp.wait_ge(outq[u], 16 * (NT // 2 + 1))
                sp.wait_ge(xn_out, 16)

            @block.vector
            def _(dve):
                dve.sem_inc(biased if L else left_dve, 2)
                for q in range(4):
                    dve.wait_ge(x_in[q], 16)
                row_stats(core, dve, X2, bs, mean, dif, var, stat, merged).then_inc(var_ok, 1)
                dve.wait_ge(std_ok, 1)
                dve.reciprocal(rstd[:, :], std[:, :]).then_inc(rstd_ok, 1)
                dve.wait_ge(rstd_ok, 1)
                if L:
                    dve.wait_ge(tab_in, 48)
                for b in range(NB):
                    with dve.Fori(0, TS // 2) as i:
                        for u in range(2):
                            n = b * TS + 2 * i + u
                            dve.wait_ge(transposed, n + 1)
                            x_t = X2[:, bass.ds(n * D, D)]
                            mu, rs = mean[:, bass.ds(n, 1)], rstd[:, bass.ds(n, 1)]
                            dve.tensor_scalar(xs[u][:, :], x_t, mu, rs, ALU.subtract, ALU.mult)\
                                .then_inc(xn_ready, 1)
                            dve.tensor_scalar(x_t, x_t, mu, rs, ALU.subtract, ALU.mult)\
                                .then_inc(xn_kept, 1)
                        for u in range(2):
                            n = b * TS + 2 * i + u
                            dve.wait_ge(projected, n + 3)
                            dve.wait_ge(out[u], 16 * (b * TS // 2 + i) + 16)
                            if L == 0:
                                dve.tensor_copy(qs[u][:, 512:W3], psQ[u][:, 512:W3])
                                dve.tensor_copy(aff2[:, bass.ds(n * NE, NE)],
                                                psQ[u][:, W3:W3 + NE]).then_inc(left_dve, 1)
                                continue
                            dve.wait_ge(turned_odd, n + 1)
                            dve.tensor_tensor(qs[u][:, :], psQ[u][:, 0:W3], bias[:, :], ALU.add)\
                                .then_inc(biased, 1)
                            dve.wait_ge(biased, n + 3)
                            dve.wait_ge(outq[u], 16 * (b * TS // 2 + i) + 16)
                            qk = qs[u][:, :].rearrange("p (g c) -> p g c", g=NG)[:, :, 0:2 * GW]\
                                .rearrange("p g (h f z) -> p g h f z", f=DH // 2, z=2)
                            o = qo[u][:, :, :].rearrange("p g (h f z) -> p g h f z", f=DH // 2, z=2)
                            tab = lambda t_: t_[:, bass.ds((2 * i + u) * (DH // 2), DH // 2)]
                            m = dm[u][:, :, :].rearrange("p a (g h f) -> p a g h f", g=NG, f=DH // 2)
                            cs = bc(bc(tab(cosT), 1, 2 * HG), 1, NG)
                            sn = bc(bc(tab(sinT), 1, 2 * HG), 1, NG)
                            dve.tensor_tensor(m[:, 0], qk[:, :, :, :, 0], cs, ALU.mult)
                            dve.tensor_tensor(m[:, 1], qk[:, :, :, :, 1], sn, ALU.mult).then_inc(dve_mul, 1)
                            dve.wait_ge(dve_mul, n + 1)
                            dve.tensor_tensor(o[:, :, :, :, 0], m[:, 0], m[:, 1], ALU.subtract)\
                                .then_inc(turned_even, 1)

            if L:
                @block.gpsimd
                def _(pool):
                    pool.sem_inc(turned_odd, 2)
                    pool.wait_ge(tab_in, 48)
                    for b in range(NB):
                        with pool.Fori(0, TS // 2) as i:
                            for u in range(2):
                                n = b * TS + 2 * i + u
                                pool.wait_ge(biased, n + 3)
                                pool.wait_ge(outq[u], 16 * (b * TS // 2 + i) + 16)
                                qk = qs[u][:, :].rearrange("p (g c) -> p g c", g=NG)[:, :, 0:2 * GW]\
                                    .rearrange("p g (h f z) -> p g h f z", f=DH // 2, z=2)
                                o = qo[u][:, :, :].rearrange("p g (h f z) -> p g h f z", f=DH // 2, z=2)
                                tab = lambda t_: t_[:, bass.ds((2 * i + u) * (DH // 2), DH // 2)]
                                m = pm[u][:, :, :].rearrange("p a (g h f) -> p a g h f", g=NG, f=DH // 2)
                                cs = bc(bc(tab(cosT), 1, 2 * HG), 1, NG)
                                sn = bc(bc(tab(sinT), 1, 2 * HG), 1, NG)
                                pool.tensor_tensor(m[:, 0], qk[:, :, :, :, 0], sn, ALU.mult)\
                                    .then_inc(pool_mul, 1)
                                pool.tensor_tensor(m[:, 1], qk[:, :, :, :, 1], cs, ALU.mult)\
                                    .then_inc(pool_mul, 1)
                                pool.wait_ge(pool_mul, 2 * n + 2)
                                pool.tensor_tensor(o[:, :, :, :, 1], m[:, 0], m[:, 1], ALU.add)\
                                    .then_inc(turned_odd, 1)

            @block.scalar
            def _(act):
                act.sem_inc(xT_ready, 2)
                act.sem_inc(left_act, 2)
                act.wait_ge(var_ok, 1)
                act.activation(std[:, :], var[:, :], ACT.Sqrt).then_inc(std_ok, 1)
                with act.Fori(0, NT // 2) as i:
                    for u in range(2):
                        n = 2 * i + u
                        act.wait_ge(transposed, n + 3)
                        act.wait_ge(projected, n + 1)
                        act.copy(xT[u][:, :], psT[u][:, 0:D]).then_inc(xT_ready, 1)
                    if L == 0:
                        for u in range(2):
                            n = 2 * i + u
                            act.wait_ge(projected, n + 3)
                            act.wait_ge(out[u], 16 * i + 16)
                            act.copy(qs[u][:, 0:512], psQ[u][:, 0:512]).then_inc(left_act, 1)

            @block.tensor
            def _(pe):
                pe.sem_inc(transposed, 2)
                pe.sem_inc(projected, 2)
                pe.wait_ge(w_in, 16 if L else 32)
                with pe.Fori(0, NT // 2) as i:
                    for u in range(2):
                        n = 2 * i + u
                        pe.wait_ge(xn_ready, n + 1)
                        pe.wait_ge(xT_ready, n + 1)
                        for k in range(KD):
                            t = pe.transpose(psT[u][:, k * P:k * P + P], xs[u][:, k * P:k * P + P], T.idf)
                        t.then_inc(transposed, 1)
                    for u in range(2):
                        n = 2 * i + u
                        pe.wait_ge(xT_ready, n + 3)
                        if L == 0:
                            pe.wait_ge(left_act, n + 1)
                            pe.wait_ge(left_dve, n + 1)
                        else:
                            pe.wait_ge(biased, n + 1)
                        for a, z in ((0, 512), (512, W3)):
                            for k in range(KD):
                                m = pe.matmul(psQ[u][:, a:z], xT[u][:, k * P:k * P + P], w[:, k, a:z],
                                              start=(k == 0), stop=(k == KD - 1))
                        if L == 0:
                            for k in range(KD):
                                m = pe.matmul(psQ[u][:, W3:W3 + NE], xT[u][:, k * P:k * P + P],
                                              cent[:, k, :], start=(k == 0), stop=(k == KD - 1))
                        m.then_inc(projected, 1)
        core.end_phase()


def norm_again(core, X):
    nc = core.nc
    with ExitStack() as st:
        sb = lambda n, s, d=F32: core.sb(f"n_{n}", s, d, st)
        sem = lambda n: core.phase_sem(f"n_{n}")
        bs = sb("bs", [P, NT, 6])
        mean, dif, var, std, rstd = (sb(n, [P, NT]) for n in ("mean", "dif", "var", "std", "rstd"))
        stat, merged, var_ok, std_ok, rstd_ok = (sem(n) for n in ("stat", "merged", "var_ok", "std_ok", "rstd_ok"))
        X2 = X[:, :, :].rearrange("p t d -> p (t d)")
        with nc.Block() as block:
            @block.vector
            def _(dve):
                row_stats(core, dve, X2, bs, mean, dif, var, stat, merged).then_inc(var_ok, 1)
                dve.wait_ge(std_ok, 1)
                dve.reciprocal(rstd[:, :], std[:, :]).then_inc(rstd_ok, 1)
                dve.wait_ge(rstd_ok, 1)
                with dve.Fori(0, NT) as n:
                    x_t = X2[:, bass.ds(n * D, D)]
                    dve.tensor_scalar(x_t, x_t, mean[:, bass.ds(n, 1)], rstd[:, bass.ds(n, 1)],
                                      ALU.subtract, ALU.mult)

            @block.scalar
            def _(act):
                act.wait_ge(var_ok, 1)
                act.activation(std[:, :], var[:, :], ACT.Sqrt).then_inc(std_ok, 1)
        core.end_phase()


def scores_of_layer1(core, T, X):
    nc = core.nc
    with ExitStack() as st:
        sb = lambda n, s, d=F32: core.sb(f"r_{n}", s, d, st)
        ps = lambda n, c, d=F32: core.ps(f"r_{n}", c, d, st)
        sem = lambda n: core.phase_sem(f"r_{n}")
        nw = sb("nw", [P, D])
        gw = sb("gw", [P, KD, NE], BF16)
        gb = sb("gb", [P, NE], BF16)
        xc = sb("xc", [P, NT, D], BF16)
        sq = [sb(f"sq{u}", [P, D]) for u in range(2)]
        ss = sb("ss", [P, NT])
        ms = sb("ms", [P, NT])
        std = sb("std", [P, NT])
        rstd = sb("rstd", [P, NT])
        nT = [sb(f"nT{u}", [P, D], BF16) for u in range(2)]
        lg = sb("lg", [P, NT, NE], BF16)
        psT = [ps(f"psT{u}", 1024, BF16) for u in range(2)]
        psL = [ps(f"psL{u}", 512) for u in range(2)]
        tab_in = sem("tab_in")
        cast = sem("cast")
        squared = sem("squared")
        mean_ok = sem("mean_ok")
        std_ok = sem("std_ok")
        rstd_ok = sem("rstd_ok")
        normed = sem("normed")
        transposed = sem("transposed")
        copied = sem("copied")
        scored = sem("scored")
        left = sem("left")
        X2 = X[:, :, :].rearrange("p t d -> p (t d)")
        xc2 = xc[:, :, :].rearrange("p t d -> p (t d)")
        nf2 = T.nf[:, :, :].rearrange("p t d -> p (t d)")
        lg2 = lg[:, :, :].rearrange("p t e -> p (t e)")
        with nc.Block() as block:
            @block.sync
            def _(sp):
                sp.dma_start(nw[:, :], T.nw_dram.partition_broadcast(P)).then_inc(tab_in, 16)
                sp.dma_start(gw[:, :, :], T.gw_dram.rearrange("(k p) n -> p k n", p=P)).then_inc(tab_in, 16)
                sp.dma_start(gb[:, :], T.gb_dram.partition_broadcast(P)).then_inc(tab_in, 16)

            @block.vector
            def _(dve):
                dve.sem_inc(left, 2)
                with dve.Fori(0, NT // 8) as i:
                    dve.tensor_copy(xc2[:, bass.ds(i * 8 * D, 8 * D)],
                                    X2[:, bass.ds(i * 8 * D, 8 * D)]).then_inc(cast, 1)
                dve.wait_ge(squared, NT + 2)
                dve.tensor_scalar(ms[:, :], ss[:, :], 1.0 / D, EPS, ALU.mult, ALU.add).then_inc(mean_ok, 1)
                dve.wait_ge(std_ok, 1)
                dve.reciprocal(rstd[:, :], std[:, :]).then_inc(rstd_ok, 1)
                dve.wait_ge(rstd_ok, 1)
                dve.wait_ge(tab_in, 48)
                with dve.Fori(0, NT // 2) as i:
                    for u in range(2):
                        n = 2 * i + u
                        dve.scalar_tensor_tensor(nf2[:, bass.ds(n * D, D)], xc2[:, bass.ds(n * D, D)],
                                                 rstd[:, bass.ds(n, 1)], nw[:, :],
                                                 ALU.mult, ALU.mult).then_inc(normed, 1)
                    for u in range(2):
                        n = 2 * i + u
                        dve.wait_ge(scored, n + 3)
                        dve.tensor_tensor(lg2[:, bass.ds(n * NE, NE)], psL[u][:, 0:NE], gb[:, :],
                                          ALU.add).then_inc(left, 1)
                dve.wait_ge(left, NT + 2)
                dve.tensor_copy(T.aff[:, :, :], lg[:, :, :])

            @block.scalar
            def _(act):
                act.sem_inc(copied, 2)
                act.wait_ge(cast, NT // 8)
                act.sem_inc(squared, 2)
                with act.Fori(0, NT // 2) as i:
                    for u in range(2):
                        n = 2 * i + u
                        act.wait_ge(squared, n + 1)
                        act.activation(sq[u][:, :], xc2[:, bass.ds(n * D, D)], ACT.Square,
                                       accum_out=ss[:, bass.ds(n, 1)]).then_inc(squared, 1)
                act.wait_ge(mean_ok, 1)
                act.activation(std[:, :], ms[:, :], ACT.Sqrt).then_inc(std_ok, 1)
                with act.Fori(0, NT // 2) as i:
                    for u in range(2):
                        n = 2 * i + u
                        act.wait_ge(transposed, n + 1)
                        act.wait_ge(scored, n + 1)
                        act.copy(nT[u][:, :], psT[u][:, 0:D]).then_inc(copied, 1)

            @block.tensor
            def _(pe):
                pe.sem_inc(scored, 2)
                pe.wait_ge(tab_in, 48)
                with pe.Fori(0, NT // 2) as i:
                    for u in range(2):
                        n = 2 * i + u
                        pe.wait_ge(normed, n + 1)
                        pe.wait_ge(copied, n + 1)
                        for k in range(KD):
                            t = pe.transpose(psT[u][:, k * P:k * P + P], nf2[:, bass.ds(n * D + k * P, P)],
                                             T.idb[:, :])
                        t.then_inc(transposed, 1)
                    for u in range(2):
                        n = 2 * i + u
                        pe.wait_ge(copied, n + 3)
                        pe.wait_ge(left, n + 1)
                        for k in range(KD):
                            m = pe.matmul(psL[u][:, 0:NE], nT[u][:, k * P:k * P + P], gw[:, k, :],
                                          start=(k == 0), stop=(k == KD - 1))
                        m.then_inc(scored, 1)
        core.end_phase()


def route(core, T, L):
    nc = core.nc
    NCH = L + 1
    NV = NCH * NT
    NS = (SLOT1 if L else SLOT0) + 2
    with ExitStack() as st:
        sb = lambda n, s, d=F32: core.sb(f"t{L}_{n}", s, d, st)
        ps = lambda n, c, d=F32: core.ps(f"t{L}_{n}", c, d, st)
        sem = lambda n: core.phase_sem(f"t{L}_{n}")
        aff = sb("aff", [P, NT, NE])
        mx = sb("mx", [P, NCH, NT])
        eq = sb("eq", [P, NT, NE])
        pk = sb("pk", [P, NT])
        oh = sb("oh", [P, NV, NE])
        tot = sb("tot", [P, NV, NE])
        run = [sb(f"run{i}", [P, NV, NE]) for i in range(2)]
        over = sb("over", [P, NE, NV])
        nt_e = sb("nt_e", [P, NE])
        cum = [sb(f"cum{i}", [P, NE]) for i in range(2)]
        base = sb("base", [P, NE])
        past = sb("past", [P, NS, NE])
        eidf = sb("eidf", [P, NS])
        where = sb("where", [P, NV, NE])
        posf = sb("posf", [P, NV])
        ex = sb("ex", [P, 3, NT])
        psR = ps("psR", 512)
        psS = ps("psS", 512)
        step = sem("step")
        onehot = sem("onehot")
        ranked = sem("ranked")
        differ = sem("differ")
        expd = sem("expd")
        placed = sem("placed")
        scattered = sem("scattered")
        k128 = T.cst[:, C_K128:C_K128 + NV]
        slot = T.cst[:, C_SLOT:C_SLOT + NS]
        pick = T.cst[:, C_PICK:C_PICK + NE]
        with nc.Block() as block:
            @block.vector
            def _(dve):
                done = [0]

                def then(ins):
                    done[0] += 1
                    ins.then_inc(step, 1)
                    dve.wait_ge(step, done[0])

                then(dve.tensor_copy(aff[:, :, :], T.aff[:, :, :]))
                for c in range(NCH):
                    ohc = oh[:, c * NT:(c + 1) * NT, :]
                    then(dve.tensor_reduce(mx[:, c, :], aff[:, :, :], AX.X, ALU.max))
                    then(dve.tensor_tensor(eq[:, :, :], aff[:, :, :], bc(mx[:, c, :], 2, NE), ALU.is_ge))
                    then(dve.tensor_tensor(eq[:, :, :], eq[:, :, :], bc(pick, 1, NT), ALU.mult))
                    then(dve.tensor_reduce(pk[:, :], eq[:, :, :], AX.X, ALU.max))
                    then(dve.tensor_tensor(ohc, bc(pk[:, :], 2, NE), bc(pick, 1, NT), ALU.is_equal))
                    if c + 1 < NCH:
                        then(dve.scalar_tensor_tensor(aff[:, :, :], ohc, BIG, aff[:, :, :],
                                                      ALU.mult, ALU.add))
                dve.sem_inc(onehot, 1)
                dve.wait_ge(ranked, 1)
                then(dve.tensor_copy(tot[:, :, :].rearrange("p t e -> p (t e)"), psS[:, 0:NV * NE]))
                src, sh, k = tot, 1, 0
                while sh < NV:
                    dst = run[k % 2]
                    dve.tensor_copy(dst[:, 0:sh, :], src[:, 0:sh, :])
                    then(dve.tensor_tensor(dst[:, sh:NV, :], src[:, sh:NV, :], src[:, 0:NV - sh, :], ALU.add))
                    src, sh, k = dst, 2 * sh, k + 1
                count = src[:, NV - 1, :]
                then(dve.tensor_tensor(over[:, :, :], bc(count, 2, NV), bc(k128, 1, NE), ALU.is_gt))
                then(dve.tensor_reduce(nt_e[:, :], over[:, :, :], AX.X, ALU.add))
                prev, sh, j = nt_e, 1, 0
                while sh < NE:
                    dst = cum[j % 2]
                    dve.tensor_copy(dst[:, 0:sh], prev[:, 0:sh])
                    then(dve.tensor_tensor(dst[:, sh:NE], prev[:, sh:NE], prev[:, 0:NE - sh], ALU.add))
                    prev, sh, j = dst, 2 * sh, j + 1
                then(dve.tensor_tensor(base[:, :], prev[:, :], nt_e[:, :], ALU.subtract))
                then(dve.tensor_scalar(base[:, :], base[:, :], float(P), None, ALU.mult))
                then(dve.tensor_tensor(past[:, :, :], bc(slot, 2, NE), bc(prev[:, :], 1, NS), ALU.is_ge))
                then(dve.tensor_reduce(eidf[:, :], past[:, :, :], AX.X, ALU.add))
                then(dve.tensor_scalar(eidf[:, :], eidf[:, :], float(NE - 1), None, ALU.min))
                dve.tensor_copy(T.eid[:, 0:NS], eidf[:, :])
                then(dve.tensor_tensor(where[:, :, :], src[:, :, :], tot[:, :, :], ALU.subtract))
                then(dve.tensor_tensor(where[:, :, :], where[:, :, :], bc(base[:, :], 1, NV), ALU.add))
                then(dve.tensor_tensor(where[:, :, :].rearrange("p t e -> p (t e)"),
                                       where[:, :, :].rearrange("p t e -> p (t e)"),
                                       psR[:, 0:NV * NE], ALU.add))
                then(dve.tensor_tensor(where[:, :, :], where[:, :, :], oh[:, :, :], ALU.mult))
                then(dve.tensor_reduce(posf[:, :], where[:, :, :], AX.X, ALU.add))
                dve.tensor_copy(T.pos[:, 0:NV], posf[:, :]).then_inc(placed, 1)
                if L == 0:
                    dve.tensor_copy(T.top[:, 0, :], mx[:, 0, :])
                else:
                    dve.tensor_tensor(ex[:, 0, :], mx[:, 1, :], mx[:, 0, :], ALU.subtract).then_inc(differ, 1)
                    dve.wait_ge(expd, 1)
                    then(dve.tensor_scalar(ex[:, 2, :], ex[:, 1, :], 1.0, None, ALU.add))
                    then(dve.reciprocal(T.top[:, 0, :], ex[:, 2, :]))
                    then(dve.tensor_tensor(T.top[:, 1, :], ex[:, 1, :], T.top[:, 0, :], ALU.mult))

            @block.scalar
            def _(act):
                if L:
                    act.wait_ge(differ, 1)
                    act.activation(ex[:, 1, :], ex[:, 0, :], ACT.Exp).then_inc(expd, 1)

            @block.tensor
            def _(pe):
                pe.wait_ge(onehot, 1)
                flat = oh[:, :, :].rearrange("p t e -> p (t e)")
                pe.matmul(psR[:, 0:NV * NE], T.cst[:, C_UP:C_UP + P], flat, start=True, stop=True)
                pe.matmul(psS[:, 0:NV * NE], T.cst[:, C_ONE:C_ONE + P], flat, start=True, stop=True)\
                    .then_inc(ranked, 1)

            @block.gpsimd
            def _(pool):
                pool.wait_ge(placed, 1)
                pool.wait_ge(T.cleared[L], 16)
                for v in range(NV):
                    rows = T.nf[:, v % NT, :] if L else T.X[:, v, :]
                    pool.indirect_dma_start(
                        out=T.sorted_dram[L], out_offset=bass.IndirectOffsetOnAxis(ap=T.pos[:, v:v + 1], axis=0),
                        in_=rows, in_offset=None).then_inc(scattered, 16)
                pool.wait_ge(scattered, 16 * NV)
        core.end_phase()


def experts0(core, T):
    nc = core.nc
    with ExitStack() as st:
        sb = lambda n, s, d=F32: core.sb(f"e0_{n}", s, d, st)
        ps = lambda n, c, d=F32: core.ps(f"e0_{n}", c, d, st)
        sem = lambda n: core.phase_sem(f"e0_{n}")
        FC = F0 // P
        b1 = sb("b1", [P, NE * F0])
        b2 = sb("b2", [P, NE * D])
        gb = sb("gb", [P, NE, 2, KD])
        xs = [sb(f"xs{u}", [P, D]) for u in range(2)]
        xT = [sb(f"xT{u}", [P, KD, P]) for u in range(2)]
        h = sb("h", [P, F0])
        hT = sb("hT", [P, F0])
        y = [sb(f"y{u}", [P, D]) for u in range(2)]
        psT = ps("psT", 512)
        psH = ps("psH", 1024)
        psG = ps("psG", 1024)
        psY = ps("psY", 512)
        tab_in = sem("tab_in")
        x_in = [sem(f"x_in{u}") for u in range(2)]
        y_out = [sem(f"y_out{u}") for u in range(2)]
        x_turned = sem("x_turned")
        xT_ready = sem("xT_ready")
        hidden = sem("hidden")
        h_ready = sem("h_ready")
        h_turned = sem("h_turned")
        hT_ready = sem("hT_ready")
        result = sem("result")
        y_ready = sem("y_ready")
        w1f = T.w1[:, :, :, :].rearrange("p e k f -> p (e k f)")
        w2f = T.w2[:, :, :, :].rearrange("p e k d -> p (e k d)")
        gbf = gb[:, :, :, :].rearrange("p e a k -> p (e a k)")
        xd = T.sorted_dram[0].rearrange("(s p) d -> s p d", p=P)
        yd = T.result_dram[0].rearrange("(s p) d -> s p d", p=P)
        NS = SLOT0
        with nc.Block() as block:
            @block.sync
            def _(sp):
                sp.dma_start(gb[:, :, :, :], T.gb0_dram.rearrange("p (e a k) -> p e a k", e=NE, a=2))\
                    .then_inc(tab_in, 16)
                sp.dma_start(b1[:, :], T.b1_dram.partition_broadcast(P)).then_inc(tab_in, 16)
                sp.dma_start(b2[:, :], T.b2_dram.partition_broadcast(P)).then_inc(tab_in, 16)
                sp.sem_inc(y_out[0], 16)
                sp.sem_inc(y_out[1], 16)
                for u in range(2):
                    sp.dma_start(xs[u][:, :], xd[u]).then_inc(x_in[u], 16)
                with sp.Fori(0, NS // 2) as i:
                    for u in range(2):
                        s = 2 * i + u
                        sp.wait_ge(x_turned, s + 3)
                        sp.dma_start(xs[u][:, :], xd[bass.ds(s + 2, 1)].rearrange("s p d -> (s p) d"))\
                            .then_inc(x_in[u], 16)
                        sp.wait_ge(y_ready, s + 2)
                        sp.dma_start(yd[bass.ds(s, 1)].rearrange("s p d -> (s p) d"), y[u][:, :])\
                            .then_inc(y_out[u], 16)
                for u in range(2):
                    sp.wait_ge(y_out[u], 16 * (NS // 2 + 1))
                    sp.wait_ge(x_in[u], 16 * (NS // 2 + 1))

            @block.vector
            def _(dve):
                dve.sem_inc(h_ready, 1)
                dve.sem_inc(y_ready, 1)
                dve.wait_ge(tab_in, 48)
                def bias1(s):
                    e = dve.value_load(T.eid[0:1, bass.ds(s, 1)], min_val=0, max_val=NE - 1)
                    dve.wait_ge(hidden, s + 3)
                    dve.wait_ge(h_turned, s + 1)
                    dve.tensor_tensor(h[:, :], psH[:, :], b1[:, bass.ds(e * F0, F0)], ALU.add)\
                        .then_inc(h_ready, 1)

                def bias2(s, u, k_out):
                    e = dve.value_load(T.eid[0:1, bass.ds(s, 1)], min_val=0, max_val=NE - 1)
                    dve.wait_ge(result, s + 2)
                    dve.wait_ge(y_out[u], k_out)
                    dve.tensor_tensor(y[u][:, :], psY[:, 0:D], b2[:, bass.ds(e * D, D)], ALU.add)\
                        .then_inc(y_ready, 1)

                bias1(0)
                with dve.Fori(0, NS // 2) as i:
                    for u in range(2):
                        s = 2 * i + u
                        bias1(s + 1)
                        bias2(s, u, 16 * i + 16)

            @block.scalar
            def _(act):
                act.sem_inc(xT_ready, 1)
                act.sem_inc(hT_ready, 1)
                act.wait_ge(tab_in, 48)

                def affine(u, s):
                    e = act.value_load(T.eid[0:1, bass.ds(s, 1)], min_val=0, max_val=NE - 1)
                    act.wait_ge(x_turned, s + 3)
                    act.wait_ge(hidden, s + 1)
                    for k in range(KD):
                        a = act.activation(xT[u][:, k, :], psT[:, k * P:k * P + P], ACT.Identity,
                                           scale=gbf[:, bass.ds(e * 4 + k, 1)],
                                           bias=gbf[:, bass.ds(e * 4 + 2 + k, 1)])
                    a.then_inc(xT_ready, 1)

                affine(0, 0)
                affine(1, 1)
                with act.Fori(0, NS // 2) as i:
                    for u in range(2):
                        s = 2 * i + u
                        act.wait_ge(h_turned, s + 2)
                        act.wait_ge(result, s + 1)
                        for a in range(2):
                            r = act.activation(hT[:, a * 512:a * 512 + 512], psG[:, a * 512:a * 512 + 512],
                                               ACT.Relu)
                        r.then_inc(hT_ready, 1)
                        affine(u, s + 2)

            @block.tensor
            def _(pe):
                pe.sem_inc(x_turned, 2)
                pe.sem_inc(hidden, 2)
                pe.sem_inc(h_turned, 1)
                pe.sem_inc(result, 1)
                pe.wait_ge(T.w1_in, 16 * NE)
                pe.wait_ge(T.w2_in, 16 * NE)

                def turn_x(u, s, loads):
                    pe.wait_ge(x_in[u], 16 * loads)
                    pe.wait_ge(xT_ready, s + 1)
                    for k in range(KD):
                        t = pe.transpose(psT[:, k * P:k * P + P], xs[u][:, k * P:k * P + P], T.idf)
                    t.then_inc(x_turned, 1)

                def layer1(u, s):
                    e = pe.value_load(T.eid[0:1, bass.ds(s, 1)], min_val=0, max_val=NE - 1)
                    pe.wait_ge(xT_ready, s + 2)
                    pe.wait_ge(h_ready, s + 1)
                    for n in range(2):
                        for k in range(KD):
                            m = pe.matmul(psH[:, n * 512:n * 512 + 512], xT[u][:, k, :],
                                          w1f[:, bass.ds(e * (KD * F0) + k * F0 + n * 512, 512)],
                                          start=(k == 0), stop=(k == KD - 1))
                    m.then_inc(hidden, 1)

                turn_x(0, 0, 1)
                turn_x(1, 1, 1)
                layer1(0, 0)
                with pe.Fori(0, NS // 2) as i:
                    for u in range(2):
                        s = 2 * i + u
                        pe.wait_ge(h_ready, s + 2)
                        pe.wait_ge(hT_ready, s + 1)
                        for f in range(FC):
                            t = pe.transpose(psG[:, f * P:f * P + P], h[:, f * P:f * P + P], T.idf)
                        t.then_inc(h_turned, 1)
                        layer1(1 - u, s + 1)
                        turn_x(u, s + 2, i + 2)
                        e = pe.value_load(T.eid[0:1, bass.ds(s, 1)], min_val=0, max_val=NE - 1)
                        pe.wait_ge(hT_ready, s + 2)
                        pe.wait_ge(y_ready, s + 1)
                        for f in range(FC):
                            m = pe.matmul(psY[:, 0:D], hT[:, f * P:f * P + P],
                                          w2f[:, bass.ds(e * (FC * D) + f * D, D)],
                                          start=(f == 0), stop=(f == FC - 1))
                        m.then_inc(result, 1)
        core.end_phase()


def experts1(core, T):
    nc = core.nc
    with ExitStack() as st:
        sb = lambda n, s, d=F32: core.sb(f"e1_{n}", s, d, st)
        ps = lambda n, c, d=F32: core.ps(f"e1_{n}", c, d, st)
        sem = lambda n: core.phase_sem(f"e1_{n}")
        W = 2 * F1
        NPT = 3
        NP = SLOT1 // 2
        KF = F1 // P
        w1 = sb("w1", [P, NE, KD, W], BF16)
        w2 = sb("w2", [P, NE, KF, D], BF16)
        b1h = sb("b1h", [P, NE * W], BF16)
        b2h = sb("b2h", [P, NE * D], BF16)
        row = sb("row", [P, P], BF16)
        warm = sb("warm", [P, 1])
        xs = [sb(f"xs{u}", [P, 2, D], BF16) for u in range(2)]
        xT = [sb(f"xT{u}", [P, 2, KD, P], BF16) for u in range(2)]
        g = sb("g", [P, 2, F1])
        sg = sb("sg", [P, 2, F1])
        lin = sb("lin", [P, 2, F1])
        gl = sb("gl", [P, 2, F1])
        r1 = sb("r1", [P, 2, F1])
        r2 = sb("r2", [P, 2, F1])
        parts = [sb(f"parts{u}", [P, NPT, 2, F1], BF16) for u in range(2)]
        aT = sb("aT", [P, 2, NPT * F1], BF16)
        y = [sb(f"y{u}", [P, 2, D]) for u in range(2)]
        psX = [ps(f"psX{u}", 1024, BF16) for u in range(2)]
        psP = ps("psP", 1024)
        psA = ps("psA", 2048, BF16)
        psY = [ps(f"psY{u}", 512) for u in range(2)]
        tab_in = sem("tab_in")
        row_ok = sem("row_ok")
        x_in = [sem(f"x_in{u}") for u in range(2)]
        y_out = [sem(f"y_out{u}") for u in range(2)]
        x_turned = sem("x_turned")
        xT_ready = sem("xT_ready")
        hidden = sem("hidden")
        g_ready = sem("g_ready")
        clipped = sem("clipped")
        sig_ready = sem("sig_ready")
        step = sem("step")
        split = sem("split")
        a_turned = sem("a_turned")
        aT_ready = sem("aT_ready")
        result = sem("result")
        y_ready = sem("y_ready")
        w1f = w1[:, :, :, :].rearrange("p e k f -> p (e k f)")
        w2f = w2[:, :, :, :].rearrange("p e k d -> p (e k d)")
        xd = T.sorted_dram[1].rearrange("(n s p) d -> n p s d", p=P, s=2)
        yd = T.result_dram[1].rearrange("(n s p) d -> n p s d", p=P, s=2)
        pair_of = lambda ap, n: ap[n] if isinstance(n, int) else ap[bass.ds(n, 1)].rearrange("n p s d -> (n p) s d")

        def over_pairs(eng, lo, hi, body):
            with eng.Fori(0, (hi - lo) // 2) as q:
                for v in range(2):
                    body(2 * q + (lo + v), (lo + v) % 2)

        def uses(n, u):
            return 8 * (n - u)

        with nc.Block() as block:
            @block.sync
            def _(sp):
                sp.dma_start(w1[:, :, :, :], T.m1_dram.rearrange("e (k p) f -> p e k f", p=P)).then_inc(tab_in, 16)
                sp.dma_start(w2[:, :, :, :], T.m2_dram.rearrange("e (k p) d -> p e k d", p=P)).then_inc(tab_in, 16)
                sp.dma_start(b1h[:, :], T.mb1_dram.partition_broadcast(P)).then_inc(tab_in, 16)
                sp.dma_start(b2h[:, :], T.mb2_dram.partition_broadcast(P)).then_inc(tab_in, 16)
                sp.sem_inc(y_out[0], 16)
                sp.sem_inc(y_out[1], 16)
                for u in range(2):
                    sp.dma_start(xs[u][:, :, :], xd[u]).then_inc(x_in[u], 16)

                def load(n, u):
                    sp.wait_ge(x_turned, n + 1)
                    sp.dma_start(xs[u][:, :, :], pair_of(xd, n)).then_inc(x_in[u], 16)

                over_pairs(sp, 2, NP, load)
                load(NP, 0)
                for u in range(2):
                    sp.wait_ge(y_out[u], 16 * (NP // 2 + 1))

            @block.gpsimd
            def _(pool):
                pool.memset(row[:, :], 0.0).then_inc(row_ok, 1)
                pool.wait_ge(row_ok, 1)
                pool.memset(row[0:1, :], 1.0).then_inc(row_ok, 1)

            @block.vector
            def _(dve):
                dve.sem_inc(clipped, 1)
                pair = psP[:, :].rearrange("p (s f) -> p s f", s=2)

                def activate(n, u):
                    def then(ins, k):
                        ins.then_inc(step, 1)
                        dve.wait_ge(step, 5 * n + k)

                    dve.wait_ge(hidden, n + 3)
                    dve.tensor_scalar(g[:, :, :], pair[:, :, 0:F1], 7.0, None, ALU.min).then_inc(g_ready, 1)
                    dve.tensor_scalar(lin[:, :, :], pair[:, :, F1:W], 7.0, -7.0, ALU.min, ALU.max)\
                        .then_inc(clipped, 1)
                    dve.wait_ge(sig_ready, n + 1)
                    then(dve.tensor_tensor(gl[:, :, :], g[:, :, :], sg[:, :, :], ALU.mult), 1)
                    dve.wait_ge(clipped, n + 2)
                    then(dve.scalar_tensor_tensor(r1[:, :, :], lin[:, :, :], 1.0, gl[:, :, :], ALU.add, ALU.mult), 2)
                    dve.wait_ge(a_turned, n + 1)
                    then(dve.tensor_scalar(parts[u][:, 0], r1[:, :, :], 0.0, None, ALU.add), 3)
                    then(dve.tensor_tensor(r2[:, :, :], r1[:, :, :], parts[u][:, 0], ALU.subtract), 4)
                    then(dve.tensor_scalar(parts[u][:, 1], r2[:, :, :], 0.0, None, ALU.add), 5)
                    dve.tensor_tensor(parts[u][:, 2], r2[:, :, :], parts[u][:, 1], ALU.subtract)\
                        .then_inc(split, 1)

                over_pairs(dve, 0, NP, activate)

            @block.scalar
            def _(act):
                act.sem_inc(xT_ready, 2)
                act.sem_inc(aT_ready, 1)
                act.sem_inc(y_ready, 2)
                act.activation(warm[:, :], T.cst[:, C_ONE:C_ONE + 1], ACT.Sigmoid)

                def copy_x(n, u):
                    act.wait_ge(x_turned, n + 3)
                    act.wait_ge(hidden, n + 1)
                    act.copy(xT[u][:, :, :, :].rearrange("p s k t -> p (s k t)"), psX[u][:, 0:2 * D])\
                        .then_inc(xT_ready, 1)

                def sigmoid(n):
                    act.wait_ge(g_ready, n + 1)
                    act.activation(sg[:, :, :], g[:, :, :], ACT.Sigmoid, scale=1.702).then_inc(sig_ready, 1)

                def copy_a(n):
                    act.wait_ge(a_turned, n + 3)
                    act.wait_ge(result, n + 1)
                    act.copy(aT[:, :, :], psA[:, :].rearrange("p (s c) -> p s c", s=2)[:, :, 0:NPT * F1])\
                        .then_inc(aT_ready, 1)

                def copy_y(n, u):
                    act.wait_ge(result, n + 2)
                    act.wait_ge(y_out[u], uses(n, u) + 16)
                    act.copy(y[u][:, :, :].rearrange("p s d -> p (s d)"), psY[u][:, :]).then_inc(y_ready, 1)

                def store_y(n, u):
                    act.wait_ge(y_ready, n + 3)
                    act.dma_start(pair_of(yd, n), y[u][:, :, :]).then_inc(y_out[u], 16)

                copy_x(0, 0)
                sigmoid(0)
                copy_x(1, 1)
                copy_x(2, 0)
                sigmoid(1)
                copy_a(0)

                def body(n, u):
                    copy_x(n + 2, u)
                    sigmoid(n + 1)
                    copy_y(n - 1, 1 - u)
                    copy_a(n)
                    store_y(n - 1, 1 - u)

                over_pairs(act, 1, NP - 1, body)
                copy_y(NP - 2, 0)
                copy_a(NP - 1)
                store_y(NP - 2, 0)
                copy_y(NP - 1, 1)
                store_y(NP - 1, 1)

            @block.tensor
            def _(pe):
                pe.sem_inc(x_turned, 2)
                pe.sem_inc(hidden, 2)
                pe.sem_inc(a_turned, 2)
                pe.sem_inc(result, 1)
                pe.wait_ge(tab_in, 64)
                pe.wait_ge(row_ok, 2)
                expert = lambda s: pe.value_load(T.eid[0:1, s:s + 1] if isinstance(s, int) else
                                                 T.eid[0:1, bass.ds(s, 1)], min_val=0, max_val=NE - 1)

                def turn_x(n, u):
                    pe.wait_ge(x_in[u], uses(n, u) + 16)
                    pe.wait_ge(xT_ready, n + 1)
                    for s in range(2):
                        for k in range(KD):
                            c = (s * KD + k) * P
                            t = pe.transpose(psX[u][:, c:c + P], xs[u][:, s, k * P:k * P + P], T.idb[:, :])
                    t.then_inc(x_turned, 1)

                def layer1(n, u):
                    es = [expert(2 * n + s) for s in range(2)]
                    pe.wait_ge(xT_ready, n + 3)
                    pe.wait_ge(clipped, n + 1)
                    for s, e in enumerate(es):
                        for k in range(KD):
                            pe.matmul(psP[:, s * W:s * W + W], xT[u][:, s, k, :],
                                      w1f[:, bass.ds(e * (KD * W) + k * W, W)], start=(k == 0), stop=False)
                        m = pe.matmul(psP[:, s * W:s * W + W], row[:, :], b1h[:, bass.ds(e * W, W)],
                                      start=False, stop=True)
                    m.then_inc(hidden, 1)

                def turn_a(n, u):
                    pe.wait_ge(split, n + 1)
                    pe.wait_ge(aT_ready, n + 1)
                    for s in range(2):
                        for a in range(NPT):
                            for k in range(KF):
                                c = s * 1024 + a * F1 + k * P
                                t = pe.transpose(psA[:, c:c + P], parts[u][:, a, s, k * P:k * P + P], T.idb[:, :])
                    t.then_inc(a_turned, 1)

                def layer2(n, u):
                    es = [expert(2 * n + s) for s in range(2)]
                    pe.wait_ge(aT_ready, n + 2)
                    pe.wait_ge(y_ready, n + 1)
                    for s, e in enumerate(es):
                        dst = psY[u][:, s * D:s * D + D]
                        for a in range(NPT):
                            for k in range(KF):
                                c = a * F1 + k * P
                                pe.matmul(dst, aT[:, s, c:c + P], w2f[:, bass.ds(e * (KF * D) + k * D, D)],
                                          start=(a == 0 and k == 0), stop=False)
                        m = pe.matmul(dst, row[:, :], b2h[:, bass.ds(e * D, D)], start=False, stop=True)
                    m.then_inc(result, 1)

                turn_x(0, 0)
                layer1(0, 0)
                turn_x(1, 1)
                layer1(1, 1)
                turn_x(2, 0)
                turn_a(0, 0)

                def body(n, u):
                    layer1(n + 1, 1 - u)
                    turn_x(n + 2, u)
                    layer2(n - 1, 1 - u)
                    turn_a(n, u)

                over_pairs(pe, 1, NP - 1, body)
                layer2(NP - 2, 0)
                turn_a(NP - 1, 1)
                layer2(NP - 1, 1)
        core.end_phase()


def gate(core, T, L):
    nc = core.nc
    with ExitStack() as st:
        sb = lambda n, s, d=F32: core.sb(f"g{L}_{n}", s, d, st)
        sem = lambda n: core.phase_sem(f"g{L}_{n}")
        R = 4
        xn = [sb(f"xn{u}", [P, D]) for u in range(R)]
        ya = [sb(f"ya{u}", [P, D]) for u in range(R)]
        yb = [sb(f"yb{u}", [P, D]) for u in range(R)]
        va = [sb(f"va{u}", [P, D]) for u in range(R)]
        vb = [sb(f"vb{u}", [P, D]) for u in range(R)]
        hb = [sb(f"hb{u}", [P, 2, D], BF16) for u in range(R)]
        fo = [sb(f"fo{u}", [P, D], BF16 if L else F32) for u in range(R)]
        go = [sb(f"go{u}", [P, D]) for u in range(R)]
        al = sb("al", [P, NT])
        be = sb("be", [P, NT])
        xn_in = [sem(f"xn_in{u}") for u in range(R)]
        y_in = [sem(f"y_in{u}") for u in range(R)]
        g_out = [sem(f"g_out{u}") for u in range(R)]
        alpha_ok = sem("alpha_ok")
        beta_ok = sem("beta_ok")
        step = sem("step")
        mixed = sem("mixed")
        gated = sem("gated")
        xd = T.xn_dram.rearrange("(t p) d -> t p d", p=P)
        gd = T.gate_dram.rearrange("(t p) d -> t p d", p=P)
        NR = NT // R
        with nc.Block() as block:
            @block.sync
            def _(sp):
                for t in range(NT):
                    u = t % R
                    if t >= R:
                        sp.wait_ge(mixed, t - R + 1)
                    sp.dma_start(xn[u][:, :], xd[t]).then_inc(xn_in[u], 16)
                    if t >= R - 1:
                        v = t - R + 1
                        sp.wait_ge(gated, v + 1)
                        sp.dma_start(gd[v], go[v % R][:, :]).then_inc(g_out[v % R], 16)
                for v in range(NT - R + 1, NT):
                    sp.wait_ge(gated, v + 1)
                    sp.dma_start(gd[v], go[v % R][:, :]).then_inc(g_out[v % R], 16)
                for u in range(R):
                    sp.wait_ge(g_out[u], 16 * NR)

            @block.gpsimd
            def _(pool):
                for t in range(NT):
                    u = t % R
                    if t >= R:
                        pool.wait_ge(mixed, t - R + 1)
                    for c in range(L + 1):
                        v = c * NT + t
                        pool.indirect_dma_start(
                            out=(yb if c else ya)[u][:, :], out_offset=None, in_=T.result_dram[L],
                            in_offset=bass.IndirectOffsetOnAxis(ap=T.pos[:, v:v + 1], axis=0))\
                            .then_inc(y_in[u], 16)

            @block.vector
            def _(dve):
                done = [0]

                def then(ins):
                    done[0] += 1
                    ins.then_inc(step, 1)
                    dve.wait_ge(step, done[0])

                if L == 0:
                    dve.wait_ge(alpha_ok, 1)
                    dve.tensor_scalar(be[:, :], al[:, :], -1.0, 1.0, ALU.mult, ALU.add).then_inc(beta_ok, 1)
                    dve.wait_ge(beta_ok, 1)
                for t in range(NT):
                    u = t % R
                    k = t // R + 1
                    dve.wait_ge(xn_in[u], 16 * k)
                    dve.wait_ge(y_in[u], 16 * (L + 1) * k)
                    if t >= R:
                        dve.wait_ge(gated, t - R + 1)
                    if L == 0:
                        then(dve.tensor_tensor(va[u][:, :], xn[u][:, :], ya[u][:, :], ALU.add))
                        then(dve.tensor_scalar(vb[u][:, :], xn[u][:, :], be[:, t:t + 1], None, ALU.mult))
                        dve.scalar_tensor_tensor(fo[u][:, :], va[u][:, :], al[:, t:t + 1], vb[u][:, :],
                                                 ALU.mult, ALU.add).then_inc(mixed, 1)
                    else:
                        then(dve.tensor_scalar(va[u][:, :], yb[u][:, :], T.top[:, 1, t:t + 1], None, ALU.mult))
                        dve.tensor_copy(hb[u][:, 1, :], xn[u][:, :])
                        then(dve.scalar_tensor_tensor(hb[u][:, 0, :], ya[u][:, :], T.top[:, 0, t:t + 1],
                                                      va[u][:, :], ALU.mult, ALU.add))
                        dve.tensor_tensor(fo[u][:, :], hb[u][:, 0, :], hb[u][:, 1, :], ALU.add)\
                            .then_inc(mixed, 1)

            @block.scalar
            def _(act):
                if L == 0:
                    act.activation(al[:, :], T.top[:, 0, :], ACT.Sigmoid).then_inc(alpha_ok, 1)
                for t in range(NT):
                    u = t % R
                    act.wait_ge(mixed, t + 1)
                    if t >= R:
                        act.wait_ge(g_out[u], 16 * (t // R))
                    act.activation(go[u][:, :], fo[u][:, :], ACT.Silu).then_inc(gated, 1)
        core.end_phase()


def combine(core, T, L, O, x_dram, w_dram, out_dram):
    nc = core.nc
    with ExitStack() as st:
        sb = lambda n, s, d=F32: core.sb(f"c{L}_{n}", s, d, st)
        ps = lambda n, c, d=F32: core.ps(f"c{L}_{n}", c, d, st)
        sem = lambda n: core.phase_sem(f"c{L}_{n}")
        w = sb("w", [P, KD, D])
        bias = sb("bias", [P, D])
        x = [sb(f"x{u}", [P, D]) for u in range(2)]
        g = [sb(f"g{u}", [P, D]) for u in range(2)]
        os_ = [sb(f"os{u}", [P, D]) for u in range(2)]
        oT = [sb(f"oT{u}", [P, D]) for u in range(2)]
        s0 = [sb(f"s0{u}", [P, D]) for u in range(2)]
        s1 = [sb(f"s1{u}", [P, D]) for u in range(2)]
        r = [sb(f"r{u}", [P, D]) for u in range(2)]
        psT = [ps(f"psT{u}", 512) for u in range(2)]
        psS = [ps(f"psS{u}", 512) for u in range(2)]
        passed = sem("passed")
        w_in = sem("w_in")
        xg_in = [sem(f"xg_in{u}") for u in range(2)]
        staged = sem("staged")
        turned = sem("turned")
        oT_ready = sem("oT_ready")
        product = sem("product")
        biased = sem("biased")
        gated = sem("gated")
        added = sem("added")
        out = [sem(f"out{u}") for u in range(2)]
        xd = x_dram.rearrange("(t p) d -> t p d", p=P)
        gd = T.gate_dram.rearrange("(t p) d -> t p d", p=P)
        od = out_dram.rearrange("(t p) d -> t p d", p=P)
        tile = lambda ap, n: ap[bass.ds(n, 1)].rearrange("t p d -> (t p) d")
        with nc.Block() as block:
            @block.sync
            def _(sp):
                sp.dma_start(w[:, :, :], w_dram.rearrange("(k p) n -> p k n", p=P)).then_inc(w_in, 16)
                if L:
                    sp.dma_start(bias[:, :], T.bproj_dram.partition_broadcast(P)).then_inc(w_in, 16)
                sp.sem_inc(out[0], 16)
                sp.sem_inc(out[1], 16)
                with sp.Fori(0, NT // 2) as i:
                    for u in range(2):
                        n = 2 * i + u
                        sp.wait_ge(added, n + 1)
                        sp.dma_start(x[u][:, :], tile(xd, n)).then_inc(xg_in[u], 16)
                        sp.dma_start(g[u][:, :], tile(gd, n)).then_inc(xg_in[u], 16)
                for u in range(2):
                    sp.wait_ge(out[u], 16 * (NT // 2 + 1))

            @block.gpsimd
            def _(pool):
                for b in range(NB):
                    with pool.Fori(0, TS // 2) as i:
                        for u in range(2):
                            n = b * TS + 2 * i + u
                            pool.wait_ge(turned, n + 1)
                            pool.sem_inc(passed, 1)
                            src = O[:, b * NG:(b + 1) * NG, :, :].rearrange("p g t c -> p g (t c)")[
                                :, :, bass.ds((2 * i + u) * GW, GW)]
                            pool.tensor_copy(os_[u][:, :].rearrange("p (g c) -> p g c", g=NG), src)\
                                .then_inc(staged, 1)

            @block.tensor
            def _(pe):
                pe.sem_inc(turned, 2)
                pe.sem_inc(product, 2)
                pe.wait_ge(w_in, 32 if L else 16)
                with pe.Fori(0, NT // 2) as i:
                    for u in range(2):
                        n = 2 * i + u
                        pe.wait_ge(staged, n + 1)
                        pe.wait_ge(oT_ready, n + 1)
                        for k in range(KD):
                            t = pe.transpose(psT[u][:, k * P:k * P + P], os_[u][:, k * P:k * P + P], T.idf)
                        t.then_inc(turned, 1)
                    for u in range(2):
                        n = 2 * i + u
                        pe.wait_ge(oT_ready, n + 3)
                        pe.wait_ge(biased, n + 1)
                        for k in range(KD):
                            m = pe.matmul(psS[u][:, 0:D], oT[u][:, k * P:k * P + P], w[:, k, :],
                                          start=(k == 0), stop=(k == KD - 1))
                        m.then_inc(product, 1)

            @block.vector
            def _(dve):
                dve.sem_inc(biased, 2)
                dve.sem_inc(added, 2)
                if L:
                    dve.wait_ge(w_in, 32)
                with dve.Fori(0, NT // 2) as i:
                    for u in range(2):
                        n = 2 * i + u
                        dve.wait_ge(product, n + 3)
                        dve.wait_ge(xg_in[u], 32 * i + 32)
                        if L:
                            dve.tensor_tensor(s0[u][:, :], psS[u][:, 0:D], bias[:, :], ALU.add)\
                                .then_inc(biased, 1)
                            dve.wait_ge(biased, n + 3)
                            dve.tensor_tensor(s1[u][:, :], s0[u][:, :], g[u][:, :], ALU.mult)\
                                .then_inc(gated, 1)
                            dve.wait_ge(gated, n + 1)
                        else:
                            dve.tensor_tensor(s1[u][:, :], psS[u][:, 0:D], g[u][:, :], ALU.mult)\
                                .then_inc(biased, 1)
                            dve.wait_ge(biased, n + 3)
                        dve.wait_ge(out[u], 16 * i + 16)
                        dve.tensor_tensor(r[u][:, :], s1[u][:, :], x[u][:, :], ALU.add).then_inc(added, 1)

            @block.scalar
            def _(act):
                act.sem_inc(oT_ready, 2)
                with act.Fori(0, NT // 2) as i:
                    for u in range(2):
                        n = 2 * i + u
                        act.wait_ge(turned, n + 3)
                        act.wait_ge(product, n + 1)
                        act.copy(oT[u][:, :], psT[u][:, 0:D]).then_inc(oT_ready, 1)
                    for u in range(2):
                        n = 2 * i + u
                        act.wait_ge(added, n + 3)
                        act.dma_start(tile(od, n), r[u][:, :]).then_inc(out[u], 16)
        core.end_phase()


def unit_maxima():
    return [(c, i4, h, hf) for c in range(NC) for i4 in range(CT) for h in range(HG)
            for hf in range(2 if CT * c + i4 >= 8 else 1)]


def piece_tiles(c, i4, h, hf):
    return min(8, CT * c + i4 + 1 - 8 * hf)


PIECES = unit_maxima()
NPIECE = len(PIECES)
NSCORE = sum(CT * (c + 1) * HG for c in range(NC))
NGROUP = NSCORE // HG
AHEAD = [n for n in range(NPIECE) if sum(piece_tiles(*p) for p in PIECES[:n]) >= HG * 58][0] // 2 * 2


def chunk_end(c):
    return sum(p[0] <= c for p in PIECES)


def group_number(c, j):
    return CT * c * (c + 1) // 2 + j


def maxima_steps(which, lo, hi):
    out = []
    for n in range(lo, hi):
        out.append(("max", which) + (n,) + PIECES[n])
        if n + 1 == chunk_end(PIECES[n][0]):
            out.append(("negate", which, PIECES[n][0]))
    return out


def attention_plan(kind):
    turns = [("turn", 1, b % 2, b // 2 % HG, b // (2 * HG)) for b in range(4 * HG)]
    if kind == "first":
        out = list(turns)
        for s in maxima_steps(1, 0, AHEAD):
            out.append(s)
            if s[0] == "negate":
                out += [("lift", 1, s[2], 0), ("lift", 1, s[2], 1)]
        return out
    scores = [("score", 0, c, j, h) for c in range(NC) for j in range(CT * (c + 1)) for h in range(HG)]
    tiles = [min(CT, CT * (s[2] + 1) - s[3]) for s in scores]
    at = [sum(tiles[:n]) for n in range(NSCORE + 1)]
    beside = [[] for _ in scores]

    def spread(steps, lo, hi):
        weight = [piece_tiles(*s[3:]) if s[0] == "max" else 0 if s[0] == "negate" else 1 for s in steps]
        total, gone = sum(weight), 0
        for s, w in zip(steps, weight):
            where = lo + (hi - lo) * gone / total
            slot = max(n for n in range(NSCORE) if at[n] <= where)
            beside[slot].append(s)
            if s[0] == "negate":
                beside[slot + 3].append(("lift", s[1], s[2], 0))
                beside[slot + 5].append(("lift", s[1], s[2], 1))
            gone += w

    spread(maxima_steps(0, AHEAD, NPIECE), 0, HG * 70)
    if kind != "tail":
        spread(turns, HG * 3, HG * 64)
        spread(maxima_steps(1, 0, AHEAD), HG * 71, HG * 133)
    plan = []
    for n, s in enumerate(scores):
        _, _, c, j, h = s
        plan.append(s)
        plan += beside[n]
        if h == HG - 1:
            if j:
                plan.append(("value", 0, c, j - 1))
                if j == 2 and (c or kind != "head"):
                    plan.append(("finish", 0, c - 1) if c else ("finish", -1, NC - 1))
            elif c:
                plan += [("value", 0, c - 1, CT * c - 1), ("take", 0, c - 1)]
            elif kind != "head":
                plan += [("value", -1, NC - 1, CT * NC - 1), ("take", -1, NC - 1)]
    if kind == "tail":
        plan += [("value", 0, NC - 1, CT * NC - 1), ("take", 0, NC - 1), ("finish", 0, NC - 1)]
    return plan


class Plan:

    def __init__(self, kind):
        self.steps, self.bank = [], 0
        self.last_use = {}
        for s in attention_plan(kind):
            self.steps.append((s, self.bank))
            if s[0] == "turn":
                self.last_use["turn"] = self.bank
            if s[0] == "lift":
                self.last_use["lift", s[1], s[2]] = self.bank
            self.bank += s[0] in ("turn", "lift", "finish")


def attention(core, T, L, O):
    nc = core.nc
    first, head, body, tail = (Plan(k) for k in ("first", "head", "body", "tail"))
    with ExitStack() as st:
        sb = lambda n, s, d=F32: core.sb(f"s{L}_{n}", s, d, st)
        ps = lambda n, c, d=F32: core.ps(f"s{L}_{n}", c, d, st)
        sem = lambda n: core.phase_sem(f"s{L}_{n}")
        raw = [sb(f"raw{u}", [P, TS, 3 * GW]) for u in range(2)]
        rest = sb("rest", [P, TS, GW])
        qst = sb("qst", [P, TS, HG, NPART, DH], BF16)
        kst = sb("kst", [P, TS, HG, KR + MR], BF16)
        va = [sb(f"va{u}", [P, TS, HG, 32]) for u in range(2)]
        qT = [sb(f"qT{u}", [P, HG, S], BF16) for u in range(2)]
        kT = [sb(f"kT{u}", [P, HG, S], BF16) for u in range(2)]
        NPB = 8
        pr = [sb(f"pr{i}", [P, CH]) for i in range(NPB)]
        half = sb("half", [P, CT, HG, 2])
        nm = sb("nm", [P, CT, HG])
        nmp = sb("nmp", [P, CT, HG, MR], BF16)
        osb = sb("osb", [P, CH])
        rcp = sb("rcp", [P, CT, HG])
        psM = [ps(f"psM{i}", 1024) for i in range(2)]
        psS = [ps(f"psS{i}", CH) for i in range(2)]
        psV = ps("psV", CH)
        psX = ps("psX", 512)
        psXb = psX[:, :].bitcast(BF16)
        loaded = [sem(f"loaded{u}") for u in range(2)]
        pad_ok = sem("pad_ok")
        passed = sem("passed")
        split = sem("split")
        parts_ready = sem("parts_ready")
        staged = sem("staged")
        stacks_used = sem("stacks_used")
        bank_full = sem("bank_full")
        bank_free = sem("bank_free")
        rowscores = sem("rowscores")
        reduced = sem("reduced")
        half_ok = sem("half_ok")
        max_split = sem("max_split")
        scored = sem("scored")
        exped = sem("exped")
        valued = sem("valued")
        taken = sem("taken")
        rcp_ok = sem("rcp_ok")
        O2 = O[:, :, :, :].rearrange("p n t c -> p (n t c)")
        qd = T.qkv.rearrange("n p t c -> n p (t c)")

        def segments(eng, emit):
            emit(first, -1, 1, 0, None)
            emit(head, 0, 0, first.bank, first)
            base = first.bank + head.bank
            with eng.Fori(0, NU // 2 - 1) as i:
                emit(body, 2 * i + 1, 1, 2 * body.bank * i + base, head)
                emit(body, 2 * i + 2, 0, 2 * body.bank * i + base + body.bank, body)
            emit(tail, NU - 1, 1, base + (NU - 2) * body.bank, body)

        def lifted(plan, before, c, bank0):
            if ("lift", 0, c) in plan.last_use:
                return bank0 + plan.last_use["lift", 0, c] + 2
            return bank0 - (before.bank - before.last_use["lift", 1, c]) + 2

        for c in range(NC):
            key = ("lift", 1, c)
            if key in head.last_use:
                assert head.bank - head.last_use[key] == body.bank - body.last_use[key]

        def first_col(c, j):
            return max(0, j - CT * c) * P

        with nc.Block() as block:
            @block.sync
            def _(sp):
                for m in range(2):
                    sp.wait_ge(staged, m + 1)
                    sp.dma_start(raw[m][:, :, :].rearrange("p t c -> p (t c)"), qd[m]).then_inc(loaded[m], 16)
                with sp.Fori(1, NU // 2) as i:
                    for u in range(2):
                        m = 2 * i + u
                        sp.wait_ge(staged, m + 1)
                        sp.dma_start(raw[u][:, :, :].rearrange("p t c -> p (t c)"),
                                     qd[bass.ds(m, 1)].rearrange("n p c -> (n p) c")).then_inc(loaded[u], 16)

            @block.gpsimd
            def _(pool):
                pool.sem_inc(staged, 2)
                for u in range(2):
                    pool.memset(va[u][:, :, :, DH:32], 0.0).then_inc(pad_ok, 1)
                pool.memset(kst[:, :, :, KR:KR + MR], 1.0).then_inc(pad_ok, 1)
                pool.wait_ge(pad_ok, 3)
                for u in range(2):
                    pool.memset(va[u][:, :, :, DH:DH + 1], 1.0).then_inc(pad_ok, 1)
                pool.wait_ge(pad_ok, 5)

                def stage(i):
                    for u in range(2):
                        m = 2 * i + u
                        pool.wait_ge(loaded[u], 16 * i + 16)
                        pool.wait_ge(stacks_used, m + 1)
                        pool.sem_inc(passed, 1)
                        q = raw[u][:, :, 0:GW].rearrange("p t (h d) -> p t h d", h=HG)
                        k = raw[u][:, :, GW:2 * GW].rearrange("p t (h d) -> p t h d", h=HG)
                        r = rest[:, :, :].rearrange("p t (h d) -> p t h d", h=HG)
                        Q = lambda s: qst[:, :, :, s, :]
                        K = lambda s: kst[:, :, :, s * DH:(s + 1) * DH]
                        done = [0]

                        def then(ins):
                            done[0] += 1
                            ins.then_inc(split, 1)
                            pool.wait_ge(split, 8 * m + done[0])
                            pool.sem_inc(passed, 1)

                        then(pool.tensor_copy(Q(0), q))
                        pool.tensor_copy(Q(1), Q(0))
                        pool.tensor_copy(Q(3), Q(0))
                        then(pool.tensor_tensor(r, q, Q(0), ALU.subtract))
                        then(pool.tensor_copy(Q(2), r))
                        pool.tensor_copy(Q(4), Q(2))
                        then(pool.tensor_tensor(Q(5), r, Q(2), ALU.subtract))
                        then(pool.tensor_copy(K(0), k))
                        pool.tensor_copy(K(2), K(0))
                        pool.tensor_copy(K(5), K(0))
                        then(pool.tensor_tensor(r, k, K(0), ALU.subtract))
                        then(pool.tensor_copy(K(1), r))
                        pool.tensor_copy(K(4), K(1))
                        then(pool.tensor_tensor(K(3), r, K(1), ALU.subtract))
                        pool.sem_inc(parts_ready, 1)
                        free = 2 if isinstance(i, int) else NGROUP * (2 * (i - 1) + u + 1) + 2
                        pool.wait_ge(valued, free)
                        pool.sem_inc(passed, 1)
                        pool.tensor_copy(va[u][:, :, :, 0:DH],
                                         raw[u][:, :, 2 * GW:3 * GW].rearrange("p t (h d) -> p t h d", h=HG))\
                            .then_inc(staged, 1)
                stage(0)
                with pool.Fori(1, NU // 2) as i:
                    stage(i)

            @block.tensor
            def _(pe):
                pe.sem_inc(stacks_used, 1)
                pe.sem_inc(valued, 2)

                def emit(plan, n, u, bank0, before):
                    for step, bank in plan.steps:
                        kind, which = step[0], step[1]
                        par = (u + which) % 2
                        m = n + which
                        if kind == "turn":
                            _, _, isk, h, lo = step
                            if (isk, h, lo) == (0, 0, 0):
                                pe.wait_ge(parts_ready, m + 1)
                            pe.wait_ge(bank_free, bank0 + bank + 1)
                            rows = KR + MR if isk else KR
                            for t in range(8):
                                src = kst[:, 8 * lo + t, h, :] if isk else \
                                    qst[:, 8 * lo + t, h, :, :].rearrange("p s d -> p (s d)")
                                x = pe.transpose(psXb[0:rows, t * P:t * P + P], src, T.idb[:, :])
                            x.then_inc(bank_full, 1)
                            if bank == plan.last_use["turn"]:
                                pe.wait_ge(bank_full, bank0 + bank + 1)
                                pe.sem_inc(stacks_used, 1)
                        elif kind == "max":
                            _, _, k, c, i4, h, hf = step
                            if which and k == 0:
                                pe.wait_ge(bank_free, bank0 + plan.last_use["turn"] + 2)
                            pe.wait_ge(reduced, NPIECE * m + k + 1)
                            i = CT * c + i4
                            end = P * (i + 1)
                            k0, k1 = 1024 * hf, min(1024 * hf + 1024, end)
                            dst = psM[k % 2]
                            for a in range(k0, k1, 512):
                                z = min(a + 512, k1)
                                x = pe.matmul(dst[:, a - k0:z - k0], qT[par][0:KR, h, i * P:i * P + P],
                                              kT[par][0:KR, h, a:z], start=True, stop=(z < end))
                            if k1 == end:
                                x = pe.matmul(dst[:, end - P - k0:end - k0], T.idb[:, :], T.mqb[:, :],
                                              start=False, stop=True)
                            x.then_inc(rowscores, 1)
                        elif kind == "lift":
                            _, _, c, pair = step
                            if pair == 0:
                                pe.wait_ge(max_split, NC * m + c + 1)
                            pe.wait_ge(bank_free, bank0 + bank + 1)
                            for hh in range(2):
                                for i4 in range(CT):
                                    x = pe.transpose(psXb[KR:KR + MR, hh * CH + i4 * P:hh * CH + i4 * P + P],
                                                     nmp[:, i4, 2 * pair + hh, :], T.idb[:, :])
                            x.then_inc(bank_full, 1)
                        elif kind == "score":
                            _, _, c, j, h = step
                            k = HG * group_number(c, j) + h
                            if j == 0 and h == 0:
                                pe.wait_ge(bank_free, lifted(plan, before, c, bank0))
                            pe.wait_ge(exped, NSCORE * m + k + 1)
                            a = first_col(c, j)
                            diag = j >= CT * c
                            x = pe.matmul(psS[k % 2][:, a:CH], kT[par][0:KR + MR, h, j * P:j * P + P],
                                          qT[par][0:KR + MR, h, c * CH + a:c * CH + CH],
                                          start=True, stop=not diag)
                            if diag:
                                x = pe.matmul(psS[k % 2][:, a:a + P], T.idb[:, :], T.mkb[:, :],
                                              start=False, stop=True)
                            x.then_inc(scored, 1)
                        elif kind == "value":
                            _, _, c, j = step
                            g = group_number(c, j)
                            pe.wait_ge(exped, NSCORE * m + HG * g + HG + 2)
                            if j == 0:
                                pe.wait_ge(taken, NC * m + c + 1)
                                if c == 0:
                                    pe.wait_ge(staged, m + 3)
                            a = first_col(c, j)
                            for h in range(HG):
                                x = pe.matmul(psV[32 * h:32 * h + 32, a:CH], va[par][:, j, h, :],
                                              pr[(HG * g + h) % NPB][:, a:CH],
                                              start=(j == 0), stop=(j == CT * c + CT - 1))
                            x.then_inc(valued, 1)
                        elif kind == "finish":
                            _, _, c = step
                            pe.wait_ge(taken, NC * m + c + 2)
                            pe.wait_ge(bank_free, bank0 + bank + 1)
                            for i4 in range(CT):
                                x = pe.transpose(psX[:, i4 * P:i4 * P + P], osb[:, i4 * P:i4 * P + P], T.idf)
                            x.then_inc(bank_full, 1)

                segments(pe, emit)

            @block.scalar
            def _(act):
                act.sem_inc(exped, 2)

                def emit(plan, n, u, bank0, before):
                    for step, bank in plan.steps:
                        kind, which = step[0], step[1]
                        par = (u + which) % 2
                        m = n + which
                        if kind == "turn":
                            _, _, isk, h, lo = step
                            act.wait_ge(bank_full, bank0 + bank + 1)
                            rows = KR + MR if isk else KR
                            dst = kT[par] if isk else qT[par]
                            act.copy(dst[0:rows, h, lo * 1024:lo * 1024 + 1024], psXb[0:rows, 0:1024])\
                                .then_inc(bank_free, 1)
                        elif kind == "score":
                            _, _, c, j, h = step
                            g = group_number(c, j)
                            k = HG * g + h
                            a = first_col(c, j)
                            act.wait_ge(scored, NSCORE * m + k + 1)
                            if h == 0:
                                act.wait_ge(valued, NGROUP * m + g + 1)
                            act.activation(pr[k % NPB][:, a:CH], psS[k % 2][:, a:CH], ACT.Exp,
                                           scale=float(DH) ** -0.5).then_inc(exped, 1)

                segments(act, emit)

            @block.vector
            def _(dve):
                dve.sem_inc(bank_free, 1)
                dve.sem_inc(reduced, 2)
                dve.sem_inc(taken, 1)

                def emit(plan, n, u, bank0, before):
                    for step, bank in plan.steps:
                        kind, which = step[0], step[1]
                        par = (u + which) % 2
                        m = n + which
                        if kind == "max":
                            _, _, k, c, i4, h, hf = step
                            dve.wait_ge(rowscores, NPIECE * m + k + 1)
                            w = P * piece_tiles(c, i4, h, hf)
                            dve.tensor_reduce(half[:, i4, h, hf:hf + 1], psM[k % 2][:, 0:w], AX.X, ALU.max,
                                              negate=True).then_inc(reduced, 1)
                        elif kind == "negate":
                            _, _, c = step
                            g = NC * m + c
                            dve.wait_ge(reduced, NPIECE * m + chunk_end(c) + 2)
                            if c >= 2:
                                dve.tensor_tensor(nm[:, :, :], half[:, :, :, 0], half[:, :, :, 1], ALU.min)\
                                    .then_inc(half_ok, 1)
                            else:
                                dve.tensor_copy(nm[:, :, :], half[:, :, :, 0]).then_inc(half_ok, 1)
                            dve.wait_ge(half_ok, 2 * g + 1)
                            dve.tensor_copy(nmp[:, :, :, 0], nm[:, :, :]).then_inc(half_ok, 1)
                            dve.wait_ge(half_ok, 2 * g + 2)
                            dve.tensor_tensor(nmp[:, :, :, 1], nm[:, :, :], nmp[:, :, :, 0], ALU.subtract)\
                                .then_inc(max_split, 1)
                        elif kind == "lift":
                            _, _, c, pair = step
                            dve.wait_ge(bank_full, bank0 + bank + 1)
                            dve.tensor_copy(qT[par][KR:KR + MR, 2 * pair:2 * pair + 2, c * CH:c * CH + CH],
                                            psXb[KR:KR + MR, :].rearrange("p (h q) -> p h q", h=2))\
                                .then_inc(bank_free, 1)
                        elif kind == "take":
                            _, _, c = step
                            dve.wait_ge(valued, NGROUP * m + group_number(c, CT * (c + 1)) + 2)
                            dve.tensor_copy(osb[:, :], psV[:, :]).then_inc(taken, 1)
                        elif kind == "finish":
                            _, _, c = step
                            dve.wait_ge(bank_full, bank0 + bank + 1)
                            view = psX[:, :].rearrange("p (t h w) -> p t h w", t=CT, h=HG)
                            dve.reciprocal(rcp[:, :, :], view[:, :, :, DH]).then_inc(rcp_ok, 1)
                            dve.wait_ge(rcp_ok, NC * m + c + 1)
                            dst = O2[:, bass.ds(m * (TS * GW) + c * CT * GW, CT * GW)]
                            dve.tensor_tensor(dst.rearrange("p (t h d) -> p t h d", t=CT, h=HG),
                                              view[:, :, :, 0:DH], bc(rcp[:, :, :], 3, DH), ALU.mult)\
                                .then_inc(bank_free, 1)

                segments(dve, emit)
        core.end_phase()


def build(nc, ins, out):
    with ExitStack() as stack:
        core = Core(nc, stack)

        class T:
            pass

        T.cst_dram, T.cos_dram, T.sin_dram = ins["cst"], ins["cos"], ins["sin"]
        T.cent_dram, T.w1_dram, T.w2_dram = ins["cent"], ins["w1"], ins["w2"]
        T.gb0_dram, T.b1_dram, T.b2_dram = ins["gb0"], ins["b1"], ins["b2"]
        T.bqkv_dram, T.bproj_dram = ins["bqkv"], ins["bproj"]
        T.nw_dram, T.gw_dram, T.gb_dram = ins["nw"], ins["gw"], ins["gb"]
        T.m1_dram, T.m2_dram, T.mb1_dram, T.mb2_dram = ins["m1"], ins["m2"], ins["mb1"], ins["mb2"]
        T.qkv = core.dram("qkv", [NU, P, TS, 3 * GW])
        T.xn_dram = core.dram("xn", [NT * P, D])
        T.gate_dram = core.dram("gatev", [NT * P, D])
        x1_dram = core.dram("x1", [NT * P, D])
        T.sorted_dram = [core.dram("sorted0", [(SLOT0 + 2) * P, D]), core.dram("sorted1", [(SLOT1 + 2) * P, D], BF16)]
        T.result_dram = [core.dram("result0", [SLOT0 * P, D]), core.dram("result1", [SLOT1 * P, D])]
        load_constants(core, T)
        T.w1_in = core.sem("w1_in")
        T.w2_in = core.sem("w2_in")
        T.cleared = [core.sem("cleared0"), core.sem("cleared1")]
        T.aff = core.sb("aff", [P, NT, NE])
        T.pos = core.sb("pos", [P, 2 * NT], U32)
        T.eid = core.sb("eid", [P, SLOT1 + 2], I32)
        T.top = core.sb("top", [P, 2, NT])

        with nc.Block() as block:
            @block.scalar
            def _(act):
                act.dma_start(T.sorted_dram[0].rearrange("(s p) d -> p s d", p=P),
                              bc(T.zero[:, :], 1, SLOT0 + 2)).then_inc(T.cleared[0], 16)
                act.dma_start(T.sorted_dram[1].rearrange("(s p) d -> p s d", p=P),
                              bc(T.zero[:, 0:D // 2].bitcast(BF16), 1, SLOT1 + 2)).then_inc(T.cleared[1], 16)

        with ExitStack() as st:
            T.w1 = core.sb("w1", [P, NE, KD, F0], F32, st)
            T.w2 = core.sb("w2", [P, NE, F0 // P, D], F32, st)
            with ExitStack() as sx:
                T.X = core.sb("X0", [P, NT, D], F32, sx)
                norm_project(core, T, 0, ins["x"], ins["wqkv0"], T.X)
                norm_again(core, T.X)
                route(core, T, 0)
            experts0(core, T)
        gate(core, T, 0)
        with ExitStack() as st:
            O = core.sb("O0", [P, NU, TS, GW], F32, st)
            attention(core, T, 0, O)
            combine(core, T, 0, O, ins["x"], ins["wo0"], x1_dram)

        with ExitStack() as st:
            T.X = core.sb("X1", [P, NT, D], F32, st)
            T.nf = core.sb("nf", [P, NT, D], BF16, st)
            norm_project(core, T, 1, x1_dram, ins["wqkv1"], T.X)
            scores_of_layer1(core, T, T.X)
            route(core, T, 1)
        experts1(core, T)
        gate(core, T, 1)
        with ExitStack() as st:
            O = core.sb("O1", [P, NU, TS, GW], F32, st)
            attention(core, T, 1, O)
            combine(core, T, 1, O, x1_dram, ins["wo1"], out)


def kernel(**inputs):
    import numpy as _np
    import concourse.bacc as _bacc
    from concourse import mybir as _mybir
    from concourse.bass_utils import run_bass_kernel_spmd as _run

    a = {k: _np.asarray(v) for k, v in inputs.items()}
    def grouped(q, k, v):
        parts = [_np.reshape(m, m.shape[:-1] + (NG, GW)) for m in (q, k, v)]
        return _np.ascontiguousarray(_np.stack(parts, axis=-2).reshape(q.shape[:-1] + (3 * D,)))

    wq1 = a["L1_attn_Wqkv"]
    bq1 = a["L1_attn_bqkv"]
    m1 = a["L1_ffn_mlp1_weight"]
    mb1 = a["L1_ffn_mlp1_bias"]
    cos, sin = rotary_tables()
    col = lambda t: t.reshape(NE, KD, P).transpose(2, 0, 1)
    arrays = {
        "x": a["L0_attn_x"].reshape(NT * P, D),
        "wqkv0": grouped(a["L0_attn_W_Q"], a["L0_attn_W_K"], a["L0_attn_W_V"]),
        "wo0": a["L0_attn_W_o"],
        "cent": a["L0_ffn_centroids"].T,
        "w1": a["L0_ffn_w1"].transpose(0, 2, 1),
        "w2": a["L0_ffn_w2"].transpose(0, 2, 1),
        "b1": a["L0_ffn_b1"].reshape(-1),
        "b2": a["L0_ffn_b2"].reshape(-1),
        "gb0": _np.stack([col(a["L0_ffn_ln_g"]), col(a["L0_ffn_ln_b"])], axis=2).reshape(P, -1),
        "wqkv1": grouped(wq1[:, 0:D], wq1[:, D:2 * D], wq1[:, 2 * D:]),
        "bqkv": grouped(bq1[0:D], bq1[D:2 * D], bq1[2 * D:]),
        "wo1": a["L1_attn_Wproj"],
        "bproj": a["L1_attn_bproj"],
        "nw": a["L1_ffn_norm_weight"],
        "gw": a["L1_ffn_gate_weight"].T,
        "gb": a["L1_ffn_gate_bias"],
        "m1": _np.concatenate([m1[:, 0::2], m1[:, 1::2]], axis=1).transpose(0, 2, 1),
        "mb1": _np.concatenate([mb1[:, 0::2], mb1[:, 1::2]], axis=1).reshape(-1),
        "m2": a["L1_ffn_mlp2_weight"].transpose(0, 2, 1),
        "mb2": a["L1_ffn_mlp2_bias"].reshape(-1),
        "cst": constant_table(), "cos": cos, "sin": sin,
    }
    nc = _bacc.Bacc("TRN2", target_bir_lowering=False, num_devices=1)
    feed, ins = {}, {}
    for name, v in arrays.items():
        v = _np.ascontiguousarray(v)
        feed["in_" + name] = v
        ins[name] = nc.dram_tensor("in_" + name, v.shape, _mybir.dt.from_np(v.dtype), kind="ExternalInput").ap()
    out = nc.dram_tensor("out", (NT * P, D), _mybir.dt.from_np(_np.dtype("float32")), kind="ExternalOutput").ap()
    build(nc, ins, out)
    r = _run(nc, [feed], core_ids=[0])
    return r.results[0]["out"].reshape(NB, S, D)
```

```python
from contextlib import ExitStack

import numpy as np

import concourse.bass as bass
from concourse import mybir

F32 = mybir.dt.float32
BF16 = mybir.dt.bfloat16
I32 = mybir.dt.int32
U32 = mybir.dt.uint32
ALU = mybir.AluOpType
ACT = mybir.ActivationFunctionType
AX = mybir.AxisListType

P = 128
D = 256
KD = D // P
H = 16
DH = D // H
HG = 4
NG = H // HG
GW = HG * DH
S = 2048
NB = 2
TS = S // P
NT = NB * TS
NU = NG * NB
NE = 8
F0 = 1024
F1 = 256
EPS = 1e-5
SLOT0 = 40
SLOT1 = 72
CH = 512
CT = CH // P
NC = S // CH
NPART = 6
KR = NPART * DH
MR = 2
BIG = -1.0e30

C_ID, C_UP, C_MQ, C_MK, C_ONE, C_K128, C_SLOT, C_PICK = 0, 128, 256, 384, 512, 640, 704, 784
C_COLS = 792


def constant_table():
    t = np.zeros((P, C_COLS), np.float32)
    r = np.arange(P)
    t[:, C_ID:C_ID + P] = np.eye(P)
    t[:, C_UP:C_UP + P] = r[:, None] < r[None, :]
    t[:, C_MQ:C_MQ + P] = np.where(r[None, :] > r[:, None], BIG, 0)
    t[:, C_MK:C_MK + P] = np.where(r[:, None] > r[None, :], BIG, 0)
    t[:, C_ONE:C_ONE + P] = 1
    t[:, C_K128:C_K128 + 64] = 128 * np.arange(64)
    t[:, C_SLOT:C_SLOT + 80] = np.arange(80)
    t[:, C_PICK:C_PICK + NE] = NE - np.arange(NE)
    return t


def rotary_tables():
    inv = np.float32(1.0) / np.float32(10000.0) ** (np.arange(0, DH, 2, dtype=np.float32) / np.float32(DH))
    f = np.arange(S, dtype=np.float32)[:, None] * inv[None, :].astype(np.float32)
    lay = lambda a: np.ascontiguousarray(a.reshape(TS, P, DH // 2).transpose(1, 0, 2).reshape(P, -1))
    return lay(np.cos(f).astype(np.float32)), lay(np.sin(f).astype(np.float32))


class Core:

    def __init__(self, nc, stack):
        self.nc, self.stack, self.held = nc, stack, []

    def sb(self, name, shape, dt=F32, stack=None):
        return (stack or self.stack).enter_context(self.nc.sbuf_tensor(name, shape, dt))

    def ps(self, name, cols, dt=F32, stack=None):
        return (stack or self.stack).enter_context(self.nc.psum_tensor(name, [P, cols], dt))

    def sem(self, name):
        return self.stack.enter_context(self.nc.semaphore(name))

    def phase_sem(self, name):
        self.held.append(self.nc.alloc_semaphore(name))
        return self.held[-1]

    def end_phase(self):
        self.nc.clear_and_free_semaphores(self.held)
        self.held = []
        self.nc.all_engine_barrier()

    def dram(self, name, shape, dt=F32):
        return self.nc.dram_tensor(name, shape, dt).ap()


def bc(ap, axis, n):
    ap = ap.unsqueeze(axis)
    shape = list(ap.shape)
    shape[axis] = n
    return ap.to_broadcast(shape)


def load_constants(core, T):
    nc = core.nc
    T.cst = core.sb("cst", [P, C_COLS])
    T.idb = core.sb("idb", [P, P], BF16)
    T.mqb = core.sb("mqb", [P, P], BF16)
    T.mkb = core.sb("mkb", [P, P], BF16)
    T.zero = core.sb("zero", [P, D])
    T.idf = T.cst[:, C_ID:C_ID + P]
    cst_in = core.sem("cst_in")
    zero_done = core.sem("zero_done")
    with nc.Block() as block:
        @block.sync
        def _(sp):
            sp.dma_start(T.cst[:, :], T.cst_dram).then_inc(cst_in, 16)

        @block.gpsimd
        def _(pool):
            pool.memset(T.zero[:, :], 0.0).then_inc(zero_done, 1)

        @block.vector
        def _(dve):
            dve.wait_ge(cst_in, 16)
            dve.tensor_copy(T.idb[:, :], T.idf)
            dve.tensor_copy(T.mqb[:, :], T.cst[:, C_MQ:C_MQ + P])
            dve.tensor_copy(T.mkb[:, :], T.cst[:, C_MK:C_MK + P])


def merge_stats(dve, bs, mean, dif, var, merged, call):
    dve.tensor_tensor(mean, bs[:, :, 1], bs[:, :, 4], ALU.add).then_inc(merged, 1)
    dve.tensor_tensor(dif, bs[:, :, 1], bs[:, :, 4], ALU.subtract).then_inc(merged, 1)
    dve.tensor_tensor(var, bs[:, :, 2], bs[:, :, 5], ALU.add).then_inc(merged, 1)
    dve.wait_ge(merged, 6 * call + 3)
    dve.tensor_scalar(mean, mean, 0.5, None, ALU.mult).then_inc(merged, 1)
    dve.tensor_tensor(dif, dif, dif, ALU.mult).then_inc(merged, 1)
    dve.tensor_scalar(var, var, 1.0 / D, EPS, ALU.mult, ALU.add).then_inc(merged, 1)
    dve.wait_ge(merged, 6 * call + 6)
    return dve.scalar_tensor_tensor(var, dif, 0.25, var, ALU.mult, ALU.add)


def norm_project(core, T, L, x_dram, w_dram, X):
    nc = core.nc
    W3 = 3 * D
    NQ = 4
    TQ = NT // NQ
    NPAIR = NT // 2
    with ExitStack() as st:
        sb = lambda n, s, d=F32: core.sb(f"a{L}_{n}", s, d, st)
        ps = lambda n, c, d=F32: core.ps(f"a{L}_{n}", c, d, st)
        sem = lambda n: core.phase_sem(f"a{L}_{n}")
        w = sb("w", [P, KD, W3])
        cent = sb("cent", [P, KD, NE])
        bs = [sb(f"bs{k}", [P, NT, 6]) for k in range(2)]
        mean = [sb(f"mean{k}", [P, NT]) for k in range(2)]
        dif = [sb(f"dif{k}", [P, NT]) for k in range(2)]
        var = [sb(f"var{k}", [P, NT]) for k in range(2)]
        std = [sb(f"std{k}", [P, NT]) for k in range(2)]
        rstd = [sb(f"rstd{k}", [P, NT]) for k in range(2)]
        xs = [sb(f"xs{u}", [P, D]) for u in range(4)]
        xT = [sb(f"xT{u}", [P, D]) for u in range(4)]
        qs = [sb(f"qs{u}", [P, W3]) for u in range(2)]
        psT = [ps(f"psT{u}", 512) for u in range(2)]
        psQ = [ps(f"psQ{u}", 1024) for u in range(2)]
        x_in = [sem(f"x_in{q}") for q in range(NQ)]
        w_in = sem("w_in")
        stat = sem("stat")
        merged = sem("merged")
        var_ok = [sem(f"var_ok{k}") for k in range(2)]
        std_ok = [sem(f"std_ok{k}") for k in range(2)]
        rstd_ok = [sem(f"rstd_ok{k}") for k in range(2)]
        xn_ready = sem("xn_ready")
        xn_kept = sem("xn_kept")
        transposed = sem("transposed")
        xT_ready = sem("xT_ready")
        projected = sem("projected")
        left_act = sem("left_act")
        left_dve = sem("left_dve")
        out = [sem(f"out{u}") for u in range(2)]
        xn_out = sem("xn_out")
        passed = sem("passed")
        X2 = X[:, :, :].rearrange("p t d -> p (t d)")
        aff2 = T.aff[:, :, :].rearrange("p t e -> p (t e)")
        xd = x_dram.rearrange("(t p) d -> p t d", p=P)
        if L:
            bias = sb("bias", [P, W3])
            cosT = sb("cos", [P, TS * DH // 2])
            sinT = sb("sin", [P, TS * DH // 2])
            qo = [sb(f"qo{u}", [P, NG, 2 * GW]) for u in range(2)]
            dm = [sb(f"dm{u}", [P, 2, NG * 2 * HG * DH // 2]) for u in range(2)]
            pm = [sb(f"pm{u}", [P, 2, NG * 2 * HG * DH // 2]) for u in range(2)]
            sq = [sb(f"sq{u}", [P, D]) for u in range(2)]
            nf2 = T.nf[:, :, :].rearrange("p t d -> p (t d)")
            tab_in = sem("tab_in")
            biased = sem("biased")
            dve_mul = sem("dve_mul")
            pool_mul = sem("pool_mul")
            turned_even = sem("turned_even")
            turned_odd = sem("turned_odd")
            outq = [sem(f"outq{u}") for u in range(2)]
            cast = sem("cast")
            squared = sem("squared")

        def pairs(eng, lo, hi, body):
            with eng.Fori(0, (hi - lo) // 2) as j:
                for v in range(2):
                    body(2 * j + (lo + v), v)

        def pipelined(eng, far, ahead, behind, upcoming, over):
            upcoming(0)
            for p in range(far):
                ahead(p, p, 0)
            for q in range(NQ):
                lo, hi = NPAIR // NQ * q, NPAIR // NQ * (q + 1)

                def body(p, v):
                    ahead(p + far, (v + far) % 2, q)
                    behind(p, v, q)

                pairs(eng, lo, hi - 2, body)
                if q + 1 < NQ:
                    upcoming(q + 1)
                for p in (hi - 2, hi - 1):
                    if p + far < NPAIR:
                        ahead(p + far, (p + far) % 2, (p + far) * NQ // NPAIR)
                    behind(p, p % 2, q)
                over(q)

        with nc.Block() as block:
            @block.sync
            def _(sp):
                for q in range(NQ):
                    sp.dma_start(X[:, TQ * q:TQ * q + TQ, :], xd[:, TQ * q:TQ * q + TQ, :])\
                        .then_inc(x_in[q], 16)
                    if q == 0:
                        sp.dma_start(w[:, :, :], w_dram.rearrange("(k p) n -> p k n", p=P)).then_inc(w_in, 16)
                        if L == 0:
                            sp.dma_start(cent[:, :, :],
                                         T.cent_dram.rearrange("(k p) n -> p k n", p=P)).then_inc(w_in, 16)
                        else:
                            sp.dma_start(bias[:, :], T.bqkv_dram.partition_broadcast(P)).then_inc(tab_in, 16)
                            sp.dma_start(cosT[:, :], T.cos_dram).then_inc(tab_in, 16)
                            sp.dma_start(sinT[:, :], T.sin_dram).then_inc(tab_in, 16)
                sp.sem_inc(out[0], 16)
                sp.sem_inc(out[1], 16)
                if L:
                    sp.sem_inc(outq[0], 16)
                    sp.sem_inc(outq[1], 16)
                for q in range(NQ):
                    b = q * NB // NQ

                    def store(p, v):
                        for u in range(2):
                            n = 2 * p + u
                            dst = T.qkv.rearrange("(g b) p t c -> b p g t c", b=NB)[b][
                                :, :, bass.ds(n - b * TS, 1), :]
                            src = qs[u][:, :].rearrange("p (g t c) -> p g t c", g=NG, t=1)
                            if L == 0:
                                sp.wait_ge(left_act, n + 3)
                                sp.wait_ge(left_dve, n + 3)
                                sp.dma_start(dst, src).then_inc(out[u], 16)
                            else:
                                sp.wait_ge(biased, n + 3)
                                sp.dma_start(dst[:, :, :, 2 * GW:3 * GW],
                                             src[:, :, :, 2 * GW:3 * GW]).then_inc(out[u], 16)
                                sp.wait_ge(turned_even, n + 1)
                                sp.sem_inc(passed, 1)
                                sp.wait_ge(turned_odd, n + 3)
                                sp.sem_inc(passed, 1)
                                sp.dma_start(dst[:, :, :, 0:2 * GW],
                                             qo[u][:, :, :].rearrange("p g (t c) -> p g t c", t=1))\
                                    .then_inc(outq[u], 16)

                    pairs(sp, NPAIR // NQ * q, NPAIR // NQ * (q + 1), store)
                    sp.wait_ge(xn_kept, TQ * (q + 1))
                    sp.dma_start(T.xn_dram.rearrange("(t p) d -> p t d", p=P)[:, TQ * q:TQ * q + TQ, :],
                                 X[:, TQ * q:TQ * q + TQ, :]).then_inc(xn_out, 16)
                for u in range(2):
                    sp.wait_ge(out[u], 16 * (NT // 2 + 1))
                    if L:
                        sp.wait_ge(outq[u], 16 * (NT // 2 + 1))
                sp.wait_ge(xn_out, 16 * NQ)

            @block.vector
            def _(dve):
                dve.sem_inc(biased if L else left_dve, 2)
                quarter = lambda t, q: t[:, TQ * q:TQ * q + TQ]
                calls = [0]

                def rows(k, q):
                    merge_stats(dve, quarter(bs[k], q), quarter(mean[k], q), quarter(dif[k], q),
                                quarter(var[k], q), merged, calls[0]).then_inc(var_ok[k], 1)
                    calls[0] += 1

                def invert(k, q):
                    dve.wait_ge(std_ok[k], q + 1)
                    dve.reciprocal(quarter(rstd[k], q), quarter(std[k], q)).then_inc(rstd_ok[k], 1)
                    dve.wait_ge(rstd_ok[k], q + 1)

                def upcoming(q):
                    if q == 0:
                        dve.wait_ge(x_in[0], 16)
                        for t in range(TQ):
                            dve.bn_stats(bs[0][:, t, :], X[:, t, :]).then_inc(stat, 1)
                    dve.wait_ge(stat, TQ * (q + 1))
                    rows(0, q)
                    invert(0, q)
                    if q + 1 < NQ:
                        dve.wait_ge(x_in[q + 1], 16)

                def second_norm(q):
                    invert(1, q)
                    dve.wait_ge(xn_out, 16 * (q + 1))
                    for t in range(TQ * q, TQ * q + TQ):
                        dve.tensor_scalar(X[:, t, :], X[:, t, :], mean[1][:, t:t + 1], rstd[1][:, t:t + 1],
                                          ALU.subtract, ALU.mult)

                def over(q):
                    if L == 0:
                        rows(1, q)
                        if q:
                            second_norm(q - 1)
                        if q == NQ - 1:
                            second_norm(q)

                def norm(p, v, q):
                    for u in range(2):
                        n = 2 * p + u
                        if q + 1 < NQ:
                            dve.bn_stats(bs[0][:, :, :].rearrange("p t s -> p (t s)")[
                                :, bass.ds((n + TQ) * 6, 6)], X2[:, bass.ds((n + TQ) * D, D)]).then_inc(stat, 1)
                        dve.wait_ge(transposed, n + 1)
                        x_t = X2[:, bass.ds(n * D, D)]
                        mu, rs = mean[0][:, bass.ds(n, 1)], rstd[0][:, bass.ds(n, 1)]
                        dve.tensor_scalar(xs[2 * v + u][:, :], x_t, mu, rs, ALU.subtract, ALU.mult)\
                            .then_inc(xn_ready, 1)
                        dve.tensor_scalar(x_t, x_t, mu, rs, ALU.subtract, ALU.mult).then_inc(xn_kept, 1)
                        if L == 0:
                            dve.wait_ge(xn_ready, n + 1)
                            dve.sem_inc(passed, 1)
                            dve.bn_stats(bs[1][:, :, :].rearrange("p t s -> p (t s)")[:, bass.ds(n * 6, 6)],
                                         xs[2 * v + u][:, :])

                def leave(p, v, q):
                    for u in range(2):
                        n = 2 * p + u
                        dve.wait_ge(projected, n + 5)
                        dve.wait_ge(out[u], 16 * p + 16)
                        if L == 0:
                            dve.tensor_copy(qs[u][:, 512:W3], psQ[u][:, 512:W3])
                            dve.tensor_copy(aff2[:, bass.ds(n * NE, NE)],
                                            psQ[u][:, W3:W3 + NE]).then_inc(left_dve, 1)
                            continue
                        dve.wait_ge(turned_odd, n + 1)
                        dve.tensor_tensor(qs[u][:, :], psQ[u][:, 0:W3], bias[:, :], ALU.add)\
                            .then_inc(biased, 1)
                        dve.wait_ge(biased, n + 3)
                        dve.wait_ge(outq[u], 16 * p + 16)
                        qk = qs[u][:, :].rearrange("p (g c) -> p g c", g=NG)[:, :, 0:2 * GW]\
                            .rearrange("p g (h f z) -> p g h f z", f=DH // 2, z=2)
                        o = qo[u][:, :, :].rearrange("p g (h f z) -> p g h f z", f=DH // 2, z=2)
                        t = n - q * NB // NQ * TS
                        tab = lambda t_: t_[:, bass.ds(t * (DH // 2), DH // 2)]
                        m = dm[u][:, :, :].rearrange("p a (g h f) -> p a g h f", g=NG, f=DH // 2)
                        cs = bc(bc(tab(cosT), 1, 2 * HG), 1, NG)
                        sn = bc(bc(tab(sinT), 1, 2 * HG), 1, NG)
                        dve.tensor_tensor(m[:, 0], qk[:, :, :, :, 0], cs, ALU.mult)
                        dve.tensor_tensor(m[:, 1], qk[:, :, :, :, 1], sn, ALU.mult).then_inc(dve_mul, 1)
                        dve.wait_ge(dve_mul, n + 1)
                        dve.tensor_tensor(o[:, :, :, :, 0], m[:, 0], m[:, 1], ALU.subtract)\
                            .then_inc(turned_even, 1)

                if L:
                    dve.wait_ge(tab_in, 48)
                pipelined(dve, 2, norm, leave, upcoming, over)

            if L == 0:
                @block.gpsimd
                def _(pool):
                    for e in range(NE):
                        pool.wait_ge(xn_kept, NT // NE * e + 2)
                        pool.dma_start(T.w1[:, e, :, :], T.w1_dram[e].rearrange("(k p) f -> p k f", p=P))\
                            .then_inc(T.w1_in, 16)
                        pool.dma_start(T.w2[:, e, :, :], T.w2_dram[e].rearrange("(k p) d -> p k d", p=P))\
                            .then_inc(T.w2_in, 16)
                        lo, hi = (SLOT0 + 2) * e // NE, (SLOT0 + 2) * (e + 1) // NE
                        pool.dma_start(T.sorted_dram[0].rearrange("(s p) d -> p s d", p=P)[:, lo:hi, :],
                                       bc(T.zero[:, :], 1, hi - lo)).then_inc(T.cleared[0], 16)
            else:
                @block.gpsimd
                def _(pool):
                    pool.sem_inc(turned_odd, 2)
                    pool.wait_ge(tab_in, 48)
                    for b in range(NB):
                        with pool.Fori(0, TS // 2) as i:
                            for u in range(2):
                                n = b * TS + 2 * i + u
                                pool.wait_ge(biased, n + 3)
                                pool.wait_ge(outq[u], 16 * (b * TS // 2 + i) + 16)
                                qk = qs[u][:, :].rearrange("p (g c) -> p g c", g=NG)[:, :, 0:2 * GW]\
                                    .rearrange("p g (h f z) -> p g h f z", f=DH // 2, z=2)
                                o = qo[u][:, :, :].rearrange("p g (h f z) -> p g h f z", f=DH // 2, z=2)
                                tab = lambda t_: t_[:, bass.ds((2 * i + u) * (DH // 2), DH // 2)]
                                m = pm[u][:, :, :].rearrange("p a (g h f) -> p a g h f", g=NG, f=DH // 2)
                                cs = bc(bc(tab(cosT), 1, 2 * HG), 1, NG)
                                sn = bc(bc(tab(sinT), 1, 2 * HG), 1, NG)
                                pool.tensor_tensor(m[:, 0], qk[:, :, :, :, 0], sn, ALU.mult)\
                                    .then_inc(pool_mul, 1)
                                pool.tensor_tensor(m[:, 1], qk[:, :, :, :, 1], cs, ALU.mult)\
                                    .then_inc(pool_mul, 1)
                                pool.wait_ge(pool_mul, 2 * n + 2)
                                pool.tensor_tensor(o[:, :, :, :, 1], m[:, 0], m[:, 1], ALU.add)\
                                    .then_inc(turned_odd, 1)

            @block.scalar
            def _(act):
                act.sem_inc(xT_ready, 2)
                act.sem_inc(squared if L else left_act, 2)

                def root(k, q):
                    act.wait_ge(var_ok[k], q + 1)
                    act.activation(std[k][:, TQ * q:TQ * q + TQ], var[k][:, TQ * q:TQ * q + TQ], ACT.Sqrt)\
                        .then_inc(std_ok[k], 1)

                def over(q):
                    if L == 0:
                        root(1, q)

                def copy_x(p, v, q):
                    for u in range(2):
                        n = 2 * p + u
                        act.wait_ge(transposed, n + 5)
                        act.wait_ge(projected, n + 1)
                        act.copy(xT[2 * v + u][:, :], psT[u][:, 0:D]).then_inc(xT_ready, 1)

                def leave(p, v, q):
                    for u in range(2):
                        n = 2 * p + u
                        if L == 0:
                            act.wait_ge(projected, n + 5)
                            act.wait_ge(out[u], 16 * p + 16)
                            act.copy(qs[u][:, 0:512], psQ[u][:, 0:512]).then_inc(left_act, 1)
                        else:
                            act.wait_ge(xn_kept, n + 1)
                            act.activation(nf2[:, bass.ds(n * D, D)], X2[:, bass.ds(n * D, D)],
                                           ACT.Copy).then_inc(cast, 1)
                            act.wait_ge(cast, n + 1)
                            act.wait_ge(squared, n + 1)
                            act.activation(sq[u][:, :], nf2[:, bass.ds(n * D, D)], ACT.Square,
                                           accum_out=T.ss[:, bass.ds(n, 1)]).then_inc(squared, 1)

                pipelined(act, 1, copy_x, leave, lambda q: root(0, q), over)

            @block.tensor
            def _(pe):
                pe.sem_inc(transposed, 4)
                pe.sem_inc(projected, 4)

                def turn(p, v, q):
                    for u in range(2):
                        n = 2 * p + u
                        pe.wait_ge(xn_ready, n + 1)
                        pe.wait_ge(xT_ready, n + 1)
                        for k in range(KD):
                            t = pe.transpose(psT[u][:, k * P:k * P + P], xs[2 * v + u][:, k * P:k * P + P],
                                             T.idf)
                        t.then_inc(transposed, 1)

                def project(p, v, q):
                    for u in range(2):
                        n = 2 * p + u
                        pe.wait_ge(xT_ready, n + 3)
                        if L == 0:
                            pe.wait_ge(left_act, n + 1)
                            pe.wait_ge(left_dve, n + 1)
                        else:
                            pe.wait_ge(biased, n + 1)
                        lhs = xT[2 * v + u]
                        for a, z in ((0, 512), (512, W3)):
                            for k in range(KD):
                                m = pe.matmul(psQ[u][:, a:z], lhs[:, k * P:k * P + P], w[:, k, a:z],
                                              start=(k == 0), stop=(k == KD - 1))
                        if L == 0:
                            for k in range(KD):
                                m = pe.matmul(psQ[u][:, W3:W3 + NE], lhs[:, k * P:k * P + P],
                                              cent[:, k, :], start=(k == 0), stop=(k == KD - 1))
                        m.then_inc(projected, 1)

                pe.wait_ge(w_in, 16 if L else 32)
                pipelined(pe, 1, turn, project, lambda q: None, lambda q: None)
        core.end_phase()


def scores_of_layer1(core, T):
    nc = core.nc
    G = 4
    NGR = NT // G
    with ExitStack() as st:
        sb = lambda n, s, d=F32: core.sb(f"r_{n}", s, d, st)
        ps = lambda n, c, d=F32: core.ps(f"r_{n}", c, d, st)
        sem = lambda n: core.phase_sem(f"r_{n}")
        nw = sb("nw", [P, D])
        gw = sb("gw", [P, KD, NE], BF16)
        gb = sb("gb", [P, NE], BF16)
        ms = sb("ms", [P, NT])
        std = sb("std", [P, NT])
        rstd = sb("rstd", [P, NT])
        nT = [sb(f"nT{u}", [P, G * D], BF16) for u in range(2)]
        lg = sb("lg", [P, NT, NE], BF16)
        psT = [ps(f"psT{u}", G * D, BF16) for u in range(2)]
        psL = [ps(f"psL{u}", 512) for u in range(2)]
        tab_in = sem("tab_in")
        mean_ok = sem("mean_ok")
        std_ok = sem("std_ok")
        rstd_ok = sem("rstd_ok")
        normed = sem("normed")
        transposed = sem("transposed")
        copied = sem("copied")
        scored = sem("scored")
        left = sem("left")
        with nc.Block() as block:
            @block.sync
            def _(sp):
                sp.dma_start(nw[:, :], T.nw_dram.partition_broadcast(P)).then_inc(tab_in, 16)
                sp.dma_start(gw[:, :, :], T.gw_dram.rearrange("(k p) n -> p k n", p=P)).then_inc(tab_in, 16)
                sp.dma_start(gb[:, :], T.gb_dram.partition_broadcast(P)).then_inc(tab_in, 16)

            @block.vector
            def _(dve):
                dve.sem_inc(left, 2)
                dve.tensor_scalar(ms[:, :], T.ss[:, :], 1.0 / D, EPS, ALU.mult, ALU.add).then_inc(mean_ok, 1)
                dve.wait_ge(std_ok, 1)
                dve.reciprocal(rstd[:, :], std[:, :]).then_inc(rstd_ok, 1)
                dve.wait_ge(rstd_ok, 1)
                dve.wait_ge(tab_in, 48)
                for g in range(NGR + 2):
                    for t in range(G * g, G * g + G) if g < NGR else ():
                        dve.scalar_tensor_tensor(T.nf[:, t, :], T.nf[:, t, :], rstd[:, t:t + 1], nw[:, :],
                                                 ALU.mult, ALU.mult).then_inc(normed, 1)
                    if g >= 2:
                        dve.wait_ge(scored, g + 1)
                        dve.tensor_tensor(lg[:, G * (g - 2):G * (g - 1), :],
                                          psL[g % 2][:, 0:G * NE].rearrange("p (t e) -> p t e", e=NE),
                                          bc(gb[:, :], 1, G), ALU.add).then_inc(left, 1)
                dve.wait_ge(left, NGR + 2)
                dve.tensor_copy(T.aff[:, :, :], lg[:, :, :])

            @block.scalar
            def _(act):
                act.sem_inc(copied, 2)
                act.wait_ge(mean_ok, 1)
                act.activation(std[:, :], ms[:, :], ACT.Sqrt).then_inc(std_ok, 1)
                for g in range(NGR):
                    act.wait_ge(transposed, g + 1)
                    act.wait_ge(scored, g + 1)
                    act.copy(nT[g % 2][:, :], psT[g % 2][:, :]).then_inc(copied, 1)

            @block.tensor
            def _(pe):
                pe.sem_inc(scored, 2)
                pe.wait_ge(tab_in, 48)
                for g in range(NGR + 1):
                    if g < NGR:
                        pe.wait_ge(normed, G * g + G)
                        pe.wait_ge(copied, g + 1)
                        for t in range(G):
                            for k in range(KD):
                                c = (t * KD + k) * P
                                x = pe.transpose(psT[g % 2][:, c:c + P], T.nf[:, G * g + t, k * P:k * P + P],
                                                 T.idb[:, :])
                        x.then_inc(transposed, 1)
                    if g:
                        pe.wait_ge(copied, g + 2)
                        pe.wait_ge(left, g)
                        for t in range(G):
                            for k in range(KD):
                                c = (t * KD + k) * P
                                m = pe.matmul(psL[(g - 1) % 2][:, t * NE:t * NE + NE], nT[(g - 1) % 2][:, c:c + P],
                                              gw[:, k, :], start=(k == 0), stop=(k == KD - 1))
                        m.then_inc(scored, 1)
        core.end_phase()


def route(core, T, L):
    nc = core.nc
    NCH = L + 1
    NV = NCH * NT
    NS = (SLOT1 if L else SLOT0) + 2
    with ExitStack() as st:
        sb = lambda n, s, d=F32: core.sb(f"t{L}_{n}", s, d, st)
        ps = lambda n, c, d=F32: core.ps(f"t{L}_{n}", c, d, st)
        sem = lambda n: core.phase_sem(f"t{L}_{n}")
        aff = sb("aff", [P, NT, NE])
        mx = sb("mx", [P, NCH, NT])
        eq = sb("eq", [P, NT, NE])
        pk = sb("pk", [P, NT])
        oh = sb("oh", [P, NV, NE])
        tot = sb("tot", [P, NV, NE])
        run = [sb(f"run{i}", [P, NV, NE]) for i in range(2)]
        over = sb("over", [P, NE, NV])
        nt_e = sb("nt_e", [P, NE])
        cum = [sb(f"cum{i}", [P, NE]) for i in range(2)]
        base = sb("base", [P, NE])
        past = sb("past", [P, NS, NE])
        eidf = sb("eidf", [P, NS])
        where = sb("where", [P, NV, NE])
        posf = sb("posf", [P, NV])
        ex = sb("ex", [P, 3, NT])
        psR = ps("psR", 512)
        psS = ps("psS", 512)
        step = sem("step")
        onehot = sem("onehot")
        ranked = sem("ranked")
        differ = sem("differ")
        expd = sem("expd")
        placed = sem("placed")
        scattered = sem("scattered")
        k128 = T.cst[:, C_K128:C_K128 + NV]
        slot = T.cst[:, C_SLOT:C_SLOT + NS]
        pick = T.cst[:, C_PICK:C_PICK + NE]
        with nc.Block() as block:
            @block.vector
            def _(dve):
                done = [0]

                def then(ins):
                    done[0] += 1
                    ins.then_inc(step, 1)
                    dve.wait_ge(step, done[0])

                then(dve.tensor_copy(aff[:, :, :], T.aff[:, :, :]))
                for c in range(NCH):
                    ohc = oh[:, c * NT:(c + 1) * NT, :]
                    then(dve.tensor_reduce(mx[:, c, :], aff[:, :, :], AX.X, ALU.max))
                    then(dve.tensor_tensor(eq[:, :, :], aff[:, :, :], bc(mx[:, c, :], 2, NE), ALU.is_ge))
                    then(dve.tensor_tensor(eq[:, :, :], eq[:, :, :], bc(pick, 1, NT), ALU.mult))
                    then(dve.tensor_reduce(pk[:, :], eq[:, :, :], AX.X, ALU.max))
                    then(dve.tensor_tensor(ohc, bc(pk[:, :], 2, NE), bc(pick, 1, NT), ALU.is_equal))
                    if c + 1 < NCH:
                        then(dve.scalar_tensor_tensor(aff[:, :, :], ohc, BIG, aff[:, :, :],
                                                      ALU.mult, ALU.add))
                dve.sem_inc(onehot, 1)
                dve.wait_ge(ranked, 1)
                then(dve.tensor_copy(tot[:, :, :].rearrange("p t e -> p (t e)"), psS[:, 0:NV * NE]))
                src, sh, k = tot, 1, 0
                while sh < NV:
                    dst = run[k % 2]
                    dve.tensor_copy(dst[:, 0:sh, :], src[:, 0:sh, :])
                    then(dve.tensor_tensor(dst[:, sh:NV, :], src[:, sh:NV, :], src[:, 0:NV - sh, :], ALU.add))
                    src, sh, k = dst, 2 * sh, k + 1
                count = src[:, NV - 1, :]
                then(dve.tensor_tensor(over[:, :, :], bc(count, 2, NV), bc(k128, 1, NE), ALU.is_gt))
                then(dve.tensor_reduce(nt_e[:, :], over[:, :, :], AX.X, ALU.add))
                prev, sh, j = nt_e, 1, 0
                while sh < NE:
                    dst = cum[j % 2]
                    dve.tensor_copy(dst[:, 0:sh], prev[:, 0:sh])
                    then(dve.tensor_tensor(dst[:, sh:NE], prev[:, sh:NE], prev[:, 0:NE - sh], ALU.add))
                    prev, sh, j = dst, 2 * sh, j + 1
                then(dve.tensor_tensor(base[:, :], prev[:, :], nt_e[:, :], ALU.subtract))
                then(dve.tensor_scalar(base[:, :], base[:, :], float(P), None, ALU.mult))
                then(dve.tensor_tensor(past[:, :, :], bc(slot, 2, NE), bc(prev[:, :], 1, NS), ALU.is_ge))
                then(dve.tensor_reduce(eidf[:, :], past[:, :, :], AX.X, ALU.add))
                then(dve.tensor_scalar(eidf[:, :], eidf[:, :], float(NE - 1), None, ALU.min))
                dve.tensor_copy(T.eid[:, 0:NS], eidf[:, :])
                then(dve.tensor_tensor(where[:, :, :], src[:, :, :], tot[:, :, :], ALU.subtract))
                then(dve.tensor_tensor(where[:, :, :], where[:, :, :], bc(base[:, :], 1, NV), ALU.add))
                then(dve.tensor_tensor(where[:, :, :].rearrange("p t e -> p (t e)"),
                                       where[:, :, :].rearrange("p t e -> p (t e)"),
                                       psR[:, 0:NV * NE], ALU.add))
                then(dve.tensor_tensor(where[:, :, :], where[:, :, :], oh[:, :, :], ALU.mult))
                then(dve.tensor_reduce(posf[:, :], where[:, :, :], AX.X, ALU.add))
                dve.tensor_copy(T.pos[:, 0:NV], posf[:, :]).then_inc(placed, 1)
                if L == 0:
                    dve.tensor_copy(T.top[:, 0, :], mx[:, 0, :])
                else:
                    dve.tensor_tensor(ex[:, 0, :], mx[:, 1, :], mx[:, 0, :], ALU.subtract).then_inc(differ, 1)
                    dve.wait_ge(expd, 1)
                    then(dve.tensor_scalar(ex[:, 2, :], ex[:, 1, :], 1.0, None, ALU.add))
                    then(dve.reciprocal(T.top[:, 0, :], ex[:, 2, :]))
                    then(dve.tensor_tensor(T.top[:, 1, :], ex[:, 1, :], T.top[:, 0, :], ALU.mult))

            @block.scalar
            def _(act):
                if L:
                    act.wait_ge(differ, 1)
                    act.activation(ex[:, 1, :], ex[:, 0, :], ACT.Exp).then_inc(expd, 1)

            @block.tensor
            def _(pe):
                pe.wait_ge(onehot, 1)
                flat = oh[:, :, :].rearrange("p t e -> p (t e)")
                pe.matmul(psR[:, 0:NV * NE], T.cst[:, C_UP:C_UP + P], flat, start=True, stop=True)
                pe.matmul(psS[:, 0:NV * NE], T.cst[:, C_ONE:C_ONE + P], flat, start=True, stop=True)\
                    .then_inc(ranked, 1)

            if L == 0:
                @block.gpsimd
                def _(pool):
                    pool.wait_ge(placed, 1)
                    scatter(T, L, pool, scattered)
                    pool.wait_ge(scattered, 16 * NV)
        core.end_phase()


def scatter(T, L, pool, scattered):
    pool.wait_ge(T.cleared[L], 16 if L else 16 * NE)
    for v in range((L + 1) * NT):
        rows = T.nf[:, v % NT, :] if L else T.X[:, v, :]
        pool.indirect_dma_start(
            out=T.sorted_dram[L], out_offset=bass.IndirectOffsetOnAxis(ap=T.pos[:, v:v + 1], axis=0),
            in_=rows, in_offset=None).then_inc(scattered, 16)


def experts0(core, T):
    nc = core.nc
    with ExitStack() as st:
        sb = lambda n, s, d=F32: core.sb(f"e0_{n}", s, d, st)
        ps = lambda n, c, d=F32: core.ps(f"e0_{n}", c, d, st)
        sem = lambda n: core.phase_sem(f"e0_{n}")
        FC = F0 // P
        b1 = sb("b1", [P, NE * F0])
        b2 = sb("b2", [P, NE * D])
        gb = sb("gb", [P, NE, 2, KD])
        xs = [sb(f"xs{u}", [P, D]) for u in range(2)]
        xT = [sb(f"xT{u}", [P, KD, P]) for u in range(2)]
        h = sb("h", [P, F0])
        hT = sb("hT", [P, F0])
        y = [sb(f"y{u}", [P, D]) for u in range(2)]
        psT = ps("psT", 512)
        psH = ps("psH", 1024)
        psG = ps("psG", 1024)
        psY = ps("psY", 512)
        tab_in = sem("tab_in")
        gb_in = sem("gb_in")
        x_in = [sem(f"x_in{u}") for u in range(2)]
        y_out = [sem(f"y_out{u}") for u in range(2)]
        x_turned = sem("x_turned")
        xT_ready = sem("xT_ready")
        hidden = sem("hidden")
        h_ready = sem("h_ready")
        h_turned = sem("h_turned")
        hT_ready = sem("hT_ready")
        result = sem("result")
        y_ready = sem("y_ready")
        w1f = T.w1[:, :, :, :].rearrange("p e k f -> p (e k f)")
        w2f = T.w2[:, :, :, :].rearrange("p e k d -> p (e k d)")
        gbf = gb[:, :, :, :].rearrange("p e a k -> p (e a k)")
        xd = T.sorted_dram[0].rearrange("(s p) d -> s p d", p=P)
        yd = T.result_dram[0].rearrange("(s p) d -> s p d", p=P)
        NS = SLOT0
        with nc.Block() as block:
            @block.sync
            def _(sp):
                sp.dma_start(gb[:, :, :, :], T.gb0_dram.rearrange("p (e a k) -> p e a k", e=NE, a=2))\
                    .then_inc(gb_in, 16)
                for u in range(2):
                    sp.dma_start(xs[u][:, :], xd[u]).then_inc(x_in[u], 16)
                sp.dma_start(b1[:, :], T.b1_dram.partition_broadcast(P)).then_inc(tab_in, 16)
                sp.dma_start(b2[:, :], T.b2_dram.partition_broadcast(P)).then_inc(tab_in, 16)
                sp.sem_inc(y_out[0], 16)
                sp.sem_inc(y_out[1], 16)
                with sp.Fori(0, NS // 2) as i:
                    for u in range(2):
                        s = 2 * i + u
                        sp.wait_ge(x_turned, s + 3)
                        sp.dma_start(xs[u][:, :], xd[bass.ds(s + 2, 1)].rearrange("s p d -> (s p) d"))\
                            .then_inc(x_in[u], 16)
                        sp.wait_ge(y_ready, s + 2)
                        sp.dma_start(yd[bass.ds(s, 1)].rearrange("s p d -> (s p) d"), y[u][:, :])\
                            .then_inc(y_out[u], 16)
                for u in range(2):
                    sp.wait_ge(y_out[u], 16 * (NS // 2 + 1))
                    sp.wait_ge(x_in[u], 16 * (NS // 2 + 1))

            @block.vector
            def _(dve):
                dve.sem_inc(h_ready, 1)
                dve.sem_inc(y_ready, 1)
                dve.wait_ge(tab_in, 32)

                def bias1(s):
                    e = dve.value_load(T.eid[0:1, bass.ds(s, 1)], min_val=0, max_val=NE - 1)
                    dve.wait_ge(hidden, s + 3)
                    dve.wait_ge(h_turned, s + 1)
                    dve.tensor_tensor(h[:, :], psH[:, :], b1[:, bass.ds(e * F0, F0)], ALU.add)\
                        .then_inc(h_ready, 1)

                def bias2(s, u, k_out):
                    e = dve.value_load(T.eid[0:1, bass.ds(s, 1)], min_val=0, max_val=NE - 1)
                    dve.wait_ge(result, s + 2)
                    dve.wait_ge(y_out[u], k_out)
                    dve.tensor_tensor(y[u][:, :], psY[:, 0:D], b2[:, bass.ds(e * D, D)], ALU.add)\
                        .then_inc(y_ready, 1)

                bias1(0)
                with dve.Fori(0, NS // 2) as i:
                    for u in range(2):
                        s = 2 * i + u
                        bias1(s + 1)
                        bias2(s, u, 16 * i + 16)

            @block.scalar
            def _(act):
                act.sem_inc(xT_ready, 1)
                act.sem_inc(hT_ready, 1)
                act.wait_ge(gb_in, 16)

                def affine(u, s):
                    e = act.value_load(T.eid[0:1, bass.ds(s, 1)], min_val=0, max_val=NE - 1)
                    act.wait_ge(x_turned, s + 3)
                    act.wait_ge(hidden, s + 1)
                    for k in range(KD):
                        a = act.activation(xT[u][:, k, :], psT[:, k * P:k * P + P], ACT.Identity,
                                           scale=gbf[:, bass.ds(e * 4 + k, 1)],
                                           bias=gbf[:, bass.ds(e * 4 + 2 + k, 1)])
                    a.then_inc(xT_ready, 1)

                affine(0, 0)
                affine(1, 1)
                with act.Fori(0, NS // 2) as i:
                    for u in range(2):
                        s = 2 * i + u
                        act.wait_ge(h_turned, s + 2)
                        act.wait_ge(result, s + 1)
                        for a in range(2):
                            r = act.activation(hT[:, a * 512:a * 512 + 512], psG[:, a * 512:a * 512 + 512],
                                               ACT.Relu)
                        r.then_inc(hT_ready, 1)
                        affine(u, s + 2)

            @block.tensor
            def _(pe):
                pe.sem_inc(x_turned, 2)
                pe.sem_inc(hidden, 2)
                pe.sem_inc(h_turned, 1)
                pe.sem_inc(result, 1)
                pe.wait_ge(T.w1_in, 16 * NE)
                pe.wait_ge(T.w2_in, 16 * NE)

                def turn_x(u, s, loads):
                    pe.wait_ge(x_in[u], 16 * loads)
                    pe.wait_ge(xT_ready, s + 1)
                    for k in range(KD):
                        t = pe.transpose(psT[:, k * P:k * P + P], xs[u][:, k * P:k * P + P], T.idf)
                    t.then_inc(x_turned, 1)

                def layer1(u, s):
                    e = pe.value_load(T.eid[0:1, bass.ds(s, 1)], min_val=0, max_val=NE - 1)
                    pe.wait_ge(xT_ready, s + 2)
                    pe.wait_ge(h_ready, s + 1)
                    for n in range(2):
                        for k in range(KD):
                            m = pe.matmul(psH[:, n * 512:n * 512 + 512], xT[u][:, k, :],
                                          w1f[:, bass.ds(e * (KD * F0) + k * F0 + n * 512, 512)],
                                          start=(k == 0), stop=(k == KD - 1))
                    m.then_inc(hidden, 1)

                turn_x(0, 0, 1)
                turn_x(1, 1, 1)
                layer1(0, 0)
                with pe.Fori(0, NS // 2) as i:
                    for u in range(2):
                        s = 2 * i + u
                        pe.wait_ge(h_ready, s + 2)
                        pe.wait_ge(hT_ready, s + 1)
                        for f in range(FC):
                            t = pe.transpose(psG[:, f * P:f * P + P], h[:, f * P:f * P + P], T.idf)
                        t.then_inc(h_turned, 1)
                        layer1(1 - u, s + 1)
                        turn_x(u, s + 2, i + 2)
                        e = pe.value_load(T.eid[0:1, bass.ds(s, 1)], min_val=0, max_val=NE - 1)
                        pe.wait_ge(hT_ready, s + 2)
                        pe.wait_ge(y_ready, s + 1)
                        for f in range(FC):
                            m = pe.matmul(psY[:, 0:D], hT[:, f * P:f * P + P],
                                          w2f[:, bass.ds(e * (FC * D) + f * D, D)],
                                          start=(f == 0), stop=(f == FC - 1))
                        m.then_inc(result, 1)
        core.end_phase()


def experts1(core, T):
    nc = core.nc
    with ExitStack() as st:
        sb = lambda n, s, d=F32: core.sb(f"e1_{n}", s, d, st)
        ps = lambda n, c, d=F32: core.ps(f"e1_{n}", c, d, st)
        sem = lambda n: core.phase_sem(f"e1_{n}")
        W = 2 * F1
        NPT = 3
        NP = SLOT1 // 2
        KF = F1 // P
        w1 = sb("w1", [P, NE, KD, W], BF16)
        w2 = sb("w2", [P, NE, KF, D], BF16)
        b1h = sb("b1h", [P, NE * W], BF16)
        b2h = sb("b2h", [P, NE * D], BF16)
        row = sb("row", [P, P], BF16)
        warm = sb("warm", [P, 1])
        xs = [sb(f"xs{u}", [P, 2, D], BF16) for u in range(2)]
        xT = [sb(f"xT{u}", [P, 2, KD, P], BF16) for u in range(2)]
        g = sb("g", [P, 2, F1])
        sg = sb("sg", [P, 2, F1])
        lin = sb("lin", [P, 2, F1])
        gl = sb("gl", [P, 2, F1])
        r1 = sb("r1", [P, 2, F1])
        r2 = [sb(f"r2{u}", [P, 2, F1]) for u in range(2)]
        parts = [sb(f"parts{u}", [P, NPT, 2, F1], BF16) for u in range(2)]
        aT = sb("aT", [P, 2, NPT * F1], BF16)
        y = [sb(f"y{u}", [P, 2, D]) for u in range(2)]
        psX = [ps(f"psX{u}", 1024, BF16) for u in range(2)]
        psP = ps("psP", 1024)
        psA = ps("psA", 2048, BF16)
        psY = [ps(f"psY{u}", 512) for u in range(2)]
        tab_in = sem("tab_in")
        tab2_in = sem("tab2_in")
        row_ok = sem("row_ok")
        x_in = [sem(f"x_in{u}") for u in range(2)]
        y_out = [sem(f"y_out{u}") for u in range(2)]
        x_turned = sem("x_turned")
        xT_ready = sem("xT_ready")
        hidden = sem("hidden")
        g_ready = sem("g_ready")
        clipped = sem("clipped")
        sig_ready = sem("sig_ready")
        step = sem("step")
        rest_ready = sem("rest_ready")
        part2 = sem("part2")
        split = sem("split")
        a_turned = sem("a_turned")
        aT_ready = sem("aT_ready")
        result = sem("result")
        y_ready = sem("y_ready")
        w1f = w1[:, :, :, :].rearrange("p e k f -> p (e k f)")
        w2f = w2[:, :, :, :].rearrange("p e k d -> p (e k d)")
        xd = T.sorted_dram[1].rearrange("(n s p) d -> n p s d", p=P, s=2)
        yd = T.result_dram[1].rearrange("(n s p) d -> n p s d", p=P, s=2)
        pair_of = lambda ap, n: ap[n] if isinstance(n, int) else ap[bass.ds(n, 1)].rearrange("n p s d -> (n p) s d")

        def over_pairs(eng, lo, hi, body):
            with eng.Fori(0, (hi - lo) // 2) as q:
                for v in range(2):
                    body(2 * q + (lo + v), (lo + v) % 2)

        def uses(n, u):
            return 8 * (n - u)

        with nc.Block() as block:
            @block.sync
            def _(sp):
                sp.dma_start(w1[:, :, :, :], T.m1_dram.rearrange("e (k p) f -> p e k f", p=P)).then_inc(tab_in, 16)
                sp.dma_start(b1h[:, :], T.mb1_dram.partition_broadcast(P)).then_inc(tab_in, 16)
                sp.sem_inc(y_out[0], 16)
                sp.sem_inc(y_out[1], 16)
                for u in range(2):
                    sp.dma_start(xs[u][:, :, :], xd[u]).then_inc(x_in[u], 16)
                sp.dma_start(w2[:, :, :, :], T.m2_dram.rearrange("e (k p) d -> p e k d", p=P)).then_inc(tab2_in, 16)
                sp.dma_start(b2h[:, :], T.mb2_dram.partition_broadcast(P)).then_inc(tab2_in, 16)

                def load(n, u):
                    sp.wait_ge(x_turned, n + 1)
                    sp.dma_start(xs[u][:, :, :], pair_of(xd, n)).then_inc(x_in[u], 16)

                over_pairs(sp, 2, NP, load)
                load(NP, 0)
                for u in range(2):
                    sp.wait_ge(y_out[u], 16 * (NP // 2 + 1))

            @block.gpsimd
            def _(pool):
                pool.memset(row[:, :], 0.0).then_inc(row_ok, 1)
                pool.wait_ge(row_ok, 1)
                pool.memset(row[0:1, :], 1.0).then_inc(row_ok, 1)

                def third(n, u):
                    pool.wait_ge(part2, n + 1)
                    pool.tensor_tensor(parts[u][:, 2], r2[u][:, :, :], parts[u][:, 1], ALU.subtract)\
                        .then_inc(split, 1)

                over_pairs(pool, 0, NP, third)

            @block.vector
            def _(dve):
                dve.sem_inc(clipped, 1)
                pair = psP[:, :].rearrange("p (s f) -> p s f", s=2)

                def activate(n, u):
                    def then(ins, k):
                        ins.then_inc(step, 1)
                        dve.wait_ge(step, 3 * n + k)

                    dve.wait_ge(hidden, n + 3)
                    dve.tensor_scalar(g[:, :, :], pair[:, :, 0:F1], 7.0, None, ALU.min).then_inc(g_ready, 1)
                    dve.tensor_scalar(lin[:, :, :], pair[:, :, F1:W], 7.0, -7.0, ALU.min, ALU.max)\
                        .then_inc(clipped, 1)
                    dve.wait_ge(sig_ready, n + 1)
                    then(dve.tensor_tensor(gl[:, :, :], g[:, :, :], sg[:, :, :], ALU.mult), 1)
                    dve.wait_ge(clipped, n + 2)
                    then(dve.scalar_tensor_tensor(r1[:, :, :], lin[:, :, :], 1.0, gl[:, :, :], ALU.add, ALU.mult), 2)
                    dve.wait_ge(a_turned, n + 1)
                    then(dve.tensor_scalar(parts[u][:, 0], r1[:, :, :], 0.0, None, ALU.add), 3)
                    dve.tensor_tensor(r2[u][:, :, :], r1[:, :, :], parts[u][:, 0], ALU.subtract)\
                        .then_inc(rest_ready, 1)

                over_pairs(dve, 0, NP, activate)

            @block.scalar
            def _(act):
                act.sem_inc(xT_ready, 2)
                act.sem_inc(aT_ready, 1)
                act.sem_inc(y_ready, 2)
                act.activation(warm[:, :], T.cst[:, C_ONE:C_ONE + 1], ACT.Sigmoid)

                def copy_x(n, u):
                    act.wait_ge(x_turned, n + 3)
                    act.wait_ge(hidden, n + 1)
                    act.copy(xT[u][:, :, :, :].rearrange("p s k t -> p (s k t)"), psX[u][:, 0:2 * D])\
                        .then_inc(xT_ready, 1)

                def sigmoid(n):
                    act.wait_ge(g_ready, n + 1)
                    act.activation(sg[:, :, :], g[:, :, :], ACT.Sigmoid, scale=1.702).then_inc(sig_ready, 1)

                def second(n, u):
                    act.wait_ge(rest_ready, n + 1)
                    act.copy(parts[u][:, 1], r2[u][:, :, :]).then_inc(part2, 1)

                def copy_a(n):
                    act.wait_ge(a_turned, n + 3)
                    act.wait_ge(result, n + 1)
                    act.copy(aT[:, :, :], psA[:, :].rearrange("p (s c) -> p s c", s=2)[:, :, 0:NPT * F1])\
                        .then_inc(aT_ready, 1)

                def copy_y(n, u):
                    act.wait_ge(result, n + 2)
                    act.wait_ge(y_out[u], uses(n, u) + 16)
                    act.copy(y[u][:, :, :].rearrange("p s d -> p (s d)"), psY[u][:, :]).then_inc(y_ready, 1)

                def store_y(n, u):
                    act.wait_ge(y_ready, n + 3)
                    act.dma_start(pair_of(yd, n), y[u][:, :, :]).then_inc(y_out[u], 16)

                copy_x(0, 0)
                sigmoid(0)
                second(0, 0)
                copy_x(1, 1)
                copy_x(2, 0)
                sigmoid(1)
                copy_a(0)
                second(1, 1)

                def body(n, u):
                    copy_x(n + 2, u)
                    sigmoid(n + 1)
                    copy_y(n - 1, 1 - u)
                    copy_a(n)
                    second(n + 1, 1 - u)
                    store_y(n - 1, 1 - u)

                over_pairs(act, 1, NP - 1, body)
                copy_y(NP - 2, 0)
                copy_a(NP - 1)
                store_y(NP - 2, 0)
                copy_y(NP - 1, 1)
                store_y(NP - 1, 1)

            @block.tensor
            def _(pe):
                pe.sem_inc(x_turned, 2)
                pe.sem_inc(hidden, 2)
                pe.sem_inc(a_turned, 2)
                pe.sem_inc(result, 1)
                pe.wait_ge(tab_in, 32)
                pe.wait_ge(row_ok, 2)

                def experts(n):
                    _, values = nc.values_load_multi_w_load_instructions(
                        T.eid[0:1, bass.ds(2 * n, 2)], engines=[mybir.EngineType.PE], min_val=0, max_val=NE - 1)
                    return values

                def turn_x(n, u):
                    pe.wait_ge(x_in[u], uses(n, u) + 16)
                    pe.wait_ge(xT_ready, n + 1)
                    for s in range(2):
                        for k in range(KD):
                            c = (s * KD + k) * P
                            t = pe.transpose(psX[u][:, c:c + P], xs[u][:, s, k * P:k * P + P], T.idb[:, :])
                    t.then_inc(x_turned, 1)

                def layer1(n, u):
                    es = experts(n)
                    pe.wait_ge(xT_ready, n + 3)
                    pe.wait_ge(clipped, n + 1)
                    for s, e in enumerate(es):
                        for k in range(KD):
                            pe.matmul(psP[:, s * W:s * W + W], xT[u][:, s, k, :],
                                      w1f[:, bass.ds(e * (KD * W) + k * W, W)], start=(k == 0), stop=False)
                        m = pe.matmul(psP[:, s * W:s * W + W], row[:, :], b1h[:, bass.ds(e * W, W)],
                                      start=False, stop=True)
                    m.then_inc(hidden, 1)

                def turn_a(n, u):
                    pe.wait_ge(split, n + 1)
                    pe.wait_ge(aT_ready, n + 1)
                    for s in range(2):
                        for a in range(NPT):
                            for k in range(KF):
                                c = s * 1024 + a * F1 + k * P
                                t = pe.transpose(psA[:, c:c + P], parts[u][:, a, s, k * P:k * P + P], T.idb[:, :])
                    t.then_inc(a_turned, 1)

                def layer2(n, u):
                    es = experts(n)
                    pe.wait_ge(aT_ready, n + 2)
                    pe.wait_ge(y_ready, n + 1)
                    for s, e in enumerate(es):
                        dst = psY[u][:, s * D:s * D + D]
                        for a in range(NPT):
                            for k in range(KF):
                                c = a * F1 + k * P
                                pe.matmul(dst, aT[:, s, c:c + P], w2f[:, bass.ds(e * (KF * D) + k * D, D)],
                                          start=(a == 0 and k == 0), stop=False)
                        m = pe.matmul(dst, row[:, :], b2h[:, bass.ds(e * D, D)], start=False, stop=True)
                    m.then_inc(result, 1)

                turn_x(0, 0)
                layer1(0, 0)
                turn_x(1, 1)
                layer1(1, 1)
                turn_x(2, 0)
                turn_a(0, 0)

                def body(n, u):
                    layer1(n + 1, 1 - u)
                    turn_x(n + 2, u)
                    layer2(n - 1, 1 - u)
                    turn_a(n, u)

                pe.wait_ge(tab2_in, 32)
                over_pairs(pe, 1, NP - 1, body)
                layer2(NP - 2, 0)
                turn_a(NP - 1, 1)
                layer2(NP - 1, 1)
        core.end_phase()


def combine(core, T, L, O, x_dram, w_dram, out_dram):
    nc = core.nc
    NPAIR = NT // 2
    with ExitStack() as st:
        sb = lambda n, s, d=F32: core.sb(f"c{L}_{n}", s, d, st)
        ps = lambda n, c, d=F32: core.ps(f"c{L}_{n}", c, d, st)
        sem = lambda n: core.phase_sem(f"c{L}_{n}")
        two = lambda n, d=F32: [sb(f"{n}{v}", [P, 2, D], d) for v in range(2)]
        w = sb("w", [P, KD, D])
        bias = sb("bias", [P, D])
        RY = 4
        x = [sb(f"x{v}", [P, 2, D]) for v in range(RY)]
        xn = [sb(f"xn{v}", [P, 2, D]) for v in range(RY)]
        ya = [sb(f"ya{v}", [P, 2, D]) for v in range(RY)]
        yb = [sb(f"yb{v}", [P, 2, D]) for v in range(RY)]
        va2, vb2 = two("va"), two("vb")
        hb2 = [sb(f"hb{v}", [P, 2, 2, D], BF16) for v in range(2)]
        fo = two("fo", BF16 if L else F32)
        g = two("g")
        os_, oT = two("os"), two("oT")
        s0, s1 = two("s0"), two("s1")
        r = two("r")
        al = sb("al", [P, NT])
        be = sb("be", [P, NT])
        warm = sb("warm", [P, 1])
        psT = [ps(f"psT{v}", 512) for v in range(2)]
        psS = [ps(f"psS{v}", 512) for v in range(2)]
        w_in = sem("w_in")
        x_in = [sem(f"x_in{v}") for v in range(RY)]
        y_in = [sem(f"y_in{v}") for v in range(RY)]
        alpha_ok = sem("alpha_ok")
        step = sem("step")
        mixed = sem("mixed")
        gated = sem("gated")
        staged = sem("staged")
        turned = sem("turned")
        oT_ready = sem("oT_ready")
        product = sem("product")
        biased = sem("biased")
        multiplied = sem("multiplied")
        added = sem("added")
        out = [sem(f"out{v}") for v in range(2)]
        pair = lambda ap, p: ap.rearrange("(t p) d -> p t d", p=P)[:, bass.ds(2 * p, 2), :]
        uses = lambda p, v: 8 * (p - v)

        def over_pairs(eng, body):
            with eng.Fori(0, NPAIR // RY - 1) as j:
                for v in range(RY):
                    body(RY * j + v, v, RY)
            for p in range(NPAIR - RY, NPAIR):
                body(p, p % RY, NPAIR - 1 - p)

        with nc.Block() as block:
            @block.sync
            def _(sp):
                sp.dma_start(w[:, :, :], w_dram.rearrange("(k p) n -> p k n", p=P)).then_inc(w_in, 16)
                if L:
                    sp.dma_start(bias[:, :], T.bproj_dram.partition_broadcast(P)).then_inc(w_in, 16)
                sp.sem_inc(out[0], 16)
                sp.sem_inc(out[1], 16)

                def load(p, w4):
                    sp.wait_ge(added, p + 1)
                    sp.dma_start(x[w4][:, :, :], pair(x_dram, p)).then_inc(x_in[w4], 16)
                    sp.wait_ge(mixed, p + 1)
                    sp.dma_start(xn[w4][:, :, :], pair(T.xn_dram, p)).then_inc(x_in[w4], 16)

                def body(p, w4, left):
                    v = w4 % 2
                    sp.wait_ge(added, p + RY + 1)
                    sp.dma_start(pair(out_dram, p), r[v][:, :, :]).then_inc(out[v], 16)
                    if left >= RY:
                        load(p + RY, w4)

                for p in range(RY):
                    load(p, p)
                over_pairs(sp, body)
                for v in range(2):
                    sp.wait_ge(out[v], 16 * (NPAIR // 2 + 1))

            @block.gpsimd
            def _(pool):
                for t in range(NT):
                    p, u = t // 2, t % 2
                    pool.wait_ge(mixed, p + 1)
                    for c in range(L + 1):
                        k = c * NT + t
                        pool.indirect_dma_start(
                            out=(yb if c else ya)[p % RY][:, u, :], out_offset=None, in_=T.result_dram[L],
                            in_offset=bass.IndirectOffsetOnAxis(ap=T.pos[:, k:k + 1], axis=0))\
                            .then_inc(y_in[p % RY], 16)

            @block.vector
            def _(dve):
                dve.sem_inc(mixed, RY)
                dve.sem_inc(biased, 2)
                dve.sem_inc(added, RY)
                NSTEP = 3 if L else 2

                def mix(p, w4):
                    v = w4 % 2
                    va, vb, hb = va2[v], vb2[v], hb2[v]

                    def then(ins, k):
                        ins.then_inc(step, 1)
                        if k:
                            dve.wait_ge(step, NSTEP * p + k)

                    dve.wait_ge(x_in[w4], 32 // RY * (p - w4) + 32)
                    dve.wait_ge(y_in[w4], (L + 1) * (32 // RY * (p - w4) + 32))
                    col = lambda t, u: t[:, bass.ds(2 * p + u, 1)]
                    if L == 0:
                        then(dve.tensor_tensor(va[:, :, :], xn[w4][:, :, :], ya[w4][:, :, :], ALU.add), 0)
                        dve.tensor_scalar(vb[:, 0, :], xn[w4][:, 0, :], col(be, 0), None, ALU.mult)
                        then(dve.tensor_scalar(vb[:, 1, :], xn[w4][:, 1, :], col(be, 1), None, ALU.mult), 2)
                        dve.wait_ge(gated, p + 1)
                        for u in range(2):
                            m = dve.scalar_tensor_tensor(fo[v][:, u, :], va[:, u, :], col(al, u), vb[:, u, :],
                                                         ALU.mult, ALU.add)
                        m.then_inc(mixed, 1)
                    else:
                        top = T.top[:, :, :].rearrange("p c t -> p (c t)")
                        w0 = lambda u: top[:, bass.ds(2 * p + u, 1)]
                        w1 = lambda u: top[:, bass.ds(2 * p + u + NT, 1)]
                        dve.tensor_scalar(va[:, 0, :], yb[w4][:, 0, :], w1(0), None, ALU.mult)
                        then(dve.tensor_scalar(va[:, 1, :], yb[w4][:, 1, :], w1(1), None, ALU.mult), 0)
                        then(dve.tensor_scalar(hb[:, 1], xn[w4][:, :, :], 0.0, None, ALU.add), 2)
                        dve.scalar_tensor_tensor(hb[:, 0, 0, :], ya[w4][:, 0, :], w0(0), va[:, 0, :],
                                                 ALU.mult, ALU.add)
                        then(dve.scalar_tensor_tensor(hb[:, 0, 1, :], ya[w4][:, 1, :], w0(1), va[:, 1, :],
                                                      ALU.mult, ALU.add), 3)
                        dve.wait_ge(gated, p + 1)
                        dve.tensor_tensor(fo[v][:, :, :], hb[:, 0], hb[:, 1], ALU.add).then_inc(mixed, 1)

                def finish(p, w4):
                    v = w4 % 2
                    dve.wait_ge(product, p + 3)
                    dve.wait_ge(gated, p + 3)
                    scores = psS[v][:, :].rearrange("p (t d) -> p t d", t=2)
                    if L:
                        dve.tensor_tensor(s0[v][:, :, :], scores, bc(bias[:, :], 1, 2), ALU.add).then_inc(biased, 1)
                        dve.wait_ge(biased, p + 3)
                        dve.tensor_tensor(s1[v][:, :, :], s0[v][:, :, :], g[v][:, :, :], ALU.mult)\
                            .then_inc(multiplied, 1)
                        dve.wait_ge(multiplied, p + 1)
                    else:
                        dve.tensor_tensor(s1[v][:, :, :], scores, g[v][:, :, :], ALU.mult).then_inc(biased, 1)
                        dve.wait_ge(biased, p + 3)
                    dve.wait_ge(out[v], uses(p, v) + 16)
                    dve.tensor_tensor(r[v][:, :, :], s1[v][:, :, :], x[w4][:, :, :], ALU.add).then_inc(added, 1)

                def body(p, w4, left):
                    v = w4 % 2
                    if left >= 1:
                        mix(p + 1, (w4 + 1) % RY)
                    finish(p, w4)

                if L == 0:
                    dve.wait_ge(alpha_ok, 1)
                    dve.tensor_scalar(be[:, :], al[:, :], -1.0, 1.0, ALU.mult, ALU.add).then_inc(alpha_ok, 1)
                    dve.wait_ge(alpha_ok, 2)
                else:
                    dve.wait_ge(w_in, 32)
                mix(0, 0)
                over_pairs(dve, body)

            @block.scalar
            def _(act):
                act.sem_inc(oT_ready, 2)
                act.sem_inc(gated, 2)
                if L == 0:
                    act.activation(al[:, :], T.top[:, 0, :], ACT.Sigmoid).then_inc(alpha_ok, 1)
                act.activation(warm[:, :], T.cst[:, C_ONE:C_ONE + 1], ACT.Silu)

                def stage(p, v):
                    act.wait_ge(turned, p + 1)
                    src = O[:, :, :, :].rearrange("p g t c -> p g (t c)")[:, :, bass.ds(p * (2 * GW), 2 * GW)]
                    act.activation(os_[v][:, :, :].rearrange("p t (g c) -> p g t c", g=NG),
                                   src.rearrange("p g (t c) -> p g t c", t=2), ACT.Copy).then_inc(staged, 1)

                def ahead(p, v):
                    act.wait_ge(turned, p + 3)
                    act.wait_ge(product, p + 1)
                    act.copy(oT[v][:, :, :].rearrange("p t d -> p (t d)"), psT[v][:, :]).then_inc(oT_ready, 1)
                    act.wait_ge(mixed, p + RY + 1)
                    act.wait_ge(added, p + RY - 1)
                    act.activation(g[v][:, :, :], fo[v][:, :, :], ACT.Silu).then_inc(gated, 1)

                def body(p, w4, left):
                    v = w4 % 2
                    if left >= 2:
                        stage(p + 2, v)
                    if left >= 1:
                        ahead(p + 1, 1 - v)

                stage(0, 0)
                stage(1, 1)
                ahead(0, 0)
                over_pairs(act, body)

            @block.tensor
            def _(pe):
                pe.sem_inc(turned, 2)
                pe.sem_inc(product, 2)
                pe.wait_ge(w_in, 32 if L else 16)

                def turn(p, v):
                    pe.wait_ge(staged, p + 1)
                    pe.wait_ge(oT_ready, p + 1)
                    for t in range(2):
                        for k in range(KD):
                            c = (t * KD + k) * P
                            m = pe.transpose(psT[v][:, c:c + P], os_[v][:, t, k * P:k * P + P], T.idf)
                    m.then_inc(turned, 1)

                def body(p, w4, left):
                    v = w4 % 2
                    if left >= 1:
                        turn(p + 1, 1 - v)
                    pe.wait_ge(oT_ready, p + 3)
                    pe.wait_ge(biased, p + 1)
                    for t in range(2):
                        for k in range(KD):
                            m = pe.matmul(psS[v][:, t * D:t * D + D], oT[v][:, t, k * P:k * P + P], w[:, k, :],
                                          start=(k == 0), stop=(k == KD - 1))
                    m.then_inc(product, 1)

                turn(0, 0)
                over_pairs(pe, body)
        core.end_phase()


def unit_maxima():
    return [(c, i4, h, kc) for c in range(NC) for i4 in range(CT) for h in range(HG) for kc in range(c + 1)]


def piece_tiles(c, i4, h, kc):
    return min(CT, CT * (c - kc) + i4 + 1)


PIECES = unit_maxima()
NPIECE = len(PIECES)
NSCORE = sum(CT * (c + 1) * HG for c in range(NC))
NGROUP = NSCORE // HG
AHEAD = [n for n in range(NPIECE) if sum(piece_tiles(*p) for p in PIECES[:n]) >= HG * 58][0]


RING = 3
PSTRIDE = -(-NPIECE // RING) * RING
piece_count = lambda k: PSTRIDE - NPIECE + 1 if k == NPIECE - 1 else 1


def chunk_end(c):
    return sum(p[0] <= c for p in PIECES)


def group_number(c, j):
    return CT * c * (c + 1) // 2 + j


def maxima_steps(which, lo, hi):
    out = []
    for n in range(lo, hi):
        out.append(("max", which) + (n,) + PIECES[n])
        if n + 1 == chunk_end(PIECES[n][0]):
            out.append(("negate", which, PIECES[n][0]))
    return out


def attention_plan(kind):
    turns = [("turn", 1, b % 2, b // 2 % HG, b // (2 * HG)) for b in range(4 * HG)]
    if kind == "first":
        early, late = turns[:2 * HG], turns[2 * HG:]
        pieces = maxima_steps(1, 0, chunk_end(0))
        every = len(pieces) // len(late)
        for n, s in enumerate(pieces):
            early.append(s)
            if n % every == 0 and late:
                early.append(late.pop(0))
        return early + late + [("lift", 1, 0, 0), ("lift", 1, 0, 1)]
    scores = [("score", 0, c, j, h) for c in range(NC) for j in range(CT * (c + 1)) for h in range(HG)]
    tiles = [min(CT, CT * (s[2] + 1) - s[3]) for s in scores]
    at = [sum(tiles[:n]) for n in range(NSCORE + 1)]
    beside = [[] for _ in scores]

    def spread(steps, lo, hi):
        weight = [piece_tiles(*s[3:]) if s[0] == "max" else 0 if s[0] == "negate" else 1 for s in steps]
        total, gone = sum(weight), 0
        for s, w in zip(steps, weight):
            where = lo + (hi - lo) * gone / total
            slot = max(n for n in range(NSCORE) if at[n] <= where)
            beside[slot].append(s)
            if s[0] == "negate":
                beside[slot + 3].append(("lift", s[1], s[2], 0))
                beside[slot + 5].append(("lift", s[1], s[2], 1))
            gone += w

    if kind == "head":
        for c in range(1, NC):
            begin = lambda c: HG * CT * c * (c + 1) // 2
            spread(maxima_steps(0, chunk_end(c - 1), chunk_end(c)), at[begin(c - 1)], at[begin(c) - 6])
    else:
        spread(maxima_steps(0, AHEAD, NPIECE), 0, HG * 70)
    if kind != "tail":
        spread(turns, *((HG * 36, HG * 77) if kind == "head" else (HG * 2, HG * 69)))
        spread(maxima_steps(1, 0, AHEAD), HG * (79 if kind == "head" else 71), HG * 133)
    places = [(), (3,), (1, 3), (1, 3, 3), (0, 1, 2, 3), (0, 1, 2, 3, 3), (0, 0, 1, 2, 3, 3)]
    plan = []
    for n in range(0, NSCORE, HG):
        _, _, c, j, _ = scores[n]
        others = [x for b in beside[n:n + HG] for x in b]
        place = places[len(others)] if len(others) < len(places) else \
            [(HG + 1) * k // len(others) for k in range(len(others))]
        for h in range(HG):
            plan.append(scores[n + h])
            plan += [x for x, p in zip(others, place) if p == h]
        if j:
            plan.append(("value", 0, c, j - 1))
        elif c:
            plan += [("value", 0, c - 1, CT * c - 1), ("take", 0, c - 1)]
        elif kind != "head":
            plan += [("value", -1, NC - 1, CT * NC - 1), ("take", -1, NC - 1)]
        plan += [x for x, p in zip(others, place) if p == HG]
        if j == 2 and (c or kind != "head"):
            plan.append(("finish", 0, c - 1) if c else ("finish", -1, NC - 1))
    if kind == "tail":
        plan += [("value", 0, NC - 1, CT * NC - 1), ("take", 0, NC - 1), ("finish", 0, NC - 1)]
    return plan


class Plan:

    def __init__(self, kind):
        self.steps, self.bank = [], 0
        self.last_use = {}
        for s in attention_plan(kind):
            self.steps.append((s, self.bank))
            if s[0] == "turn":
                self.last_use["turn", s[4]] = self.bank
            if s[0] == "lift":
                self.last_use["lift", s[1], s[2]] = self.bank
            self.bank += s[0] in ("turn", "lift", "finish")


def attention(core, T, L, O):
    nc = core.nc
    first, head, body, tail = (Plan(k) for k in ("first", "head", "body", "tail"))
    with ExitStack() as st:
        sb = lambda n, s, d=F32: core.sb(f"s{L}_{n}", s, d, st)
        ps = lambda n, c, d=F32: core.ps(f"s{L}_{n}", c, d, st)
        sem = lambda n: core.phase_sem(f"s{L}_{n}")
        raw = [sb(f"raw{u}", [P, TS, 3 * GW]) for u in range(2)]
        rest = sb("rest", [P, TS, GW])
        qst = sb("qst", [P, TS, HG, NPART, DH], BF16)
        kst = sb("kst", [P, TS, HG, KR + MR], BF16)
        va = [sb(f"va{u}", [P, TS, HG, 32]) for u in range(2)]
        qT = [sb(f"qT{u}", [P, HG, S], BF16) for u in range(2)]
        kT = [sb(f"kT{u}", [P, HG, S], BF16) for u in range(2)]
        NPB = 8
        pr = [sb(f"pr{i}", [P, CH]) for i in range(NPB)]
        piece = sb("piece", [P, CT, HG, NC])
        nm = sb("nm", [P, CT, HG])
        nmp = sb("nmp", [P, CT, HG, MR], BF16)
        osb = sb("osb", [P, CH])
        rcp = sb("rcp", [P, CT, HG])
        psM = [ps(f"psM{i}", CH) for i in range(RING)]
        psS = [ps(f"psS{i}", CH) for i in range(RING)]
        psV = ps("psV", CH)
        psX = ps("psX", 512)
        psXb = psX[:, :].bitcast(BF16)
        psVb = psV[:, :].bitcast(BF16)
        loaded = [sem(f"loaded{u}") for u in range(2)]
        pad_ok = sem("pad_ok")
        passed = sem("passed")
        split = sem("split")
        parts_ready = sem("parts_ready")
        staged = sem("staged")
        stacks_used = sem("stacks_used")
        bank_full = sem("bank_full")
        bank_free = sem("bank_free")
        rowscores = sem("rowscores")
        reduced = sem("reduced")
        row_max = sem("row_max")
        max_split = sem("max_split")
        scored = sem("scored")
        exped = sem("exped")
        valued = sem("valued")
        taken = sem("taken")
        rcp_ok = sem("rcp_ok")
        scattered = sem("scattered")
        O2 = O[:, :, :, :].rearrange("p n t c -> p (n t c)")
        qd = T.qkv.rearrange("n p t c -> n p (t c)")

        def segments(eng, emit):
            emit(first, -1, 1, 0, None)
            emit(head, 0, 0, first.bank, first)
            base = first.bank + head.bank
            with eng.Fori(0, NU // 2 - 1) as i:
                emit(body, 2 * i + 1, 1, 2 * body.bank * i + base, head)
                emit(body, 2 * i + 2, 0, 2 * body.bank * i + base + body.bank, body)
            emit(tail, NU - 1, 1, base + (NU - 2) * body.bank, body)

        def lifted(plan, before, c, bank0):
            if ("lift", 0, c) in plan.last_use:
                return bank0 + plan.last_use["lift", 0, c] + 2
            plans = (head, body) if before is head else (before,)
            return bank0 - min(x.bank - x.last_use["lift", 1, c] for x in plans) + 2

        def first_col(c, j):
            return max(0, j - CT * c) * P

        def split_unit(eng, u, m, passed=None):
            q = raw[u][:, :, 0:GW].rearrange("p t (h d) -> p t h d", h=HG)
            k = raw[u][:, :, GW:2 * GW].rearrange("p t (h d) -> p t h d", h=HG)
            r = rest[:, :, :].rearrange("p t (h d) -> p t h d", h=HG)
            Q = lambda s: qst[:, :, :, s, :]
            K = lambda s: kst[:, :, :, s * DH:(s + 1) * DH]
            done = [0]

            def then(ins):
                done[0] += 1
                ins.then_inc(split, 1)
                eng.wait_ge(split, 8 * m + done[0])
                if passed is not None:
                    eng.sem_inc(passed, 1)

            then(eng.tensor_copy(Q(0), q))
            eng.tensor_copy(Q(1), Q(0))
            eng.tensor_copy(Q(3), Q(0))
            then(eng.tensor_tensor(r, q, Q(0), ALU.subtract))
            then(eng.tensor_copy(Q(2), r))
            eng.tensor_copy(Q(4), Q(2))
            then(eng.tensor_tensor(Q(5), r, Q(2), ALU.subtract))
            then(eng.tensor_copy(K(0), k))
            eng.tensor_copy(K(2), K(0))
            eng.tensor_copy(K(5), K(0))
            then(eng.tensor_tensor(r, k, K(0), ALU.subtract))
            then(eng.tensor_copy(K(1), r))
            eng.tensor_copy(K(4), K(1))
            then(eng.tensor_tensor(K(3), r, K(1), ALU.subtract))

        with nc.Block() as block:
            @block.sync
            def _(sp):
                for m in range(2):
                    sp.wait_ge(staged, m + 1)
                    sp.dma_start(raw[m][:, :, :].rearrange("p t c -> p (t c)"), qd[m]).then_inc(loaded[m], 16)
                with sp.Fori(1, NU // 2) as i:
                    for u in range(2):
                        m = 2 * i + u
                        sp.wait_ge(staged, m + 1)
                        sp.dma_start(raw[u][:, :, :].rearrange("p t c -> p (t c)"),
                                     qd[bass.ds(m, 1)].rearrange("n p c -> (n p) c")).then_inc(loaded[u], 16)

            @block.gpsimd
            def _(pool):
                pool.sem_inc(staged, 2)
                for u in range(2):
                    pool.memset(va[u][:, :, :, DH:32], 0.0).then_inc(pad_ok, 1)
                pool.memset(kst[:, :, :, KR:KR + MR], 1.0).then_inc(pad_ok, 1)
                pool.wait_ge(pad_ok, 3)
                for u in range(2):
                    pool.memset(va[u][:, :, :, DH:DH + 1], 1.0).then_inc(pad_ok, 1)
                pool.wait_ge(pad_ok, 5)

                def stage(i):
                    for u in range(2):
                        m = 2 * i + u
                        pool.wait_ge(loaded[u], 16 * i + 16)
                        pool.wait_ge(stacks_used, m + 1)
                        pool.sem_inc(passed, 1)
                        if isinstance(i, int) and u == 0:
                            pool.wait_ge(parts_ready, 1)
                            pool.tensor_copy(va[u][:, :, :, 0:DH],
                                             raw[u][:, :, 2 * GW:3 * GW].rearrange("p t (h d) -> p t h d", h=HG))\
                                .then_inc(staged, 1)
                            continue
                        split_unit(pool, u, m, passed)
                        pool.sem_inc(parts_ready, 1)
                        free = 2 if isinstance(i, int) else NGROUP * (2 * (i - 1) + u + 1) + 2
                        pool.wait_ge(valued, free)
                        pool.sem_inc(passed, 1)
                        pool.tensor_copy(va[u][:, :, :, 0:DH],
                                         raw[u][:, :, 2 * GW:3 * GW].rearrange("p t (h d) -> p t h d", h=HG))\
                            .then_inc(staged, 1)
                stage(0)
                if L:
                    scatter(T, L, pool, scattered)
                else:
                    pool.dma_start(T.sorted_dram[1].rearrange("(s p) d -> p s d", p=P),
                                   bc(T.zero[:, 0:D // 2].bitcast(BF16), 1, SLOT1 + 2)).then_inc(T.cleared[1], 16)
                with pool.Fori(1, NU // 2) as i:
                    stage(i)
                if L:
                    pool.wait_ge(scattered, 16 * 2 * NT)

            @block.tensor
            def _(pe):
                pe.sem_inc(stacks_used, 1)
                pe.sem_inc(valued, 2)
                pe.wait_ge(pad_ok, 5)

                def emit(plan, n, u, bank0, before):
                    for step, bank in plan.steps:
                        kind, which = step[0], step[1]
                        par = (u + which) % 2
                        m = n + which
                        if kind == "turn":
                            _, _, isk, h, lo = step
                            if (isk, h, lo) == (0, 0, 0):
                                pe.wait_ge(parts_ready, m + 1)
                            odd = plan is first and bank % 2 == 1
                            pe.wait_ge(bank_free, max(bank, 1) if plan is first else bank0 + bank + 1)
                            dst = psVb if odd else psXb
                            rows = KR + MR if isk else KR
                            for t in range(8):
                                src = kst[:, 8 * lo + t, h, :] if isk else \
                                    qst[:, 8 * lo + t, h, :, :].rearrange("p s d -> p (s d)")
                                x = pe.transpose(dst[0:rows, t * P:t * P + P], src, T.idb[:, :])
                            x.then_inc(bank_full, 1)
                            if bank == plan.last_use["turn", 1]:
                                pe.wait_ge(bank_full, bank0 + bank + 1)
                                pe.sem_inc(stacks_used, 1)
                        elif kind == "max":
                            _, _, k, c, i4, h, kc = step
                            for lo in range(2):
                                if which and k == chunk_end(2 * lo - 1) and ("turn", lo) in plan.last_use \
                                        and plan.last_use["turn", lo] < bank:
                                    pe.wait_ge(bank_free, bank0 + plan.last_use["turn", lo] + 2)
                            pe.wait_ge(reduced, PSTRIDE * m + k + 1)
                            i = CT * c + i4
                            w = P * piece_tiles(c, i4, h, kc)
                            x = pe.matmul(psM[k % RING][:, 0:w], qT[par][0:KR, h, i * P:i * P + P],
                                          kT[par][0:KR, h, kc * CH:kc * CH + w], start=True, stop=(kc < c))
                            if kc == c:
                                x = pe.matmul(psM[k % RING][:, w - P:w], T.idb[:, :], T.mqb[:, :],
                                              start=False, stop=True)
                            x.then_inc(rowscores, piece_count(k))
                        elif kind == "lift":
                            _, _, c, pair = step
                            if pair == 0:
                                pe.wait_ge(max_split, NC * m + c + 1)
                            pe.wait_ge(bank_free, bank0 + bank + 1)
                            for hh in range(2):
                                for i4 in range(CT):
                                    x = pe.transpose(psXb[KR:KR + MR, hh * CH + i4 * P:hh * CH + i4 * P + P],
                                                     nmp[:, i4, 2 * pair + hh, :], T.idb[:, :])
                            x.then_inc(bank_full, 1)
                        elif kind == "score":
                            _, _, c, j, h = step
                            k = HG * group_number(c, j) + h
                            if j == 0 and h == 0:
                                pe.wait_ge(bank_free, lifted(plan, before, c, bank0))
                            pe.wait_ge(exped, NSCORE * m + (k + 1 if k else RING))
                            dst = psS[k % RING]
                            a = first_col(c, j)
                            diag = j >= CT * c
                            x = pe.matmul(dst[:, a:CH], kT[par][0:KR + MR, h, j * P:j * P + P],
                                          qT[par][0:KR + MR, h, c * CH + a:c * CH + CH],
                                          start=True, stop=not diag)
                            if diag:
                                x = pe.matmul(dst[:, a:a + P], T.idb[:, :], T.mkb[:, :],
                                              start=False, stop=True)
                            x.then_inc(scored, 1)
                        elif kind == "value":
                            _, _, c, j = step
                            g = group_number(c, j)
                            pe.wait_ge(exped, NSCORE * m + HG * (g + 1) + RING)
                            if j == 0:
                                pe.wait_ge(taken, NC * m + c + 1)
                                if c == 0:
                                    pe.wait_ge(staged, m + 3)
                            a = first_col(c, j)
                            for h in range(HG):
                                x = pe.matmul(psV[32 * h:32 * h + 32, a:CH], va[par][:, j, h, :],
                                              pr[(HG * g + h) % NPB][:, a:CH],
                                              start=(j == 0), stop=(j == CT * c + CT - 1))
                            x.then_inc(valued, 1)
                        elif kind == "finish":
                            _, _, c = step
                            pe.wait_ge(taken, NC * m + c + 2)
                            pe.wait_ge(bank_free, bank0 + bank + 1)
                            for i4 in range(CT):
                                x = pe.transpose(psX[:, i4 * P:i4 * P + P], osb[:, i4 * P:i4 * P + P], T.idf)
                            x.then_inc(bank_full, 1)

                segments(pe, emit)

            @block.scalar
            def _(act):
                act.sem_inc(exped, RING)

                def emit(plan, n, u, bank0, before):
                    for step, bank in plan.steps:
                        kind, which = step[0], step[1]
                        par = (u + which) % 2
                        m = n + which
                        if kind == "turn":
                            _, _, isk, h, lo = step
                            act.wait_ge(bank_full, bank0 + bank + 1)
                            rows = KR + MR if isk else KR
                            dst = kT[par] if isk else qT[par]
                            src = psVb if plan is first and bank % 2 == 1 else psXb
                            act.copy(dst[0:rows, h, lo * 1024:lo * 1024 + 1024], src[0:rows, 0:1024])\
                                .then_inc(bank_free, 1)
                        elif kind == "score":
                            _, _, c, j, h = step
                            g = group_number(c, j)
                            k = HG * g + h
                            a = first_col(c, j)
                            act.wait_ge(scored, NSCORE * m + k + 1)
                            if h == 0:
                                act.wait_ge(valued, NGROUP * m + g + 1)
                            act.activation(pr[k % NPB][:, a:CH], psS[k % RING][:, a:CH],
                                           ACT.Exp, scale=float(DH) ** -0.5).then_inc(exped, 1)

                segments(act, emit)

            @block.vector
            def _(dve):
                dve.sem_inc(bank_free, 1)
                dve.sem_inc(reduced, RING)
                dve.sem_inc(taken, 1)
                dve.wait_ge(loaded[0], 16)
                split_unit(dve, 0, 0)
                dve.sem_inc(parts_ready, 1)

                def emit(plan, n, u, bank0, before):
                    for step, bank in plan.steps:
                        kind, which = step[0], step[1]
                        par = (u + which) % 2
                        m = n + which
                        if kind == "max":
                            _, _, k, c, i4, h, kc = step
                            dve.wait_ge(rowscores, PSTRIDE * m + k + 1)
                            w = P * piece_tiles(c, i4, h, kc)
                            dve.tensor_reduce(piece[:, i4, h, kc:kc + 1], psM[k % RING][:, 0:w], AX.X, ALU.max,
                                              negate=True).then_inc(reduced, piece_count(k))
                        elif kind == "negate":
                            _, _, c = step
                            g = NC * m + c
                            dve.wait_ge(reduced, PSTRIDE * m + chunk_end(c) + RING)
                            dve.tensor_reduce(nm[:, :, :], piece[:, :, :, 0:c + 1], AX.X, ALU.min)\
                                .then_inc(row_max, 1)
                            dve.wait_ge(row_max, 2 * g + 1)
                            dve.tensor_copy(nmp[:, :, :, 0], nm[:, :, :]).then_inc(row_max, 1)
                            dve.wait_ge(row_max, 2 * g + 2)
                            dve.tensor_tensor(nmp[:, :, :, 1], nm[:, :, :], nmp[:, :, :, 0], ALU.subtract)\
                                .then_inc(max_split, 1)
                        elif kind == "lift":
                            _, _, c, pair = step
                            dve.wait_ge(bank_full, bank0 + bank + 1)
                            dve.tensor_copy(qT[par][KR:KR + MR, 2 * pair:2 * pair + 2, c * CH:c * CH + CH],
                                            psXb[KR:KR + MR, :].rearrange("p (h q) -> p h q", h=2))\
                                .then_inc(bank_free, 1)
                        elif kind == "take":
                            _, _, c = step
                            dve.wait_ge(valued, NGROUP * m + group_number(c, CT * (c + 1)) + 2)
                            dve.tensor_copy(osb[:, :], psV[:, :]).then_inc(taken, 1)
                        elif kind == "finish":
                            _, _, c = step
                            dve.wait_ge(bank_full, bank0 + bank + 1)
                            view = psX[:, :].rearrange("p (t h w) -> p t h w", t=CT, h=HG)
                            dve.reciprocal(rcp[:, :, :], view[:, :, :, DH]).then_inc(rcp_ok, 1)
                            dve.wait_ge(rcp_ok, NC * m + c + 1)
                            dst = O2[:, bass.ds(m * (TS * GW) + c * CT * GW, CT * GW)]
                            dve.tensor_tensor(dst.rearrange("p (t h d) -> p t h d", t=CT, h=HG),
                                              view[:, :, :, 0:DH], bc(rcp[:, :, :], 3, DH), ALU.mult)\
                                .then_inc(bank_free, 1)

                segments(dve, emit)
        core.end_phase()


def build(nc, ins, out):
    with ExitStack() as stack:
        core = Core(nc, stack)

        class T:
            pass

        T.cst_dram, T.cos_dram, T.sin_dram = ins["cst"], ins["cos"], ins["sin"]
        T.cent_dram, T.w1_dram, T.w2_dram = ins["cent"], ins["w1"], ins["w2"]
        T.gb0_dram, T.b1_dram, T.b2_dram = ins["gb0"], ins["b1"], ins["b2"]
        T.bqkv_dram, T.bproj_dram = ins["bqkv"], ins["bproj"]
        T.nw_dram, T.gw_dram, T.gb_dram = ins["nw"], ins["gw"], ins["gb"]
        T.m1_dram, T.m2_dram, T.mb1_dram, T.mb2_dram = ins["m1"], ins["m2"], ins["mb1"], ins["mb2"]
        T.qkv = core.dram("qkv", [NU, P, TS, 3 * GW])
        T.xn_dram = core.dram("xn", [NT * P, D])
        x1_dram = core.dram("x1", [NT * P, D])
        T.sorted_dram = [core.dram("sorted0", [(SLOT0 + 2) * P, D]), core.dram("sorted1", [(SLOT1 + 2) * P, D], BF16)]
        T.result_dram = [core.dram("result0", [SLOT0 * P, D]), core.dram("result1", [SLOT1 * P, D])]
        load_constants(core, T)
        T.w1_in = core.sem("w1_in")
        T.w2_in = core.sem("w2_in")
        T.cleared = [core.sem("cleared0"), core.sem("cleared1")]
        T.aff = core.sb("aff", [P, NT, NE])
        T.pos = core.sb("pos", [P, 2 * NT], U32)
        T.eid = core.sb("eid", [P, SLOT1 + 2], I32)
        T.top = core.sb("top", [P, 2, NT])

        with ExitStack() as st:
            T.w1 = core.sb("w1", [P, NE, KD, F0], F32, st)
            T.w2 = core.sb("w2", [P, NE, F0 // P, D], F32, st)
            with ExitStack() as sx:
                T.X = core.sb("X0", [P, NT, D], F32, sx)
                norm_project(core, T, 0, ins["x"], ins["wqkv0"], T.X)
                route(core, T, 0)
            experts0(core, T)
        with ExitStack() as st:
            O = core.sb("O0", [P, NG, NT, GW], F32, st)
            attention(core, T, 0, O)
            combine(core, T, 0, O, ins["x"], ins["wo0"], x1_dram)

        with ExitStack() as st:
            T.nf = core.sb("nf", [P, NT, D], BF16, st)
            T.ss = core.sb("ss", [P, NT], F32, st)
            with ExitStack() as sx:
                T.X = core.sb("X1", [P, NT, D], F32, sx)
                norm_project(core, T, 1, x1_dram, ins["wqkv1"], T.X)
            scores_of_layer1(core, T)
            route(core, T, 1)
            O = core.sb("O1", [P, NG, NT, GW], F32, st)
            attention(core, T, 1, O)
            experts1(core, T)
            combine(core, T, 1, O, x1_dram, ins["wo1"], out)


def kernel(**inputs):
    import numpy as _np
    import concourse.bacc as _bacc
    from concourse import mybir as _mybir
    from concourse.bass_utils import run_bass_kernel_spmd as _run

    a = {k: _np.asarray(v) for k, v in inputs.items()}
    def grouped(q, k, v):
        parts = [_np.reshape(m, m.shape[:-1] + (NG, GW)) for m in (q, k, v)]
        return _np.ascontiguousarray(_np.stack(parts, axis=-2).reshape(q.shape[:-1] + (3 * D,)))

    wq1 = a["L1_attn_Wqkv"]
    bq1 = a["L1_attn_bqkv"]
    m1 = a["L1_ffn_mlp1_weight"]
    mb1 = a["L1_ffn_mlp1_bias"]
    cos, sin = rotary_tables()
    col = lambda t: t.reshape(NE, KD, P).transpose(2, 0, 1)
    arrays = {
        "x": a["L0_attn_x"].reshape(NT * P, D),
        "wqkv0": grouped(a["L0_attn_W_Q"], a["L0_attn_W_K"], a["L0_attn_W_V"]),
        "wo0": a["L0_attn_W_o"],
        "cent": a["L0_ffn_centroids"].T,
        "w1": a["L0_ffn_w1"].transpose(0, 2, 1),
        "w2": a["L0_ffn_w2"].transpose(0, 2, 1),
        "b1": a["L0_ffn_b1"].reshape(-1),
        "b2": a["L0_ffn_b2"].reshape(-1),
        "gb0": _np.stack([col(a["L0_ffn_ln_g"]), col(a["L0_ffn_ln_b"])], axis=2).reshape(P, -1),
        "wqkv1": grouped(wq1[:, 0:D], wq1[:, D:2 * D], wq1[:, 2 * D:]),
        "bqkv": grouped(bq1[0:D], bq1[D:2 * D], bq1[2 * D:]),
        "wo1": a["L1_attn_Wproj"],
        "bproj": a["L1_attn_bproj"],
        "nw": a["L1_ffn_norm_weight"],
        "gw": a["L1_ffn_gate_weight"].T,
        "gb": a["L1_ffn_gate_bias"],
        "m1": _np.concatenate([m1[:, 0::2], m1[:, 1::2]], axis=1).transpose(0, 2, 1),
        "mb1": _np.concatenate([mb1[:, 0::2], mb1[:, 1::2]], axis=1).reshape(-1),
        "m2": a["L1_ffn_mlp2_weight"].transpose(0, 2, 1),
        "mb2": a["L1_ffn_mlp2_bias"].reshape(-1),
        "cst": constant_table(), "cos": cos, "sin": sin,
    }
    nc = _bacc.Bacc("TRN2", target_bir_lowering=False, num_devices=1)
    feed, ins = {}, {}
    for name, v in arrays.items():
        v = _np.ascontiguousarray(v)
        feed["in_" + name] = v
        ins[name] = nc.dram_tensor("in_" + name, v.shape, _mybir.dt.from_np(v.dtype), kind="ExternalInput").ap()
    out = nc.dram_tensor("out", (NT * P, D), _mybir.dt.from_np(_np.dtype("float32")), kind="ExternalOutput").ap()
    build(nc, ins, out)
    r = _run(nc, [feed], core_ids=[0])
    return r.results[0]["out"].reshape(NB, S, D)
```
